# Optimizing a Trainium2 kernel written in Bass

```python
import numpy as np
import jax
import jax.numpy as jnp

def _softmax(x, axis=-1):
    return jax.nn.softmax(x, axis=axis)

def _gelu(x):
    return jax.nn.gelu(x, approximate=True)

def _silu(x):
    return jax.nn.silu(x)

def _sigmoid(x):
    return jax.nn.sigmoid(x)

def _layernorm(x, axis=-1, eps=1e-05):
    m = jnp.mean(x, axis=axis, keepdims=True)
    v = jnp.var(x, axis=axis, keepdims=True)
    return (x - m) / jnp.sqrt(v + eps)

def _scatter_add(tgt, idx, src, axis=0):
    return tgt.at[idx].add(src)

def _segment_sum(src, seg, n):
    return jax.ops.segment_sum(src, seg, n)
kernel_name = 'mk_seq_preln_d2_jaxref_r8_f9ccb4'

def setup_inputs(seed: int=0):
    np.random.seed(seed)
    _w = jnp.asarray

    def _L0_attn_setup():
        import jax, jax.numpy as jnp
        import numpy as np
        D = 256
        H = 8
        CHUNK = 128
        NORM_GK = 16.0
        EPS = 1e-05

        def _chunked_gla(q, k, v, gk):
            gkc = jnp.cumsum(gk, axis=-2)
            qd = q * jnp.exp(gkc)
            kd = k * jnp.exp(gkc[..., -1:, :] - gkc)
            A = jnp.einsum('bhnid,bhnjd->bhnij', qd, k * jnp.exp(-gkc))
            c = q.shape[-2]
            mask = jnp.tril(jnp.ones((c, c), dtype=bool))
            o_intra = jnp.einsum('bhnij,bhnjv->bhniv', jnp.where(mask, A, 0.0), v)
            decay_last = jnp.exp(gkc[..., -1, :])

            def step(S, inp):
                qd_c, kd_c, v_c, dl = inp
                o1 = jnp.einsum('bhcd,bhdv->bhcv', qd_c, S)
                S = dl[..., :, None] * S + jnp.einsum('bhcd,bhcv->bhdv', kd_c, v_c)
                return (S, o1)
            b, h, n, _, dk = q.shape
            dv = v.shape[-1]
            S0 = jnp.zeros((b, h, dk, dv), q.dtype)
            xs = (jnp.moveaxis(qd, 2, 0), jnp.moveaxis(kd, 2, 0), jnp.moveaxis(v, 2, 0), jnp.moveaxis(decay_last, 2, 0))
            _, o_inter = jax.lax.scan(step, S0, xs)
            o_inter = jnp.moveaxis(o_inter, 0, 2)
            return o_inter + o_intra
        key = jax.random.key(seed)
        ks = jax.random.split(key, 10)
        s = 0.02
        return {'x': jax.random.normal(ks[0], (4, 256, D), jnp.float32), 'Wq': jax.random.normal(ks[1], (D, D // 2), jnp.float32) * s, 'Wk': jax.random.normal(ks[2], (D, D // 2), jnp.float32) * s, 'Wkg1': jax.random.normal(ks[3], (D, 16), jnp.float32) * s, 'Wkg2': jax.random.normal(ks[4], (16, D // 2), jnp.float32) * s, 'bkg2': jnp.zeros((D // 2,), jnp.float32), 'Wv': jax.random.normal(ks[5], (D, D), jnp.float32) * s, 'Wg': jax.random.normal(ks[6], (D, D), jnp.float32) * s, 'bg': jnp.zeros((D,), jnp.float32), 'Wo': jax.random.normal(ks[7], (D, D), jnp.float32) * s}
    _L0_attn_in = _L0_attn_setup()

    def _L0_ffn_setup():
        import jax, jax.numpy as jnp
        import numpy as np
        GOLDEN_CENTER = 1.0 / np.e
        GOLDEN_LOWER = 0.5 - np.log(4.0 / 3.0)
        GOLDEN_UPPER = 0.5

        def _golden_weights(x, Wr, temperature):
            inh = jax.nn.sigmoid(x @ Wr / temperature)
            in_zone = (inh >= GOLDEN_LOWER) & (inh <= GOLDEN_UPPER)
            distance = jnp.abs(inh - GOLDEN_CENTER)
            weights = jnp.exp(-distance / 0.1) * in_zone.astype(x.dtype)
            wsum = jnp.sum(weights, axis=-1, keepdims=True)
            no_expert = wsum < 1e-08
            fb = jnp.exp(-distance / 0.3)
            _, top2 = jax.lax.top_k(fb, 2)
            fb_mask = jnp.sum(jax.nn.one_hot(top2, weights.shape[-1], dtype=x.dtype), axis=-2)
            fb_w = fb * fb_mask
            fb_w = fb_w / jnp.maximum(jnp.sum(fb_w, axis=-1, keepdims=True), 1e-08)
            weights = jnp.where(no_expert, fb_w, weights)
            weights = weights / jnp.maximum(jnp.sum(weights, axis=-1, keepdims=True), 1e-08)
            return weights
        key = jax.random.key(seed)
        ks = jax.random.split(key, 5)
        B, T, D, E, F = (2, 256, 256, 8, 256)
        s_in = 1.0 / np.sqrt(D)
        s_f = 1.0 / np.sqrt(F)
        return {'x': jax.random.normal(ks[0], (B, T, D), dtype=jnp.float32), 'Wg': jax.random.normal(ks[1], (E, D, F), dtype=jnp.float32) * s_in, 'Wu': jax.random.normal(ks[2], (E, D, F), dtype=jnp.float32) * s_in, 'Wd': jax.random.normal(ks[3], (E, F, D), dtype=jnp.float32) * s_f, 'Wr': jax.random.normal(ks[4], (D, E), dtype=jnp.float32) * s_in, 'temperature': jnp.ones((1,), dtype=jnp.float32)}
    _L0_ffn_in = _L0_ffn_setup()

    def _L1_attn_setup():
        import jax, jax.numpy as jnp
        import numpy as np
        HIDDEN = 256
        KEY_DIM = 256
        NUM_HEADS = 16
        HEAD_DIM = KEY_DIM // NUM_HEADS
        ROPE_THETA = 10000.0
        EPS = 1e-05

        def rms_norm(x, w, eps=EPS):
            var = jnp.mean(x * x, axis=-1, keepdims=True)
            return x * jax.lax.rsqrt(var + eps) * w

        def apply_rope(x, theta_base=ROPE_THETA):
            b, s, h, d = x.shape
            half = d // 2
            freqs = theta_base ** (jnp.arange(half, dtype=x.dtype) * (-2.0 / d))
            freqs = jnp.concatenate([freqs, freqs], axis=-1)
            pos = jnp.arange(s, dtype=x.dtype)
            ang = pos[:, None] * freqs[None, :]
            cos = jnp.cos(ang)[None, :, None, :]
            sin = jnp.sin(ang)[None, :, None, :]
            x_even = x[..., 0::2]
            x_odd = x[..., 1::2]
            x1 = jnp.concatenate([x_even, x_even], axis=-1)
            x2 = jnp.concatenate([x_odd, x_odd], axis=-1)
            even_mask = (jnp.arange(d) % 2 == 0)[None, None, None, :]
            return jnp.where(even_mask, cos * x1 - sin * x2, sin * x1 + cos * x2)
        key = jax.random.key(seed)
        ks = jax.random.split(key, 10)
        B, S = (2, 256)
        s_in = 1.0 / np.sqrt(HIDDEN)
        s_k = 1.0 / np.sqrt(KEY_DIM)
        return {'x': jax.random.normal(ks[0], (B, S, HIDDEN), dtype=jnp.float32), 'rms_w': jnp.ones((HIDDEN,), dtype=jnp.float32), 'wq': jax.random.normal(ks[1], (HIDDEN, KEY_DIM), dtype=jnp.float32) * s_in, 'bq': jnp.zeros((KEY_DIM,), dtype=jnp.float32), 'wk': jax.random.normal(ks[2], (HIDDEN, KEY_DIM), dtype=jnp.float32) * s_in, 'bk': jnp.zeros((KEY_DIM,), dtype=jnp.float32), 'wv': jax.random.normal(ks[3], (HIDDEN, KEY_DIM), dtype=jnp.float32) * s_in, 'bv': jnp.zeros((KEY_DIM,), dtype=jnp.float32), 'wo': jax.random.normal(ks[4], (KEY_DIM, HIDDEN), dtype=jnp.float32) * s_k, 'bo': jnp.zeros((HIDDEN,), dtype=jnp.float32)}
    _L1_attn_in = _L1_attn_setup()

    def _L1_ffn_setup():
        import jax, jax.numpy as jnp
        import numpy as np
        DIM = 256
        INTER = 176
        E = 16
        TOPK = 4
        G = 4
        TOPK_G = 2
        N_SHARED = 2
        ROUTE_SCALE = 1.0
        INIT_STD = 0.02
        B, S = (1, 256)
        key = jax.random.key(seed)
        ks = jax.random.split(key, 9)
        std = INIT_STD
        x = jax.random.normal(ks[0], (B, S, DIM), jnp.float32)
        gate_w = jax.random.normal(ks[1], (E, DIM), jnp.float32) * std
        expert_bias = jnp.zeros((E,), jnp.float32)
        w1 = jax.random.normal(ks[2], (E, DIM, INTER), jnp.float32) * std
        w3 = jax.random.normal(ks[3], (E, DIM, INTER), jnp.float32) * std
        w2 = jax.random.normal(ks[4], (E, INTER, DIM), jnp.float32) * std
        sh = N_SHARED * INTER
        sw1 = jax.random.normal(ks[5], (DIM, sh), jnp.float32) * std
        sw3 = jax.random.normal(ks[6], (DIM, sh), jnp.float32) * std
        sw2 = jax.random.normal(ks[7], (sh, DIM), jnp.float32) * std
        return {'x': x, 'gate_w': gate_w, 'expert_bias': expert_bias, 'w1': w1, 'w2': w2, 'w3': w3, 'sw1': sw1, 'sw2': sw2, 'sw3': sw3}
    _L1_ffn_in = _L1_ffn_setup()
    _d = {'L0_attn_x': _L0_attn_in['x'], 'L0_attn_Wq': _L0_attn_in['Wq'], 'L0_attn_Wk': _L0_attn_in['Wk'], 'L0_attn_Wkg1': _L0_attn_in['Wkg1'], 'L0_attn_Wkg2': _L0_attn_in['Wkg2'], 'L0_attn_bkg2': _L0_attn_in['bkg2'], 'L0_attn_Wv': _L0_attn_in['Wv'], 'L0_attn_Wg': _L0_attn_in['Wg'], 'L0_attn_bg': _L0_attn_in['bg'], 'L0_attn_Wo': _L0_attn_in['Wo'], 'L0_ffn_Wg': _L0_ffn_in['Wg'], 'L0_ffn_Wu': _L0_ffn_in['Wu'], 'L0_ffn_Wd': _L0_ffn_in['Wd'], 'L0_ffn_Wr': _L0_ffn_in['Wr'], 'L0_ffn_temperature': _L0_ffn_in['temperature'], 'L1_attn_rms_w': _L1_attn_in['rms_w'], 'L1_attn_wq': _L1_attn_in['wq'], 'L1_attn_bq': _L1_attn_in['bq'], 'L1_attn_wk': _L1_attn_in['wk'], 'L1_attn_bk': _L1_attn_in['bk'], 'L1_attn_wv': _L1_attn_in['wv'], 'L1_attn_bv': _L1_attn_in['bv'], 'L1_attn_wo': _L1_attn_in['wo'], 'L1_attn_bo': _L1_attn_in['bo'], 'L1_ffn_gate_w': _L1_ffn_in['gate_w'], 'L1_ffn_expert_bias': _L1_ffn_in['expert_bias'], 'L1_ffn_w1': _L1_ffn_in['w1'], 'L1_ffn_w2': _L1_ffn_in['w2'], 'L1_ffn_w3': _L1_ffn_in['w3'], 'L1_ffn_sw1': _L1_ffn_in['sw1'], 'L1_ffn_sw2': _L1_ffn_in['sw2'], 'L1_ffn_sw3': _L1_ffn_in['sw3']}
    _x0 = _d['L0_attn_x']
    _d['L0_attn_x'] = jax.random.normal(jax.random.fold_in(jax.random.key(seed), 1), (4, 512, 256), dtype=_x0.dtype)
    del _x0
    return _d

def reference(L0_attn_x, L0_attn_Wq, L0_attn_Wk, L0_attn_Wkg1, L0_attn_Wkg2, L0_attn_bkg2, L0_attn_Wv, L0_attn_Wg, L0_attn_bg, L0_attn_Wo, L0_ffn_Wg, L0_ffn_Wu, L0_ffn_Wd, L0_ffn_Wr, L0_ffn_temperature, L1_attn_rms_w, L1_attn_wq, L1_attn_bq, L1_attn_wk, L1_attn_bk, L1_attn_wv, L1_attn_bv, L1_attn_wo, L1_attn_bo, L1_ffn_gate_w, L1_ffn_expert_bias, L1_ffn_w1, L1_ffn_w2, L1_ffn_w3, L1_ffn_sw1, L1_ffn_sw2, L1_ffn_sw3):

    def _L0_attn_ref(x, Wq, Wk, Wkg1, Wkg2, bkg2, Wv, Wg, bg, Wo):
        import jax, jax.numpy as jnp
        import numpy as np
        D = 256
        H = 8
        CHUNK = 128
        NORM_GK = 16.0
        EPS = 1e-05

        def _chunked_gla(q, k, v, gk):
            gkc = jnp.cumsum(gk, axis=-2)
            qd = q * jnp.exp(gkc)
            kd = k * jnp.exp(gkc[..., -1:, :] - gkc)
            A = jnp.einsum('bhnid,bhnjd->bhnij', qd, k * jnp.exp(-gkc))
            c = q.shape[-2]
            mask = jnp.tril(jnp.ones((c, c), dtype=bool))
            o_intra = jnp.einsum('bhnij,bhnjv->bhniv', jnp.where(mask, A, 0.0), v)
            decay_last = jnp.exp(gkc[..., -1, :])

            def step(S, inp):
                qd_c, kd_c, v_c, dl = inp
                o1 = jnp.einsum('bhcd,bhdv->bhcv', qd_c, S)
                S = dl[..., :, None] * S + jnp.einsum('bhcd,bhcv->bhdv', kd_c, v_c)
                return (S, o1)
            b, h, n, _, dk = q.shape
            dv = v.shape[-1]
            S0 = jnp.zeros((b, h, dk, dv), q.dtype)
            xs = (jnp.moveaxis(qd, 2, 0), jnp.moveaxis(kd, 2, 0), jnp.moveaxis(v, 2, 0), jnp.moveaxis(decay_last, 2, 0))
            _, o_inter = jax.lax.scan(step, S0, xs)
            o_inter = jnp.moveaxis(o_inter, 0, 2)
            return o_inter + o_intra
        b, T, _ = x.shape
        n = T // CHUNK
        dk = D // 2 // H
        dv = D // H
        scaling = (D // H) ** (-0.5)
        q = x @ Wq
        k = x @ Wk * scaling
        gk = jax.nn.log_sigmoid(x @ Wkg1 @ Wkg2 + bkg2) / NORM_GK
        v = x @ Wv
        g = x @ Wg + bg

        def split(t, hd):
            return t.reshape(b, n, CHUNK, H, hd).transpose(0, 3, 1, 2, 4)
        o = _chunked_gla(split(q, dk), split(k, dk), split(v, dv), split(gk, dk))
        mu = o.mean(-1, keepdims=True)
        var = o.var(-1, keepdims=True)
        o = (o - mu) / jnp.sqrt(var + EPS)
        o = o.transpose(0, 2, 3, 1, 4).reshape(b, T, D)
        o = jax.nn.silu(g) * o
        return o @ Wo

    def _L0_ffn_ref(x, Wg, Wu, Wd, Wr, temperature):
        import jax, jax.numpy as jnp
        import numpy as np
        GOLDEN_CENTER = 1.0 / np.e
        GOLDEN_LOWER = 0.5 - np.log(4.0 / 3.0)
        GOLDEN_UPPER = 0.5

        def _golden_weights(x, Wr, temperature):
            inh = jax.nn.sigmoid(x @ Wr / temperature)
            in_zone = (inh >= GOLDEN_LOWER) & (inh <= GOLDEN_UPPER)
            distance = jnp.abs(inh - GOLDEN_CENTER)
            weights = jnp.exp(-distance / 0.1) * in_zone.astype(x.dtype)
            wsum = jnp.sum(weights, axis=-1, keepdims=True)
            no_expert = wsum < 1e-08
            fb = jnp.exp(-distance / 0.3)
            _, top2 = jax.lax.top_k(fb, 2)
            fb_mask = jnp.sum(jax.nn.one_hot(top2, weights.shape[-1], dtype=x.dtype), axis=-2)
            fb_w = fb * fb_mask
            fb_w = fb_w / jnp.maximum(jnp.sum(fb_w, axis=-1, keepdims=True), 1e-08)
            weights = jnp.where(no_expert, fb_w, weights)
            weights = weights / jnp.maximum(jnp.sum(weights, axis=-1, keepdims=True), 1e-08)
            return weights
        weights = _golden_weights(x, Wr, temperature)
        gate = jnp.einsum('btd,edf->betf', x, Wg)
        up = jnp.einsum('btd,edf->betf', x, Wu)
        h = jax.nn.silu(gate) * up
        e_out = jnp.einsum('betf,efd->betd', h, Wd)
        out = jnp.einsum('bte,betd->btd', weights, e_out)
        return out

    def _L1_attn_ref(x, rms_w, wq, bq, wk, bk, wv, bv, wo, bo):
        import jax, jax.numpy as jnp
        import numpy as np
        HIDDEN = 256
        KEY_DIM = 256
        NUM_HEADS = 16
        HEAD_DIM = KEY_DIM // NUM_HEADS
        ROPE_THETA = 10000.0
        EPS = 1e-05

        def rms_norm(x, w, eps=EPS):
            var = jnp.mean(x * x, axis=-1, keepdims=True)
            return x * jax.lax.rsqrt(var + eps) * w

        def apply_rope(x, theta_base=ROPE_THETA):
            b, s, h, d = x.shape
            half = d // 2
            freqs = theta_base ** (jnp.arange(half, dtype=x.dtype) * (-2.0 / d))
            freqs = jnp.concatenate([freqs, freqs], axis=-1)
            pos = jnp.arange(s, dtype=x.dtype)
            ang = pos[:, None] * freqs[None, :]
            cos = jnp.cos(ang)[None, :, None, :]
            sin = jnp.sin(ang)[None, :, None, :]
            x_even = x[..., 0::2]
            x_odd = x[..., 1::2]
            x1 = jnp.concatenate([x_even, x_even], axis=-1)
            x2 = jnp.concatenate([x_odd, x_odd], axis=-1)
            even_mask = (jnp.arange(d) % 2 == 0)[None, None, None, :]
            return jnp.where(even_mask, cos * x1 - sin * x2, sin * x1 + cos * x2)
        B, S, _ = x.shape
        residual = x
        xn = rms_norm(x, rms_w)
        q = (xn @ wq + bq).reshape(B, S, NUM_HEADS, HEAD_DIM)
        k = (xn @ wk + bk).reshape(B, S, NUM_HEADS, HEAD_DIM)
        v = (xn @ wv + bv).reshape(B, S, NUM_HEADS, HEAD_DIM)
        q = apply_rope(q)
        k = apply_rope(k)
        scores = jnp.einsum('bshd,bthd->bhst', q, k) / jnp.sqrt(jnp.asarray(HEAD_DIM, dtype=x.dtype))
        causal = jnp.tril(jnp.ones((S, S), dtype=bool))[None, None]
        scores = jnp.where(causal, scores, -jnp.inf)
        probs = jax.nn.softmax(scores, axis=-1)
        out = jnp.einsum('bhst,bthd->bshd', probs, v).reshape(B, S, KEY_DIM)
        return out @ wo + bo + residual

    def _L1_ffn_ref(x, gate_w, expert_bias, w1, w2, w3, sw1, sw2, sw3):
        import jax, jax.numpy as jnp
        import numpy as np
        DIM = 256
        INTER = 176
        E = 16
        TOPK = 4
        G = 4
        TOPK_G = 2
        N_SHARED = 2
        ROUTE_SCALE = 1.0
        INIT_STD = 0.02
        B, S = (1, 256)
        b, s, d = x.shape
        T = b * s
        xf = x.reshape(T, d)
        scores = jax.nn.sigmoid(xf @ gate_w.T)
        original_scores = scores
        scores = scores + expert_bias
        sg = scores.reshape(T, G, E // G)
        group_scores = sg.max(axis=-1)
        _, gidx = jax.lax.top_k(group_scores, TOPK_G)
        gmask = jnp.zeros((T, G), bool).at[jnp.arange(T)[:, None], gidx].set(True)
        masked = jnp.where(gmask[:, :, None], sg, -jnp.inf).reshape(T, E)
        _, idx = jax.lax.top_k(masked, TOPK)
        w = jnp.take_along_axis(original_scores, idx, axis=1)
        w = w / jnp.sum(w, axis=-1, keepdims=True)
        w = w * ROUTE_SCALE
        cw = jnp.zeros((T, E), x.dtype).at[jnp.arange(T)[:, None], idx].add(w)
        h = jax.nn.silu(jnp.einsum('td,edh->teh', xf, w1)) * jnp.einsum('td,edh->teh', xf, w3)
        y = jnp.einsum('teh,ehd,te->td', h, w2, cw)
        z = jax.nn.silu(xf @ sw1) * (xf @ sw3) @ sw2
        return (y + z).reshape(b, s, d)
    x = L0_attn_x
    x = x + _L0_attn_ref(_layernorm(x, axis=-1), L0_attn_Wq, L0_attn_Wk, L0_attn_Wkg1, L0_attn_Wkg2, L0_attn_bkg2, L0_attn_Wv, L0_attn_Wg, L0_attn_bg, L0_attn_Wo)
    x = x + _L0_ffn_ref(_layernorm(x, axis=-1), L0_ffn_Wg, L0_ffn_Wu, L0_ffn_Wd, L0_ffn_Wr, L0_ffn_temperature)
    x = x + _L1_attn_ref(_layernorm(x, axis=-1), L1_attn_rms_w, L1_attn_wq, L1_attn_bq, L1_attn_wk, L1_attn_bk, L1_attn_wv, L1_attn_bv, L1_attn_wo, L1_attn_bo)
    x = x + _L1_ffn_ref(_layernorm(x, axis=-1), L1_ffn_gate_w, L1_ffn_expert_bias, L1_ffn_w1, L1_ffn_w2, L1_ffn_w3, L1_ffn_sw1, L1_ffn_sw2, L1_ffn_sw3)
    return x

_drawn_inputs = setup_inputs


def setup_inputs(seed=0):
    import zlib

    import numpy as np

    out = dict(_drawn_inputs(seed))
    spreads = {'L0_attn_bkg2': (0.0, 0.579),
     'L0_attn_bg': (0.0, 0.1),
     'L1_attn_rms_w': (1.0, 0.2),
     'L1_attn_bq': (0.0, 0.539),
     'L1_attn_bk': (0.0, 0.799),
     'L1_attn_bv': (0.0, 0.1),
     'L1_attn_bo': (0.0, 0.1),
     'L1_ffn_expert_bias': (0.0, 0.8)}
    factors = {'L0_attn_Wkg1': 8.0,
     'L0_attn_Wkg2': 8.0,
     'L1_ffn_gate_w': 8.0,
     'L1_ffn_w1': 8.0,
     'L1_ffn_w2': 8.0,
     'L1_ffn_w3': 8.0,
     'L1_ffn_sw1': 6.004,
     'L1_ffn_sw2': 5.929,
     'L1_ffn_sw3': 5.946}
    for name, (base, spread) in spreads.items():
        noise = np.random.default_rng([zlib.crc32(name.encode()), seed]).standard_normal(out[name].shape)
        drawn = base * np.exp(spread * noise) if base else spread * noise
        out[name] = jnp.asarray(drawn.astype(out[name].dtype))
    for name, factor in factors.items():
        out[name] = (out[name] * factor).astype(out[name].dtype)
    return out
```

```python
import numpy as np
import concourse.bass as bass
from concourse import mybir
from contextlib import ExitStack

f32 = mybir.dt.float32
f32r = mybir.dt.float32r
bf16 = mybir.dt.bfloat16
u32 = mybir.dt.uint32
ALU = mybir.AluOpType
ACT = mybir.ActivationFunctionType
AX = mybir.AxisListType

P = 128
B, T, D = 4, 512, 256
KC = D // P
NT = T // P
EPS = 1e-5
LN_EXP_SET = "natural_log_exp_and_others"
H0, DK0, DV0 = 8, 16, 32
GATE_NORM = 16.0
H1, DH1 = 16, 16
HALF = DH1 // 2
HPT = P // 32
NST = H1 // HPT
E0, F0 = 8, 256
E1, F1, SH1 = 16, 176, 352
CH0 = E0 * F0 // P
CH1 = -(-(E1 * F1 + SH1) // P)
TOP0, TOP1, G1, TOPG1 = 2, 4, 4, 2
GROUP0, GROUP1 = 4, 5
WR = 128
CENTER = float(1.0 / np.e)
LOWER = float(np.float32(0.5 - np.log(4.0 / 3.0)))
UPPER = 0.5
BIG = 3.0e38

W0Q, W0K, W0G, W0R, W0V, W0N = 0, 128, 256, 512, 640, 896
W1QA, W1QB, W1KA, W1KB, W1V, W1N = 0, 128, 256, 384, 512, 768
C_ID, C_TRI, C_AVG, C_DIAG, C_RST, C_EVEN, C_ODD = 0, 128, 256, 384, 640, 1152, 1153
C_COS, C_SIN = 0, 512
C_SEL = 1024


def mm3(pe, out, w_hi, w_lo, x_hi, x_lo, first, last):
    pe.matmul(out, w_hi, x_hi, start=first, stop=False, skip_group_check=True)
    pe.matmul(out, w_hi, x_lo, start=False, stop=False, skip_group_check=True)
    return pe.matmul(out, w_lo, x_hi, start=False, stop=last, skip_group_check=True)


def sems(nc, kept, prefix, names):
    named = {n: nc.alloc_semaphore(name=f"{prefix}_{n}") for n in names.split()}
    kept.extend(named.values())
    return named


def linear_attention(nc, kept, x, psum, con, conb, ident, dram):
    ctx = ExitStack()
    with ctx:
        def sb(name, shape, dt=f32):
            return ctx.enter_context(nc.sbuf_tensor(f"a0_{name}", shape, dt))

        s = sems(nc, kept, "a0", "x_in con_in w_in wo_in wr_in w_hi w_lo wo_hi wo_lo wr_hi wr_lo zeroed "
                 "stats moments var_eps ln_var rstd0 newton xhat xT_psum xT_hi xT_lo kg1_psum kg1_hi kg1_lo "
                 "q_psum k_psum kg2_psum v_psum g_psum gate_abs gate_min gate_exp gate_ln gate_log gate_cum "
                 "gate_last decay_q decay_k decay_end qd kn kdT kd_psum kd v_sb silu_g at_psum at_sb kv_psum "
                 "kv_sb state ot_psum o_sb mean_psum centered sq var_psum o_ln o_rstd c_gated y y_hi y_lo "
                 "wo_psum x_out")
        w_raw, w_hi, w_lo = sb("w_raw", [P, KC, W0N]), sb("w_hi", [P, KC, W0N], f32r), sb("w_lo", [P, KC, W0N], f32r)
        wo_raw, wo_hi, wo_lo = sb("wo_raw", [P, KC, D]), sb("wo_hi", [P, KC, D], f32r), sb("wo_lo", [P, KC, D], f32r)
        wr_raw, wr_hi, wr_lo = sb("wr_raw", [P, P]), sb("wr_hi", [P, P], f32r), sb("wr_lo", [P, P], f32r)
        cols = sb("cols", [P, 3])
        st, mv = sb("st", [P, NT, 6]), sb("mv", [P, NT, 2])
        ve, lnv, r0, n1, n2, rstd = (sb(n, [P, NT]) for n in ("ve", "lnv", "r0", "n1", "n2", "rstd"))
        held = sb("held", [P, 4])
        xhat = sb("xhat", [P, NT, D])
        xT_hi, xT_lo = sb("xT_hi", [P, KC, T], f32r), sb("xT_lo", [P, KC, T], f32r)
        kg1_hi, kg1_lo = sb("kg1_hi", [P, T], f32r), sb("kg1_lo", [P, T], f32r)
        g_abs, g_min, g_exp, g_ln, g_log, g_cum = (sb(n, [P, T]) for n in ("g_abs", "g_min", "g_exp", "g_ln", "g_log", "g_cum"))
        g_last = sb("g_last", [P, NT])
        dq, dk, de = sb("dq", [P, T]), sb("dk", [P, T]), sb("de", [P, T])
        qd, kne, kno, kdT = (sb(n, [P, T]) for n in ("qd", "kne", "kno", "kdT"))
        kd = sb("kd", [P, NT, P])
        v_sb = sb("v_sb", [P, NT, D])
        sg = sb("sg", [P, KC, T])
        at = [sb(f"at{i}", [P, 16, P]) for i in range(2)]
        kv = [sb(f"kv{i}", [P, D]) for i in range(3)]
        stt = [kv[0], sb("state2", [P, D]), sb("state3", [P, D])]
        o_sb, cen, sq, lv, rs, y = (sb(n, [P, KC, T]) for n in ("o_sb", "cen", "sq", "lv", "rs", "y"))
        y_hi, y_lo = sb("y_hi", [P, KC, T], f32r), sb("y_lo", [P, KC, T], f32r)
        tri = con[:, C_TRI:C_TRI + P]
        avg = con[:, C_AVG:C_AVG + P]
        diag = con[:, C_DIAG:C_DIAG + D]
        rst = con[:, C_RST:C_RST + T]
        eps_col = con[:, C_ODD + 1:C_ODD + 2]
        bank = lambda i, n=1: psum[:, 512 * i:512 * (i + n)]
        xb = lambda b: x[:, bass.ds(b * NT * D, NT * D)]

        def hold(dve, place):
            dve.tensor_copy(held[:, place:place + 1], con[:, 0:1])

        block = ctx.enter_context(nc.Block())

        @block.sync
        def _(sp):
            sp.dma_start(con[:, :], dram["con"]).then_inc(s["con_in"], 16)
            sp.dma_start(conb[:, :], dram["conb"].bitcast(bf16)).then_inc(s["con_in"], 16)
            for b in range(B):
                sp.dma_start(x[:, b * NT * D:(b + 1) * NT * D].rearrange("p (i d) -> p i d", i=NT),
                             dram["x"][b].rearrange("(i p) d -> p i d", p=P)).then_inc(s["x_in"], 16)
            sp.dma_start(w_raw[:, :, :], dram["w0"]).then_inc(s["w_in"], 16)
            sp.dma_start(wr_raw[:, :], dram["wr0"]).then_inc(s["wr_in"], 16)
            sp.dma_start(cols[:, :], dram["cols0"]).then_inc(s["wr_in"], 16)
            sp.dma_start(wo_raw[:, :, :], dram["wo0"]).then_inc(s["wo_in"], 16)

        @block.gpsimd
        def _(pool):
            for t in (at[0][:, :, :], at[1][:, :, :], kv[0][:, :], kv[1][:, :], kv[2][:, :]):
                pool.memset(t, 0.0).then_inc(s["zeroed"], 1)
            for raw, hi, lo, came, n, s_hi, s_lo in ((w_raw, w_hi, w_lo, "w_in", 16, "w_hi", "w_lo"),
                                                     (wr_raw, wr_hi, wr_lo, "wr_in", 32, "wr_hi", "wr_lo"),
                                                     (wo_raw, wo_hi, wo_lo, "wo_in", 16, "wo_hi", "wo_lo")):
                pool.wait_ge(s[came], n)
                pool.tensor_copy(hi[:], raw[:]).then_inc(s[s_hi], 1)
                pool.wait_ge(s[s_hi], 1)
                pool.tensor_tensor(lo[:], raw[:], hi[:].bitcast(f32), ALU.subtract).then_inc(s[s_lo], 1)

        @block.scalar
        def _(act):
            act.wait_ge(s["wr_in"], 32)
            with act.Fori(0, B) as b:
                act.preload_act_table_set(LN_EXP_SET)
                act.wait_ge(s["var_eps"], b + 1)
                act.activation(lnv[:, :], ve[:, :], ACT.Ln).then_inc(s["ln_var"], 1)
                act.wait_ge(s["ln_var"], b + 1)
                act.activation(r0[:, :], lnv[:, :], ACT.Exp, scale=-0.5).then_inc(s["rstd0"], 1)
                act.wait_ge(s["xT_psum"], b + 1)
                act.activation(xT_hi[:, :, :], bank(0, 2).rearrange("p (k t) -> p k t", k=KC), ACT.Copy).then_inc(s["xT_hi"], 1)
                act.wait_ge(s["kg1_psum"], b + 1)
                act.activation(kg1_hi[:, :], bank(6), ACT.Copy).then_inc(s["kg1_hi"], 1)
                act.wait_ge(s["gate_min"], b + 1)
                act.activation(g_abs[:, :], bank(7), ACT.Abs, bias=cols[:, 0:1]).then_inc(s["gate_abs"], 1)
                act.wait_ge(s["gate_abs"], b + 1)
                act.activation(g_exp[:, :], g_abs[:, :], ACT.Exp, scale=-1.0).then_inc(s["gate_exp"], 1)
                act.wait_ge(s["gate_exp"], b + 1)
                act.activation(g_ln[:, :], g_exp[:, :], ACT.Ln, bias=1.0).then_inc(s["gate_ln"], 1)
                act.wait_ge(s["gate_cum"], b + 1)
                act.activation(dq[:, :], g_cum[:, :], ACT.Exp, scale=1.0 / GATE_NORM).then_inc(s["decay_q"], 1)
                act.activation(dk[:, :], g_cum[:, :], ACT.Exp, scale=-1.0 / GATE_NORM).then_inc(s["decay_k"], 1)
                act.wait_ge(s["gate_last"], b + 1)
                for n in range(NT):
                    last = act.activation(de[:, n * P:(n + 1) * P], g_cum[:, n * P:(n + 1) * P], ACT.Exp,
                                          bias=g_last[:, n:n + 1], scale=-1.0 / GATE_NORM)
                last.then_inc(s["decay_end"], 1)
                act.wait_ge(s["v_psum"], b + 1)
                act.activation(v_sb[:, :, :], bank(0, 2).rearrange("p (i d) -> p i d", i=NT), ACT.Copy).then_inc(s["v_sb"], 1)
                act.wait_ge(s["kd_psum"], b + 1)
                act.activation(kd[:, :, :], bank(6).rearrange("p (i d) -> p i d", i=NT), ACT.Copy).then_inc(s["kd"], 1)
                act.wait_ge(s["g_psum"], b + 1)
                for h in range(KC):
                    last = act.activation(sg[:, h, :], bank(4 + h), ACT.Silu, bias=cols[:, 1 + h:2 + h])
                last.then_inc(s["silu_g"], 1)
                act.preload_act_table_set(LN_EXP_SET)
                act.wait_ge(s["ot_psum"], b + 1)
                act.activation(o_sb[:, :, :], bank(0, 2).rearrange("p (k t) -> p k t", k=KC), ACT.Copy).then_inc(s["o_sb"], 1)
                act.wait_ge(s["centered"], b + 1)
                act.activation(sq[:, :, :], cen[:, :, :], ACT.Square).then_inc(s["sq"], 1)
                act.wait_ge(s["var_psum"], b + 1)
                act.activation(lv[:, :, :], bank(4, 2).rearrange("p (k t) -> p k t", k=KC), ACT.Ln, bias=eps_col).then_inc(s["o_ln"], 1)
                act.wait_ge(s["o_ln"], b + 1)
                act.activation(rs[:, :, :], lv[:, :, :], ACT.Exp, scale=-0.5).then_inc(s["o_rstd"], 1)
                act.wait_ge(s["y"], b + 1)
                act.activation(y_hi[:, :, :], y[:, :, :], ACT.Copy).then_inc(s["y_hi"], 1)

        @block.vector
        def _(dve):
            dve.wait_ge(s["con_in"], 32)
            dve.wait_ge(s["x_in"], 16 * B)
            dve.wait_ge(s["zeroed"], 5)
            dve.wait_ge(s["wr_in"], 32)
            with dve.Fori(0, B) as b:
                for i in range(NT):
                    last = dve.bn_stats(st[:, i, :], x[:, bass.ds(b * NT * D + i * D, D)])
                last.then_inc(s["stats"], 1)
                dve.wait_ge(s["stats"], b + 1)
                hold(dve, 0)
                for i in range(NT):
                    last = dve.bn_aggr(mv[:, i, :], st[:, i, :])
                last.then_inc(s["moments"], 1)
                dve.wait_ge(s["moments"], b + 1)
                dve.tensor_scalar(ve[:, :], mv[:, :, 1], EPS, None, ALU.add).then_inc(s["var_eps"], 1)
                dve.wait_ge(s["rstd0"], b + 1)
                dve.scalar_tensor_tensor(n1[:, :], r0[:, :], -0.5, r0[:, :], ALU.mult, ALU.mult).then_inc(s["newton"], 1)
                dve.wait_ge(s["newton"], 3 * b + 1)
                dve.tensor_tensor(n2[:, :], n1[:, :], ve[:, :], ALU.mult).then_inc(s["newton"], 1)
                dve.wait_ge(s["newton"], 3 * b + 2)
                dve.scalar_tensor_tensor(rstd[:, :], n2[:, :], 1.5, r0[:, :], ALU.add, ALU.mult).then_inc(s["newton"], 1)
                dve.wait_ge(s["newton"], 3 * b + 3)
                for i in range(NT):
                    last = dve.tensor_scalar(xhat[:, i, :], x[:, bass.ds(b * NT * D + i * D, D)], mv[:, i, 0:1],
                                             rstd[:, i:i + 1], ALU.subtract, ALU.mult)
                last.then_inc(s["xhat"], 1)
                dve.wait_ge(s["xT_hi"], b + 1)
                dve.tensor_tensor(xT_lo[:, :, :], bank(0, 2).rearrange("p (k t) -> p k t", k=KC),
                                  xT_hi[:, :, :].bitcast(f32), ALU.subtract).then_inc(s["xT_lo"], 1)
                dve.wait_ge(s["kg1_hi"], b + 1)
                dve.tensor_tensor(kg1_lo[:, :], bank(6), kg1_hi[:, :].bitcast(f32), ALU.subtract).then_inc(s["kg1_lo"], 1)
                dve.wait_ge(s["kg2_psum"], b + 1)
                dve.tensor_scalar(g_min[:, :], bank(7), cols[:, 0:1], 0.0, ALU.add, ALU.min).then_inc(s["gate_min"], 1)
                dve.wait_ge(s["gate_ln"], b + 1)
                dve.wait_ge(s["gate_min"], b + 1)
                dve.tensor_tensor(g_log[:, :], g_min[:, :], g_ln[:, :], ALU.subtract).then_inc(s["gate_log"], 1)
                dve.wait_ge(s["gate_log"], b + 1)
                dve.tensor_tensor_scan(g_cum[:, :], rst, g_log[:, :], 0.0, ALU.mult, ALU.add).then_inc(s["gate_cum"], 1)
                dve.wait_ge(s["gate_cum"], b + 1)
                dve.tensor_scalar(g_last[:, :], g_cum[:, P - 1::P], 1.0 / GATE_NORM, None, ALU.mult).then_inc(s["gate_last"], 1)
                dve.wait_ge(s["decay_q"], b + 1)
                dve.wait_ge(s["q_psum"], b + 1)
                dve.tensor_tensor(qd[:, :], bank(2), dq[:, :], ALU.mult).then_inc(s["qd"], 1)
                dve.wait_ge(s["decay_k"], b + 1)
                dve.wait_ge(s["k_psum"], b + 1)
                dve.scalar_tensor_tensor(kne[:, :], bank(3), con[:, C_EVEN:C_EVEN + 1], dk[:, :], ALU.mult, ALU.mult).then_inc(s["kn"], 1)
                dve.scalar_tensor_tensor(kno[:, :], bank(3), con[:, C_ODD:C_ODD + 1], dk[:, :], ALU.mult, ALU.mult).then_inc(s["kn"], 1)
                dve.wait_ge(s["decay_end"], b + 1)
                dve.scalar_tensor_tensor(kdT[:, :], bank(3), float(DV0) ** -0.5, de[:, :], ALU.mult, ALU.mult).then_inc(s["kdT"], 1)

                def masked(r):
                    dve.wait_ge(s["at_psum"], 2 * b + r + 1)
                    hold(dve, 1 + r)
                    dve.copy_predicated(at[r][:, :, :], tri.unsqueeze(1).broadcast_to([P, 16, P]).bitcast(u32),
                                        bank(2, 4).rearrange("p (a t) -> p a t", t=P)).then_inc(s["at_sb"], 1)

                masked(0)
                dve.wait_ge(s["kv_psum"], b + 1)
                hold(dve, 3)
                for n in range(3):
                    last = dve.copy_predicated(kv[n][:, :], diag.bitcast(u32), (bank(7)[:, n * D:(n + 1) * D] if n < 2 else bank(6)[:, 0:D]))
                    last.then_inc(s["kv_sb"], 1)
                dve.wait_ge(s["kv_sb"], 3 * b + 3)
                dve.scalar_tensor_tensor(stt[1][:, :], stt[0][:, :], dq[:, 2 * P - 1:2 * P], kv[1][:, :], ALU.mult, ALU.add).then_inc(s["state"], 1)
                dve.wait_ge(s["state"], 2 * b + 1)
                dve.scalar_tensor_tensor(stt[2][:, :], stt[1][:, :], dq[:, 3 * P - 1:3 * P], kv[2][:, :], ALU.mult, ALU.add).then_inc(s["state"], 1)
                masked(1)
                dve.wait_ge(s["mean_psum"], b + 1)
                dve.tensor_tensor(cen[:, :, :], o_sb[:, :, :], bank(2, 2).rearrange("p (k t) -> p k t", k=KC), ALU.subtract).then_inc(s["centered"], 1)
                dve.wait_ge(s["centered"], b + 1)
                dve.wait_ge(s["silu_g"], b + 1)
                dve.tensor_tensor(sg[:, :, :], cen[:, :, :], sg[:, :, :], ALU.mult).then_inc(s["c_gated"], 1)
                dve.wait_ge(s["c_gated"], b + 1)
                dve.wait_ge(s["o_rstd"], b + 1)
                dve.tensor_tensor(y[:, :, :], sg[:, :, :], rs[:, :, :], ALU.mult).then_inc(s["y"], 1)
                dve.wait_ge(s["y_hi"], b + 1)
                dve.tensor_tensor(y_lo[:, :, :], y[:, :, :], y_hi[:, :, :].bitcast(f32), ALU.subtract).then_inc(s["y_lo"], 1)
                dve.wait_ge(s["wo_psum"], b + 1)
                dve.tensor_tensor(xb(b), xb(b), bank(6, 2), ALU.add).then_inc(s["x_out"], 1)
                dve.wait_ge(s["x_out"], b + 1)

        @block.tensor
        def _(pe):
            pe.wait_ge(s["con_in"], 32)
            with pe.Fori(0, B) as b:
                pe.wait_ge(s["xhat"], b + 1)
                for i in range(NT):
                    for k in range(KC):
                        last = pe.transpose(bank(k)[:, i * P:(i + 1) * P], xhat[:, i, k * P:(k + 1) * P], ident)
                last.then_inc(s["xT_psum"], 1)
                pe.wait_ge(s["xT_lo"], b + 1)
                pe.wait_ge(s["w_lo"], 1)

                def project(out, col):
                    for k in range(KC):
                        last = mm3(pe, out, w_hi[:, k, col:col + P], w_lo[:, k, col:col + P], xT_hi[:, k, :], xT_lo[:, k, :], k == 0, k == KC - 1)
                    return last

                project(bank(6), W0R).then_inc(s["kg1_psum"], 1)
                project(bank(2), W0Q).then_inc(s["q_psum"], 1)
                project(bank(3), W0K).then_inc(s["k_psum"], 1)
                pe.wait_ge(s["kg1_lo"], b + 1)
                pe.wait_ge(s["wr_lo"], 1)
                mm3(pe, bank(7), wr_hi[:, :], wr_lo[:, :], kg1_hi[:, :], kg1_lo[:, :], True, True).then_inc(s["kg2_psum"], 1)
                for i in range(NT):
                    for k in range(KC):
                        tt = slice(i * P, (i + 1) * P)
                        last = mm3(pe, bank(i // 2)[:, (i % 2) * D:(i % 2 + 1) * D], xT_hi[:, k, tt], xT_lo[:, k, tt],
                                   w_hi[:, k, W0V:W0V + D], w_lo[:, k, W0V:W0V + D], k == 0, k == KC - 1)
                last.then_inc(s["v_psum"], 1)
                project(bank(4), W0G)
                project(bank(5), W0G + P).then_inc(s["g_psum"], 1)
                pe.wait_ge(s["kdT"], b + 1)
                for n in range(NT):
                    last = pe.transpose(bank(6)[:, n * P:(n + 1) * P], kdT[:, n * P:(n + 1) * P], ident)
                last.then_inc(s["kd_psum"], 1)
                pe.wait_ge(s["kn"], 2 * b + 2)
                pe.wait_ge(s["qd"], b + 1)
                pe.wait_ge(s["silu_g"], b + 1)

                def scores(r):
                    for n in (2 * r, 2 * r + 1):
                        for par in range(2):
                            for pr in range(4):
                                row = slice(32 * pr, 32 * pr + 32)
                                col = ((n % 2) * 2 + par) * P
                                last = pe.matmul(bank(2 + pr)[:, col:col + P], (kne, kno)[par][row, n * P:(n + 1) * P],
                                                 qd[row, n * P:(n + 1) * P], start=True, stop=True, tile_position=(32 * pr, 0),
                                                 skip_group_check=True)
                    last.then_inc(s["at_psum"], 1)

                scores(0)
                pe.wait_ge(s["kd"], b + 1)
                pe.wait_ge(s["v_sb"], b + 1)
                for n in range(3):
                    last = pe.matmul(bank(7)[:, n * D:(n + 1) * D] if n < 2 else bank(6)[:, 0:D], kd[:, n, :], v_sb[:, n, :],
                                     start=True, stop=True, skip_group_check=True)
                last.then_inc(s["kv_psum"], 1)
                for n in range(NT):
                    if n == 0:
                        pe.wait_ge(s["at_sb"], 2 * b + 1)
                        scores(1)
                    if n == 2:
                        pe.wait_ge(s["at_sb"], 2 * b + 2)
                    if n > 0:
                        if n == 1:
                            pe.wait_ge(s["kv_sb"], 3 * b + 3)
                        else:
                            pe.wait_ge(s["state"], 2 * b + n - 1)
                        for h in range(KC):
                            pe.matmul(bank(h)[:, n * P:(n + 1) * P], stt[n - 1][:, h * P:(h + 1) * P], qd[:, n * P:(n + 1) * P],
                                      start=True, stop=False, skip_group_check=True)
                    for h in range(H0):
                        q = 32 * (h % 4)
                        last = pe.matmul(bank(h // 4)[q:q + 32, n * P:(n + 1) * P], v_sb[:, n, h * DV0:(h + 1) * DV0],
                                         at[n // 2][:, (h // 2) * 4 + (n % 2) * 2 + h % 2, :], start=(n == 0), stop=True,
                                         tile_position=(0, q), skip_group_check=True)
                last.then_inc(s["ot_psum"], 1)
                pe.wait_ge(s["o_sb"], b + 1)
                for h in range(KC):
                    last = pe.matmul(bank(2 + h), avg, o_sb[:, h, :], start=True, stop=True)
                last.then_inc(s["mean_psum"], 1)
                pe.wait_ge(s["sq"], b + 1)
                for h in range(KC):
                    last = pe.matmul(bank(4 + h), avg, sq[:, h, :], start=True, stop=True)
                last.then_inc(s["var_psum"], 1)
                pe.wait_ge(s["y_lo"], b + 1)
                pe.wait_ge(s["wo_lo"], 1)
                for i in range(NT):
                    for k in range(KC):
                        tt = slice(i * P, (i + 1) * P)
                        last = mm3(pe, bank(6 + i // 2)[:, (i % 2) * D:(i % 2 + 1) * D], y_hi[:, k, tt], y_lo[:, k, tt],
                                   wo_hi[:, k, :], wo_lo[:, k, :], k == 0, k == KC - 1)
                last.then_inc(s["wo_psum"], 1)


class Chain:

    def __init__(self, engine, sem):
        self.engine, self.sem, self.n = engine, sem, 0

    def __call__(self, ins):
        self.n += 1
        ins.then_inc(self.sem, 1)
        self.engine.wait_ge(self.sem, self.n)


def experts(nc, kept, tag, x, psum, con, conb, dram, weights, chunks, group, router, n_exp, sel_name, route_weights):
    groups = chunks // group
    per_group = B * group
    n = B * NT
    ctx = ExitStack()
    with ctx:
        def sb(name, shape, dt=f32):
            return ctx.enter_context(nc.sbuf_tensor(f"{tag}_{name}", shape, dt))

        s = sems(nc, kept, tag, "small_in stats moments chain ln_var rstd0 xhat xT_psum xT_hi xT_lo r_hi r_lo logits "
                 "z inh dist w0 fb wx wT_psum wT split_hi split_lo gate_psum up_psum silu gated scaled h_hi h_lo down y_added")
        raw_in = list(sems(nc, kept, tag, " ".join(f"raw_in{c}" for c in range(group))).values())
        WN = 2 * KC * P + D
        raw, w_hi, w_lo = sb("raw", [P, group, WN]), sb("w_hi", [P, group, WN], f32r), sb("w_lo", [P, group, WN], f32r)
        sel = sb("sel", [WR, chunks * P], bf16)
        r_raw, r_hi, r_lo = sb("r_raw", [P, KC, n_exp]), sb("r_hi", [P, KC, n_exp], f32r), sb("r_lo", [P, KC, n_exp], f32r)
        st, mv = sb("st", [P, n, 6]), sb("mv", [P, n, 2])
        ve, lnv, r0, n1, n2, rstd = (sb(k, [P, n]) for k in ("ve", "lnv", "r0", "n1", "n2", "rstd"))
        xT_hi, xT_lo = sb("xT_hi", [P, KC, B * T], f32r), sb("xT_lo", [P, KC, B * T], f32r)
        wx, wT = sb("wx", [P, n, WR], bf16), sb("wT", [WR, B * T], bf16)
        sil, gat, h = ([sb(f"{k}{i}", [P, T]) for i in range(2)] for k in ("sil", "gat", "h"))
        h_hi, h_lo = ([sb(f"{k}{i}", [P, T], f32r) for i in range(2)] for k in ("h_hi", "h_lo"))
        side = sb("side", [P, E1 + E0 * E0 + E1 * E1 + G1 * G1])
        bank = lambda i, m=1: psum[:, 512 * i:512 * (i + m)]
        ident = con[:, C_ID:C_ID + P]
        zero = con[:, C_ODD + 2:C_ODD + 3]
        xhat = [sb(f"xhat{i}", [P, NT, D]) for i in range(2)]
        routing = route_weights(sb, s)
        block = ctx.enter_context(nc.Block())

        @block.sync
        def _(sp):
            sp.dma_start(r_raw[:, :, :], dram[router]).then_inc(s["small_in"], 16)
            if n_exp == E0:
                sp.dma_start(side[:, 0:1], dram["temp"].broadcast_to([P, 1])).then_inc(s["small_in"], 16)
            else:
                sp.dma_start(side[:, 0:E1], dram["ebias"].broadcast_to([P, E1])).then_inc(s["small_in"], 16)
            sp.dma_start(side[:, E1:], dram["tie"]).then_inc(s["small_in"], 16)
            sp.dma_start(sel[:, :], dram[sel_name].rearrange("r c p -> r (c p)").bitcast(bf16)).then_inc(s["small_in"], 16)

            for c in range(group):
                sp.dma_start(raw[:, c, :], dram[weights][c]).then_inc(raw_in[c], 16)
            with sp.Fori(1, groups) as g:
                for c in range(group):
                    sp.wait_ge(s["split_lo"], (g - 1) * group + c + 1)
                    sp.dma_start(raw[:, c, :], dram[weights][bass.ds(g * group + c, 1), :, :].rearrange("a p n -> (a p) n")).then_inc(raw_in[c], 16)

        @block.gpsimd
        def _(pool):
            pool.wait_ge(s["small_in"], 64)
            pool.tensor_copy(r_hi[:, :, :], r_raw[:, :, :]).then_inc(s["r_hi"], 1)
            pool.wait_ge(s["r_hi"], 1)
            pool.tensor_tensor(r_lo[:, :, :], r_raw[:, :, :], r_hi[:, :, :].bitcast(f32), ALU.subtract).then_inc(s["r_lo"], 1)

            def split_chunk(g, c, first):
                k = g * group + c
                pool.wait_ge(raw_in[c], (g + 1) * 16)
                if not first:
                    pool.wait_ge(s["down"], (g - 1) * per_group + (B - 1) * group + c + 1)
                pool.tensor_tensor(w_hi[:, c, :], raw[:, c, :], zero.broadcast_to([P, WN]), ALU.add).then_inc(s["split_hi"], 1)
                pool.wait_ge(s["split_hi"], k + 1)
                pool.tensor_tensor(w_lo[:, c, :], raw[:, c, :], w_hi[:, c, :].bitcast(f32), ALU.subtract).then_inc(s["split_lo"], 1)

            for c in range(group):
                split_chunk(0, c, True)
            with pool.Fori(1, groups) as g:
                for c in range(group):
                    split_chunk(g, c, False)

        @block.scalar
        def _(act):
            act.preload_act_table_set(LN_EXP_SET)
            act.wait_ge(s["chain"], 1)
            act.activation(lnv[:, :], ve[:, :], ACT.Ln).then_inc(s["ln_var"], 1)
            act.wait_ge(s["ln_var"], 1)
            act.activation(r0[:, :], lnv[:, :], ACT.Exp, scale=-0.5).then_inc(s["rstd0"], 1)
            for b in range(B):
                act.wait_ge(s["xT_psum"], b + 1)
                act.activation(xT_hi[:, :, b * T:(b + 1) * T], bank(2 * (b % 2), 2).rearrange("p (k t) -> p k t", k=KC), ACT.Copy).then_inc(s["xT_hi"], 1)
            routing["scalar"](act, bank(4)[:, 0:n * n_exp])
            act.wait_ge(s["wT_psum"], 1)
            act.activation(wT[:, :], bank(6, 2)[0:WR, :].bitcast(bf16)[:, 0:B * T], ACT.Copy).then_inc(s["wT"], 1)

            def unit(u, i, first):
                q = i % 2
                act.wait_ge(s["gate_psum"], u + 1)
                if not (first and i < 2):
                    act.wait_ge(s["gated"], u - 1)
                act.activation(sil[q][:, :], bank(2 + q), ACT.Silu).then_inc(s["silu"], 1)
                act.wait_ge(s["scaled"], u + 1)
                if not (first and i < 2):
                    act.wait_ge(s["down"], u - 1)
                act.activation(h_hi[q][:, :], h[q][:, :], ACT.Copy).then_inc(s["h_hi"], 1)

            for i in range(per_group):
                unit(i, i, True)
            with act.Fori(1, groups) as g:
                for i in range(per_group):
                    unit(g * per_group + i, i, False)

        @block.vector
        def _(dve):
            for i in range(n):
                last = dve.bn_stats(st[:, i, :], x[:, i * D:(i + 1) * D])
            last.then_inc(s["stats"], 1)
            dve.wait_ge(s["stats"], 1)
            for i in range(n):
                last = dve.bn_aggr(mv[:, i, :], st[:, i, :])
            last.then_inc(s["moments"], 1)
            dve.wait_ge(s["moments"], 1)
            step = Chain(dve, s["chain"])
            step(dve.tensor_scalar(ve[:, :], mv[:, :, 1], EPS, None, ALU.add))
            dve.wait_ge(s["rstd0"], 1)
            step(dve.scalar_tensor_tensor(n1[:, :], r0[:, :], -0.5, r0[:, :], ALU.mult, ALU.mult))
            step(dve.tensor_tensor(n2[:, :], n1[:, :], ve[:, :], ALU.mult))
            step(dve.scalar_tensor_tensor(rstd[:, :], n2[:, :], 1.5, r0[:, :], ALU.add, ALU.mult))

            def normal(b):
                if b >= 2:
                    dve.wait_ge(s["xT_psum"], b - 1)
                for i in range(NT):
                    j = b * NT + i
                    last = dve.tensor_scalar(xhat[b % 2][:, i, :], x[:, j * D:(j + 1) * D], mv[:, j, 0:1], rstd[:, j:j + 1], ALU.subtract, ALU.mult)
                last.then_inc(s["xhat"], 1)

            normal(0)
            for b in range(B):
                if b + 1 < B:
                    normal(b + 1)
                dve.wait_ge(s["xT_hi"], b + 1)
                dve.tensor_tensor(xT_lo[:, :, b * T:(b + 1) * T], bank(2 * (b % 2), 2).rearrange("p (k t) -> p k t", k=KC),
                                  xT_hi[:, :, b * T:(b + 1) * T].bitcast(f32), ALU.subtract).then_inc(s["xT_lo"], 1)
            dve.wait_ge(s["small_in"], 64)
            w = routing["vector"](dve, step, bank(4)[:, 0:n * n_exp], side)
            parts = (wx[:, :, 0:n_exp], wx[:, :, n_exp:2 * n_exp], wx[:, :, 2 * n_exp:3 * n_exp])
            rest = [routing["rest0"], routing["rest1"]]
            step(dve.memset(wx[:, :, 3 * n_exp:], 0.0))
            if n_exp == E1:
                step(dve.memset(wx[:, :, 3 * E1:3 * E1 + 1], 1.0))
            step(dve.tensor_copy(parts[0], w))
            step(dve.tensor_tensor(rest[0][:, :, :], w, parts[0], ALU.subtract))
            step(dve.tensor_copy(parts[1], rest[0][:, :, :]))
            step(dve.tensor_tensor(rest[1][:, :, :], rest[0][:, :, :], parts[1], ALU.subtract))
            dve.tensor_copy(parts[2], rest[1][:, :, :]).then_inc(s["wx"], 1)

            def unit(u, i, first):
                q = i % 2
                dve.wait_ge(s["up_psum"], u + 1)
                dve.wait_ge(s["silu"], u + 1)
                dve.tensor_tensor(gat[q][:, :], bank(4 + q), sil[q][:, :], ALU.mult).then_inc(s["gated"], 1)
                if not (first and i < 2):
                    dve.wait_ge(s["h_lo"], u - 1)
                dve.wait_ge(s["gated"], u + 1)
                dve.tensor_tensor(h[q][:, :], bank(6 + q), gat[q][:, :], ALU.mult).then_inc(s["scaled"], 1)
                dve.wait_ge(s["h_hi"], u + 1)
                dve.tensor_tensor(h_lo[q][:, :], h[q][:, :], h_hi[q][:, :].bitcast(f32), ALU.subtract).then_inc(s["h_lo"], 1)

            def gather(y, b):
                dve.wait_ge(s["down"], (y + 1) * group)
                xs = x[:, b * NT * D:(b + 1) * NT * D]
                dve.tensor_tensor(xs, xs, bank(0, 2), ALU.add).then_inc(s["y_added"], 1)

            def run(g, first):
                for b in range(B):
                    for c in range(group):
                        i = b * group + c
                        unit(g * per_group + i, i, first)
                        if c == 0 and not (first and b == 0):
                            gather(g * B + b - 1, (b - 1) % B)

            run(0, True)
            with dve.Fori(1, groups) as g:
                run(g, False)
            gather(groups * B - 1, B - 1)

        @block.tensor
        def _(pe):
            for b in range(B):
                pe.wait_ge(s["xhat"], b + 1)
                if b >= 2:
                    pe.wait_ge(s["xT_lo"], b - 1)
                for i in range(NT):
                    for k in range(KC):
                        last = pe.transpose(bank(2 * (b % 2) + k)[:, i * P:(i + 1) * P], xhat[b % 2][:, i, k * P:(k + 1) * P], ident)
                last.then_inc(s["xT_psum"], 1)
            pe.wait_ge(s["r_lo"], 1)
            for i in range(n):
                if i % NT == 0:
                    pe.wait_ge(s["xT_lo"], i // NT + 1)
                for k in range(KC):
                    tt = slice(i * P, (i + 1) * P)
                    last = mm3(pe, bank(4)[:, i * n_exp:(i + 1) * n_exp], xT_hi[:, k, tt], xT_lo[:, k, tt], r_hi[:, k, :], r_lo[:, k, :], k == 0, k == KC - 1)
            last.then_inc(s["logits"], 1)
            pe.wait_ge(s["wx"], 1)
            wT_out = bank(6, 2)[0:WR, :].bitcast(bf16)
            for i in range(n):
                last = pe.transpose(wT_out[:, i * P:(i + 1) * P], wx[:, i, :], conb[:, 0:P])
            last.then_inc(s["wT_psum"], 1)
            pe.wait_ge(s["wT"], 1)

            def up(u, i, first, fresh):
                b, c, q = i // group, i % group, i % 2
                tt = slice(b * T, (b + 1) * T)
                if fresh is not None:
                    pe.wait_ge(s["split_lo"], fresh)
                for name, at, out, used in (("gate_psum", 0, bank(2 + q), "silu"), ("up_psum", KC * P, bank(4 + q), "gated")):
                    if not (first and i < 2):
                        pe.wait_ge(s[used], u - 1)
                    for k in range(KC):
                        cc = slice(at + k * P, at + (k + 1) * P)
                        last = mm3(pe, out, w_hi[:, c, cc], w_lo[:, c, cc], xT_hi[:, k, tt], xT_lo[:, k, tt], k == 0, k == KC - 1)
                    if name == "gate_psum":
                        last.then_inc(s[name], 1)

            def spread(u, i, first, chunk):
                b, q = i // group, i % 2
                tt = slice(b * T, (b + 1) * T)
                if not (first and i < 2):
                    pe.wait_ge(s["scaled"], u - 1)
                pe.matmul(bank(6 + q), sel[:, chunk * P:(chunk + 1) * P] if isinstance(chunk, int) else sel[:, bass.ds(chunk * P, P)], wT[:, tt], start=True, stop=True).then_inc(s["up_psum"], 1)

            def down(u, i, y):
                c, q = i % group, i % 2
                pe.wait_ge(s["h_lo"], u + 1)
                if c == 0 and y is not None:
                    pe.wait_ge(s["y_added"], y)
                for t in range(NT):
                    out = bank(t // 2)[:, (t % 2) * D:(t % 2 + 1) * D]
                    dn = slice(2 * KC * P, 2 * KC * P + D)
                    tt = slice(t * P, (t + 1) * P)
                    last = mm3(pe, out, h_hi[q][:, tt], h_lo[q][:, tt], w_hi[:, c, dn], w_lo[:, c, dn], c == 0 and t % 2 == 0, c == group - 1)
                last.then_inc(s["down"], 1)

            def run(g, first):
                for i in range(per_group):
                    u = g * per_group + i
                    c = i % group
                    up(u, i, first, g * group + c + 1 if i < group else None)
                    spread(u, i, first, g * group + c)
                    if not (first and i == 0):
                        j = (i - 1) % per_group
                        bj = (i - 1) // group
                        y = None if first and bj == 0 else g * B + bj
                        down(u - 1, j, y)

            run(0, True)
            with pe.Fori(1, groups) as g:
                run(g, False)
            down(groups * per_group - 1, per_group - 1, groups * B - 1)


def golden_route(sb, s):
    n = B * NT
    inv = sb("inv_temp", [P, 1])
    z, inh, off, dist, w0, fb, zone, w1, rank, fw, rest0, rest1 = (
        sb(k, [P, n, E0]) for k in ("z", "inh", "off", "dist", "w0", "fb", "zone", "w1", "rank", "fw", "rest0", "rest1"))
    less, same = sb("less", [P, n, E0, E0]), sb("same", [P, n, E0, E0])
    wsum, none, some, fsum, finv, total, tinv = (sb(k, [P, n]) for k in ("wsum", "none", "some", "fsum", "finv", "total", "tinv"))
    flat = lambda t: t[:, :, :].rearrange("p i e -> p (i e)")
    wide = lambda t: t[:, :].unsqueeze(2).broadcast_to([P, n, E0])

    def scalar(act, logits):
        act.wait_ge(s["z"], 1)
        act.activation(flat(inh), flat(z), ACT.Sigmoid).then_inc(s["inh"], 1)
        act.wait_ge(s["dist"], 1)
        act.activation(flat(w0), flat(dist), ACT.Exp, scale=-1.0 / 0.1).then_inc(s["w0"], 1)
        act.activation(flat(fb), flat(dist), ACT.Exp, scale=-1.0 / 0.3).then_inc(s["fb"], 1)

    def vector(dve, step, logits, side):
        tie = side[:, E1:E1 + E0 * E0].rearrange("p (a c) -> p a c", a=E0).unsqueeze(1).broadcast_to([P, n, E0, E0])
        step(dve.reciprocal(inv[:, :], side[:, 0:1]))
        dve.wait_ge(s["logits"], 1)
        dve.tensor_scalar(flat(z), logits, inv[:, 0:1], None, ALU.mult).then_inc(s["z"], 1)
        dve.wait_ge(s["inh"], 1)
        step(dve.tensor_scalar(flat(off), flat(inh), CENTER, None, ALU.subtract))
        dve.scalar_tensor_tensor(flat(dist), flat(off), -1.0, flat(off), ALU.mult, ALU.max).then_inc(s["dist"], 1)
        dve.wait_ge(s["dist"], 1)
        step(dve.tensor_scalar(flat(zone), flat(inh), LOWER, None, ALU.is_ge))
        step(dve.scalar_tensor_tensor(flat(off), flat(inh), UPPER, flat(zone), ALU.is_le, ALU.mult))
        step(dve.tensor_tensor(less[:, :, :, :], dist[:, :, :].unsqueeze(2).broadcast_to([P, n, E0, E0]),
                               dist[:, :, :].unsqueeze(3).broadcast_to([P, n, E0, E0]), ALU.is_lt))
        step(dve.tensor_tensor(same[:, :, :, :], dist[:, :, :].unsqueeze(2).broadcast_to([P, n, E0, E0]),
                               dist[:, :, :].unsqueeze(3).broadcast_to([P, n, E0, E0]), ALU.is_equal))
        step(dve.tensor_tensor(same[:, :, :, :], same[:, :, :, :], tie, ALU.mult))
        step(dve.tensor_tensor(less[:, :, :, :], less[:, :, :, :], same[:, :, :, :], ALU.add))
        step(dve.tensor_reduce(rank[:, :, :], less[:, :, :, :], AX.X, ALU.add))
        dve.wait_ge(s["fb"], 1)
        step(dve.scalar_tensor_tensor(flat(fw), flat(rank), float(TOP0), flat(fb), ALU.is_lt, ALU.mult))
        step(dve.tensor_reduce(fsum[:, :], fw[:, :, :], AX.X, ALU.add))
        step(dve.tensor_scalar(fsum[:, :], fsum[:, :], 1e-8, None, ALU.max))
        step(dve.reciprocal(finv[:, :], fsum[:, :]))
        step(dve.tensor_tensor(fw[:, :, :], fw[:, :, :], wide(finv), ALU.mult))
        step(dve.tensor_tensor(flat(w1), flat(w0), flat(off), ALU.mult))
        step(dve.tensor_reduce(wsum[:, :], w1[:, :, :], AX.X, ALU.add))
        step(dve.tensor_scalar(none[:, :], wsum[:, :], 1e-8, None, ALU.is_lt))
        step(dve.tensor_scalar(some[:, :], none[:, :], -1.0, 1.0, ALU.mult, ALU.add))
        step(dve.tensor_tensor(fw[:, :, :], fw[:, :, :], wide(none), ALU.mult))
        step(dve.tensor_tensor(w1[:, :, :], w1[:, :, :], wide(some), ALU.mult))
        step(dve.tensor_tensor(flat(w1), flat(w1), flat(fw), ALU.add))
        step(dve.tensor_reduce(total[:, :], w1[:, :, :], AX.X, ALU.add))
        step(dve.tensor_scalar(total[:, :], total[:, :], 1e-8, None, ALU.max))
        step(dve.reciprocal(tinv[:, :], total[:, :]))
        step(dve.tensor_tensor(w1[:, :, :], w1[:, :, :], wide(tinv), ALU.mult))
        return w1[:, :, :]

    return {"scalar": scalar, "vector": vector, "rest0": rest0, "rest1": rest1}


def top_route(sb, s):
    n, m = B * NT, E1 // G1
    sig, sc, ms, rank, w1, rest0, rest1 = (sb(k, [P, n, E1]) for k in ("sig", "sc", "ms", "rank", "w1", "rest0", "rest1"))
    less, same = sb("less", [P, NT, E1, E1]), sb("same", [P, NT, E1, E1])
    gmax, grank, gm, pen = (sb(k, [P, n, G1]) for k in ("gmax", "grank", "gm", "pen"))
    gless, gsame = sb("gless", [P, n, G1, G1]), sb("gsame", [P, n, G1, G1])
    total, tinv = sb("total", [P, n]), sb("tinv", [P, n])
    flat = lambda t: t[:, :, :].rearrange("p i e -> p (i e)")
    grouped = lambda t: t[:, :, :].rearrange("p i (g e) -> p (i g) e", g=G1)
    spread = lambda t: t[:, :, :].rearrange("p i g -> p (i g)").unsqueeze(2).broadcast_to([P, n * G1, m])

    def scalar(act, logits):
        act.wait_ge(s["logits"], 1)
        act.activation(flat(sig), logits, ACT.Sigmoid).then_inc(s["inh"], 1)

    def vector(dve, step, logits, side):
        t0 = E1 + E0 * E0
        tie = side[:, t0:t0 + E1 * E1].rearrange("p (a c) -> p a c", a=E1).unsqueeze(1).broadcast_to([P, NT, E1, E1])
        gtie = side[:, t0 + E1 * E1:].rearrange("p (a c) -> p a c", a=G1).unsqueeze(1).broadcast_to([P, n, G1, G1])
        dve.wait_ge(s["inh"], 1)
        step(dve.tensor_tensor(sc[:, :, :], sig[:, :, :], side[:, 0:E1].unsqueeze(1).broadcast_to([P, n, E1]), ALU.add))
        step(dve.tensor_reduce(gmax[:, :, :].rearrange("p i g -> p (i g)"), grouped(sc), AX.X, ALU.max))
        a, c = gmax[:, :, :].unsqueeze(2).broadcast_to([P, n, G1, G1]), gmax[:, :, :].unsqueeze(3).broadcast_to([P, n, G1, G1])
        step(dve.tensor_tensor(gless[:, :, :, :], a, c, ALU.is_gt))
        step(dve.tensor_tensor(gsame[:, :, :, :], a, c, ALU.is_equal))
        step(dve.tensor_tensor(gsame[:, :, :, :], gsame[:, :, :, :], gtie, ALU.mult))
        step(dve.tensor_tensor(gless[:, :, :, :], gless[:, :, :, :], gsame[:, :, :, :], ALU.add))
        step(dve.tensor_reduce(grank[:, :, :], gless[:, :, :, :], AX.X, ALU.add))
        step(dve.tensor_scalar(flat(gm), flat(grank), float(TOPG1), None, ALU.is_lt))
        step(dve.tensor_scalar(flat(pen), flat(gm), -1.0, BIG, ALU.add, ALU.mult))
        step(dve.tensor_tensor(grouped(ms), grouped(sc), spread(gm), ALU.mult))
        step(dve.tensor_tensor(grouped(ms), grouped(ms), spread(pen), ALU.add))
        for b in range(B):
            mb = ms[:, b * NT:(b + 1) * NT, :]
            a, c = mb.unsqueeze(2).broadcast_to([P, NT, E1, E1]), mb.unsqueeze(3).broadcast_to([P, NT, E1, E1])
            step(dve.tensor_tensor(less[:, :, :, :], a, c, ALU.is_gt))
            step(dve.tensor_tensor(same[:, :, :, :], a, c, ALU.is_equal))
            step(dve.tensor_tensor(same[:, :, :, :], same[:, :, :, :], tie, ALU.mult))
            step(dve.tensor_tensor(less[:, :, :, :], less[:, :, :, :], same[:, :, :, :], ALU.add))
            step(dve.tensor_reduce(rank[:, b * NT:(b + 1) * NT, :], less[:, :, :, :], AX.X, ALU.add))
        step(dve.scalar_tensor_tensor(flat(w1), flat(rank), float(TOP1), flat(sig), ALU.is_lt, ALU.mult))
        step(dve.tensor_reduce(total[:, :], w1[:, :, :], AX.X, ALU.add))
        step(dve.reciprocal(tinv[:, :], total[:, :]))
        step(dve.tensor_tensor(w1[:, :, :], w1[:, :, :], tinv[:, :].unsqueeze(2).broadcast_to([P, n, E1]), ALU.mult))
        return w1[:, :, :]

    return {"scalar": scalar, "vector": vector, "rest0": rest0, "rest1": rest1}


def rotary_attention(nc, kept, x, psum, con, conb, dram):
    ctx = ExitStack()
    with ctx:
        def sb(name, shape, dt=f32):
            return ctx.enter_context(nc.sbuf_tensor(f"a1_{name}", shape, dt))

        s = sems(nc, kept, "a1", "rope_in w_in wo_in small_in w_hi w_lo wo_hi wo_lo sel_r v_pad "
                 "stats moments var_eps ln_var rstd0 newton ln_ms rms0 rms_newton xhat xr xT_psum xw xT_hi xT_lo residual "
                 "q_psum k_psum v_psum v_sb rot q_rot k_rot rot_hi rot_lo stack_psum stack_sb "
                 "score_psum max neg_max p_ready pt_psum pt_sb ot_psum recip spread_in rb_psum rb o_t o_hi o_lo wo_psum x_out")
        w_hi, w_lo = sb("w_hi", [P, KC, W1N], f32r), sb("w_lo", [P, KC, W1N], f32r)
        wo_hi, wo_lo = sb("wo_hi", [P, NST, D], f32r), sb("wo_lo", [P, NST, D], f32r)
        rope = sb("rope", [P, C_SEL])
        sel = sb("sel", [P, 16 * P], f32r)
        cols, rows = sb("cols", [P, 6]), sb("rows", [P, 2 * D])
        st, mv = sb("st", [P, NT, 6]), sb("mv", [P, NT, 2])
        ve, lnv, r0, n1, n2, rstd, ms, lnm, m0, m1, m2, rms = (
            sb(k, [P, NT]) for k in ("ve", "lnv", "r0", "n1", "n2", "rstd", "ms", "lnm", "m0", "m1", "m2", "rms"))
        xhat, xr = sb("xhat", [P, NT, D]), sb("xr", [P, NT, D])
        xw = sb("xw", [P, KC, T])
        xT_hi, xT_lo = sb("xT_hi", [P, KC, T], f32r), sb("xT_lo", [P, KC, T], f32r)
        ra, rb_ = sb("ra", [P, 2, T]), sb("rb_", [P, 2, T])
        rot = sb("rot", [P, 2, T])
        rot_hi, rot_lo = sb("rot_hi", [P, 2, T], f32r), sb("rot_lo", [P, 2, T], f32r)
        stack = [sb("q_stack", [P, NST, T], f32r), sb("k_stack", [P, NST, T], f32r)]
        vs = sb("vs", [P, NT, H1, 32])
        prob = [sb(f"prob{i}", [P, 2, T]) for i in range(2)]
        pt = [sb(f"pt{i}", [P, NT, 2, P]) for i in range(2)]
        mx, nb = sb("mx", [P, 2 * NST * NT, 2]), sb("nb", [P, 2 * NST * NT, 2])
        rsum, rinv = sb("rsum", [P, NST, NT, HPT]), sb("rinv", [P, NST, NT, HPT])
        rwide = sb("rwide", [P, NT, HPT, 32])
        rb_sb, o_t = sb("rb_sb", [P, T]), sb("o_t", [P, NST, T])
        o_hi, o_lo = sb("o_hi", [P, NST, T], f32r), sb("o_lo", [P, NST, T], f32r)
        held = sb("held", [P, 4])
        bank = lambda i, m=1: psum[:, 512 * i:512 * (i + m)]
        ident = con[:, C_ID:C_ID + P]
        xb = lambda b: x[:, bass.ds(b * NT * D, NT * D)]
        NU = 2 * NST * NT
        units = [(t, i, pr) for t in range(NST) for i in range(NT) for pr in range(2)]
        halves = [(n, r) for n, (t, i, pr) in enumerate(units) for r in range(1 if i < 2 else 2)]
        NH = len(halves)
        half_at = {nr: k for k, nr in enumerate(halves)}
        last_half = {n: max(k for k, (m, r) in enumerate(halves) if m == n) for n in range(NU)}

        def hold(dve, place):
            dve.tensor_copy(held[:, place:place + 1], con[:, 0:1])

        w_raw, wo_raw, sel_raw = sb("w_raw", [P, KC, W1N]), sb("wo_raw", [P, NST, D]), sb("sel_raw", [P, 16 * P])

        block = ctx.enter_context(nc.Block())

        @block.sync
        def _(sp):
            sp.dma_start(w_raw[:, :, :], dram["w1"]).then_inc(s["w_in"], 16)
            sp.dma_start(cols[:, :], dram["cols1"]).then_inc(s["small_in"], 16)
            sp.dma_start(rows[:, :], dram["rows1"].broadcast_to([P, 2 * D])).then_inc(s["small_in"], 16)
            sp.dma_start(rope[:, :], dram["rope"][:, 0:C_SEL]).then_inc(s["small_in"], 16)
            sp.dma_start(sel_raw[:, :], dram["rope"][:, C_SEL:]).then_inc(s["rope_in"], 16)
            sp.dma_start(wo_raw[:, :, :], dram["wo1"]).then_inc(s["wo_in"], 16)

        @block.gpsimd
        def _(pool):
            pool.memset(vs[:, :, :, :], 0.0).then_inc(s["v_pad"], 1)
            for raw, hi, lo, came, s_hi, s_lo in ((w_raw, w_hi, w_lo, "w_in", "w_hi", "w_lo"), (wo_raw, wo_hi, wo_lo, "wo_in", "wo_hi", "wo_lo")):
                pool.wait_ge(s[came], 16)
                pool.tensor_copy(hi[:], raw[:]).then_inc(s[s_hi], 1)
                pool.wait_ge(s[s_hi], 1)
                pool.tensor_tensor(lo[:], raw[:], hi[:].bitcast(f32), ALU.subtract).then_inc(s[s_lo], 1)
                if came == "w_in":
                    pool.wait_ge(s["rope_in"], 16)
                    pool.tensor_copy(sel[:, :], sel_raw[:, :]).then_inc(s["sel_r"], 1)

        @block.scalar
        def _(act):
            act.wait_ge(s["small_in"], 48)
            act.preload_act_table_set(LN_EXP_SET)
            with act.Fori(0, B) as b:
                act.wait_ge(s["var_eps"], b + 1)
                act.activation(lnv[:, :], ve[:, :], ACT.Ln).then_inc(s["ln_var"], 1)
                act.wait_ge(s["ln_var"], b + 1)
                act.activation(r0[:, :], lnv[:, :], ACT.Exp, scale=-0.5).then_inc(s["rstd0"], 1)
                act.wait_ge(s["newton"], 6 * b + 6)
                act.activation(lnm[:, :], ms[:, :], ACT.Ln).then_inc(s["ln_ms"], 1)
                act.wait_ge(s["ln_ms"], b + 1)
                act.activation(m0[:, :], lnm[:, :], ACT.Exp, scale=-0.5).then_inc(s["rms0"], 1)
                act.wait_ge(s["xT_psum"], b + 1)
                for k in range(KC):
                    last = act.activation(xw[:, k, :], bank(k), ACT.Copy, scale=cols[:, 4 + k:5 + k])
                last.then_inc(s["xw"], 1)
                act.wait_ge(s["xw"], b + 1)
                act.activation(xT_hi[:, :, :], xw[:, :, :], ACT.Copy).then_inc(s["xT_hi"], 1)
                for w, name in enumerate(("q_rot", "k_rot")):
                    act.wait_ge(s[name], b + 1)
                    act.activation(rot_hi[:, w, :], rot[:, w, :], ACT.Copy).then_inc(s["rot_hi"], 1)
                for k in range(2 * NST):
                    act.wait_ge(s["stack_psum"], 2 * NST * b + k + 1)
                    act.activation(stack[k % 2][:, k // 2, :], bank(6 + k % 2), ACT.Copy).then_inc(s["stack_sb"], 1)

                def exps(n):
                    t, i, pr = units[n]
                    act.wait_ge(s["neg_max"], NU * b + n + 1)
                    w = (i + 1) * P
                    for e in range(2):
                        last = act.activation(prob[n % 2][:, e, 0:w], bank(2 + 2 * (n % 2) + e)[:, 0:w], ACT.Exp,
                                              bias=nb[:, n, e:e + 1], scale=0.5, accum_out=rsum[:, t, i, 2 * pr + e:2 * pr + e + 1])
                    last.then_inc(s["p_ready"], 1)

                def half(k):
                    n, r = halves[k]
                    m = min(2, units[n][1] + 1 - 2 * r)
                    act.wait_ge(s["pt_psum"], NH * b + k + 1)
                    act.activation(pt[n % 2][:, 2 * r:2 * r + m, :, :], bank(6 + r)[:, 0:m * 2 * P].rearrange("p (j e t) -> p j e t", j=m, e=2),
                                   ACT.Copy).then_inc(s["pt_sb"], 1)

                for n in range(NU + 1):
                    if n < NU:
                        exps(n)
                    if n > 0:
                        for k, (m, r) in enumerate(halves):
                            if m == n - 1:
                                half(k)
                        if n % (2 * NT) == 0:
                            t = n // (2 * NT) - 1
                            act.wait_ge(s["rb_psum"], NST * b + t + 1)
                            act.activation(rb_sb[:, :], bank(6), ACT.Copy).then_inc(s["rb"], 1)
                            act.wait_ge(s["o_t"], NST * b + t + 1)
                            act.activation(o_hi[:, t, :], o_t[:, t, :], ACT.Copy).then_inc(s["o_hi"], 1)

        @block.vector
        def _(dve):
            dve.wait_ge(s["small_in"], 48)
            dve.wait_ge(s["v_pad"], 1)
            with dve.Fori(0, B) as b:
                for i in range(NT):
                    last = dve.bn_stats(st[:, i, :], x[:, bass.ds(b * NT * D + i * D, D)])
                last.then_inc(s["stats"], 1)
                dve.wait_ge(s["stats"], b + 1)
                hold(dve, 0)
                for i in range(NT):
                    last = dve.bn_aggr(mv[:, i, :], st[:, i, :])
                last.then_inc(s["moments"], 1)
                dve.wait_ge(s["moments"], b + 1)
                dve.tensor_scalar(ve[:, :], mv[:, :, 1], EPS, None, ALU.add).then_inc(s["var_eps"], 1)

                def newton(k, ins):
                    ins.then_inc(s["newton"], 1)
                    dve.wait_ge(s["newton"], 6 * b + k)

                dve.wait_ge(s["rstd0"], b + 1)
                newton(1, dve.scalar_tensor_tensor(n1[:, :], r0[:, :], -0.5, r0[:, :], ALU.mult, ALU.mult))
                newton(2, dve.tensor_tensor(n2[:, :], n1[:, :], ve[:, :], ALU.mult))
                newton(3, dve.scalar_tensor_tensor(rstd[:, :], n2[:, :], 1.5, r0[:, :], ALU.add, ALU.mult))
                newton(4, dve.tensor_tensor(m1[:, :], rstd[:, :], rstd[:, :], ALU.mult))
                newton(5, dve.tensor_tensor(m2[:, :], m1[:, :], mv[:, :, 1], ALU.mult))
                newton(6, dve.tensor_scalar(ms[:, :], m2[:, :], EPS, None, ALU.add))
                for i in range(NT):
                    last = dve.tensor_scalar(xhat[:, i, :], x[:, bass.ds(b * NT * D + i * D, D)], mv[:, i, 0:1],
                                             rstd[:, i:i + 1], ALU.subtract, ALU.mult)
                last.then_inc(s["xhat"], 1)
                dve.wait_ge(s["rms0"], b + 1)
                dve.scalar_tensor_tensor(m1[:, :], m0[:, :], -0.5, m0[:, :], ALU.mult, ALU.mult).then_inc(s["rms_newton"], 1)
                dve.wait_ge(s["rms_newton"], 3 * b + 1)
                dve.tensor_tensor(m2[:, :], m1[:, :], ms[:, :], ALU.mult).then_inc(s["rms_newton"], 1)
                dve.wait_ge(s["rms_newton"], 3 * b + 2)
                dve.scalar_tensor_tensor(rms[:, :], m2[:, :], 1.5, m0[:, :], ALU.add, ALU.mult).then_inc(s["rms_newton"], 1)
                dve.wait_ge(s["rms_newton"], 3 * b + 3)
                dve.wait_ge(s["xhat"], b + 1)
                for i in range(NT):
                    last = dve.tensor_scalar(xr[:, i, :], xhat[:, i, :], rms[:, i:i + 1], None, ALU.mult)
                last.then_inc(s["xr"], 1)
                dve.wait_ge(s["xr"], b + 1)
                wide_bo = rows[:, D:2 * D].unsqueeze(1).broadcast_to([P, NT, D])
                dve.tensor_tensor(xhat[:, :, :], xhat[:, :, :], wide_bo, ALU.add).then_inc(s["residual"], 1)
                dve.wait_ge(s["residual"], 2 * b + 1)
                dve.tensor_tensor(xb(b), xb(b), xhat[:, :, :].rearrange("p i d -> p (i d)"), ALU.add).then_inc(s["residual"], 1)
                dve.wait_ge(s["xT_hi"], b + 1)
                dve.tensor_tensor(xT_lo[:, :, :], xw[:, :, :], xT_hi[:, :, :].bitcast(f32), ALU.subtract).then_inc(s["xT_lo"], 1)
                cos, sin = rope[:, C_COS:C_COS + T], rope[:, C_SIN:C_SIN + T]
                for w, (name, psum_name) in enumerate((("q_rot", "q_psum"), ("k_rot", "k_psum"))):
                    dve.wait_ge(s[psum_name], b + 1)
                    dve.scalar_tensor_tensor(ra[:, w, :], bank(2 + 2 * w), cols[:, 2 * w:2 * w + 1], cos, ALU.add, ALU.mult)
                    dve.scalar_tensor_tensor(rb_[:, w, :], bank(3 + 2 * w), cols[:, 2 * w + 1:2 * w + 2], sin, ALU.add, ALU.mult).then_inc(s["rot"], 1)
                    dve.wait_ge(s["rot"], 2 * b + w + 1)
                    dve.tensor_tensor(rot[:, w, :], ra[:, w, :], rb_[:, w, :], ALU.add).then_inc(s[name], 1)
                for w in range(2):
                    dve.wait_ge(s["rot_hi"], 2 * b + w + 1)
                    dve.tensor_tensor(rot_lo[:, w, :], rot[:, w, :], rot_hi[:, w, :].bitcast(f32), ALU.subtract).then_inc(s["rot_lo"], 1)
                dve.wait_ge(s["v_psum"], b + 1)
                for i in range(NT):
                    last = dve.tensor_tensor(vs[:, i, :, 0:DH1], psum[:, i * D:(i + 1) * D].rearrange("p (h v) -> p h v", h=H1),
                                             rows[:, 0:D].rearrange("p (h v) -> p h v", h=H1), ALU.add)
                last.then_inc(s["v_sb"], 1)

                def maxima(n):
                    t, i, pr = units[n]
                    dve.wait_ge(s["score_psum"], NU * b + n + 1)
                    dve.tensor_reduce(mx[:, n, :], bank(2 + 2 * (n % 2), 2).rearrange("p (e t) -> p e t", e=2)[:, :, 0:(i + 1) * P], AX.X, ALU.max).then_inc(s["max"], 1)
                    dve.wait_ge(s["max"], NU * b + n + 1)
                    dve.tensor_scalar(nb[:, n, :], mx[:, n, :], -0.5, None, ALU.mult).then_inc(s["neg_max"], 1)

                for n in range(NU + 1):
                    if n < NU:
                        maxima(n)
                    if n > 0 and n % (2 * NT) == 0:
                        t = n // (2 * NT) - 1
                        dve.wait_ge(s["p_ready"], NU * b + n)
                        dve.reciprocal(rinv[:, t, :, :], rsum[:, t, :, :]).then_inc(s["recip"], 1)
                        dve.wait_ge(s["recip"], NST * b + t + 1)
                        if t > 0:
                            dve.wait_ge(s["rb_psum"], NST * b + t)
                        dve.tensor_copy(rwide[:, :, :, :], rinv[:, t, :, :].unsqueeze(3).broadcast_to([P, NT, HPT, 32])).then_inc(s["spread_in"], 1)
                        dve.wait_ge(s["rb"], NST * b + t + 1)
                        dve.wait_ge(s["ot_psum"], NU * b + n)
                        dve.tensor_tensor(o_t[:, t, :], bank(t % 2), rb_sb[:, :], ALU.mult).then_inc(s["o_t"], 1)
                        dve.wait_ge(s["o_hi"], NST * b + t + 1)
                        dve.tensor_tensor(o_lo[:, t, :], o_t[:, t, :], o_hi[:, t, :].bitcast(f32), ALU.subtract).then_inc(s["o_lo"], 1)
                dve.wait_ge(s["wo_psum"], b + 1)
                dve.wait_ge(s["residual"], 2 * b + 2)
                dve.tensor_tensor(xb(b), xb(b), bank(2, 2), ALU.add).then_inc(s["x_out"], 1)
                dve.wait_ge(s["x_out"], b + 1)

        @block.tensor
        def _(pe):
            with pe.Fori(0, B) as b:
                pe.wait_ge(s["xr"], b + 1)
                for i in range(NT):
                    for k in range(KC):
                        last = pe.transpose(bank(k)[:, i * P:(i + 1) * P], xr[:, i, k * P:(k + 1) * P], ident)
                last.then_inc(s["xT_psum"], 1)
                pe.wait_ge(s["xT_lo"], b + 1)
                pe.wait_ge(s["w_lo"], 1)

                def project(out, col):
                    for k in range(KC):
                        last = mm3(pe, out, w_hi[:, k, col:col + P], w_lo[:, k, col:col + P], xT_hi[:, k, :], xT_lo[:, k, :], k == 0, k == KC - 1)
                    return last

                project(bank(2), W1QA)
                project(bank(3), W1QB).then_inc(s["q_psum"], 1)
                project(bank(4), W1KA)
                project(bank(5), W1KB).then_inc(s["k_psum"], 1)
                for i in range(NT):
                    for k in range(KC):
                        tt = slice(i * P, (i + 1) * P)
                        last = mm3(pe, psum[:, i * D:(i + 1) * D], xT_hi[:, k, tt], xT_lo[:, k, tt],
                                   w_hi[:, k, W1V:W1V + D], w_lo[:, k, W1V:W1V + D], k == 0, k == KC - 1)
                last.then_inc(s["v_psum"], 1)
                pe.wait_ge(s["sel_r"], 1)
                for k in range(2 * NST):
                    t, w = k // 2, k % 2
                    pe.wait_ge(s["rot_lo"], 2 * b + w + 1)
                    if k >= 2:
                        pe.wait_ge(s["stack_sb"], 2 * NST * b + k - 1)
                    at = (t * 2 + w) * 2 * P
                    pe.matmul(bank(6 + k % 2), sel[:, at:at + P], rot_hi[:, w, :], start=True, stop=False, skip_group_check=True)
                    pe.matmul(bank(6 + k % 2), sel[:, at + P:at + 2 * P], rot_lo[:, w, :], start=False, stop=True, skip_group_check=True).then_inc(s["stack_psum"], 1)

                def scores(n):
                    t, i, pr = units[n]
                    if n % (2 * NT) < 2:
                        pe.wait_ge(s["stack_sb"], 2 * NST * b + 2 * t + 2)
                    if n >= 2:
                        pe.wait_ge(s["p_ready"], NU * b + n - 1)
                    for e in range(2):
                        row = slice(32 * (2 * pr + e), 32 * (2 * pr + e) + 32)
                        pe.matmul(bank(2 + 2 * (n % 2) + e)[:, 0:(i + 1) * P], stack[0][row, t, i * P:(i + 1) * P], stack[1][row, t, 0:(i + 1) * P],
                                  start=True, stop=False, tile_position=(row.start, 0), skip_group_check=True)
                    for e in range(2):
                        last = pe.matmul(bank(2 + 2 * (n % 2) + e)[:, i * P:(i + 1) * P], conb[:, 0:P], conb[:, P:2 * P], start=False, stop=True, skip_group_check=True)
                    last.then_inc(s["score_psum"], 1)

                def turn(n):
                    t, i, pr = units[n]
                    pe.wait_ge(s["p_ready"], NU * b + n + 1)
                    for r in range(1 if i < 2 else 2):
                        k = half_at[n, r]
                        prev = [q for q in range(k) if halves[q][1] == r]
                        if prev:
                            pe.wait_ge(s["pt_sb"], NH * b + prev[-1] + 1)
                        if r == 0 and n % (2 * NT) == 0 and t > 0:
                            pe.wait_ge(s["rb"], NST * b + t)
                        for j in range(2 * r, min(2 * r + 2, i + 1)):
                            for e in range(2):
                                last = pe.transpose(bank(6 + r)[:, ((j - 2 * r) * 2 + e) * P:((j - 2 * r) * 2 + e + 1) * P], prob[n % 2][:, e, j * P:(j + 1) * P], ident)
                        last.then_inc(s["pt_psum"], 1)

                def values(n):
                    t, i, pr = units[n]
                    pe.wait_ge(s["pt_sb"], NH * b + last_half[n] + 1)
                    if n % (2 * NT) == 0 and t >= 2:
                        pe.wait_ge(s["o_t"], NST * b + t - 1)
                    for e in range(2):
                        h = t * HPT + 2 * pr + e
                        q = 32 * (2 * pr + e)
                        for j in range(i + 1):
                            last = pe.matmul(bank(t % 2)[q:q + 32, i * P:(i + 1) * P], vs[:, j, h, :], pt[n % 2][:, j, e, :],
                                             start=(j == 0), stop=(j == i), tile_position=(0, q), skip_group_check=True)
                    last.then_inc(s["ot_psum"], 1)

                scores(0)
                pe.wait_ge(s["v_sb"], b + 1)
                for n in range(NU):
                    if n + 1 < NU:
                        scores(n + 1)
                    turn(n)
                    values(n)
                    if (n + 1) % (2 * NT) == 0:
                        t = n // (2 * NT)
                        pe.wait_ge(s["spread_in"], NST * b + t + 1)
                        for i in range(NT):
                            last = pe.transpose(bank(6)[:, i * P:(i + 1) * P], rwide[:, i, :, :].rearrange("p h v -> p (h v)"), ident)
                        last.then_inc(s["rb_psum"], 1)
                pe.wait_ge(s["o_lo"], NST * b + NST)
                pe.wait_ge(s["wo_lo"], 1)
                for i in range(NT):
                    for k in range(NST):
                        tt = slice(i * P, (i + 1) * P)
                        last = mm3(pe, psum[:, 1024 + i * D:1024 + (i + 1) * D], o_hi[:, k, tt], o_lo[:, k, tt],
                                   wo_hi[:, k, :], wo_lo[:, k, :], k == 0, k == NST - 1)
                last.then_inc(s["wo_psum"], 1)


def build(nc, dram, out):
    ctx = ExitStack()
    with ctx:
        x = ctx.enter_context(nc.sbuf_tensor("x", [P, B * NT * D], f32))
        con = ctx.enter_context(nc.sbuf_tensor("con", [P, C_ODD + 3], f32))
        conb = ctx.enter_context(nc.sbuf_tensor("conb", [P, 2 * P], bf16))
        psum = ctx.enter_context(nc.psum_tensor("psum", [P, 8 * 512], f32))
        ident = con[:, C_ID:C_ID + P]
        kept = []
        linear_attention(nc, kept, x, psum, con, conb, ident, dram)
        experts(nc, kept, "e0", x, psum, con, conb, dram, "f0", CH0, GROUP0, "r0", E0, "sel0", golden_route)
        nc.clear_and_free_semaphores(kept)
        nc.all_engine_barrier()
        kept = []
        rotary_attention(nc, kept, x, psum, con, conb, dram)
        experts(nc, kept, "e1", x, psum, con, conb, dram, "f1", CH1, GROUP1, "r1", E1, "sel1", top_route)
        stored = ctx.enter_context(nc.semaphore("stored"))
        with nc.Block() as block:
            @block.sync
            def _(sp):
                for b in range(B):
                    sp.dma_start(out[b].rearrange("(i p) d -> p i d", p=P),
                                 x[:, b * NT * D:(b + 1) * NT * D].rearrange("p (i d) -> p i d", i=NT)).then_inc(stored, 16)
                sp.wait_ge(stored, 16 * B)


def host_constants():
    p = np.arange(P)
    con = np.zeros((P, C_ODD + 3), np.float32)
    con[:, C_ID:C_ID + P] = np.eye(P)
    con[:, C_TRI:C_TRI + P] = p[:, None] <= p[None, :]
    con[:, C_AVG:C_AVG + P] = (p[:, None] // DV0 == p[None, :] // DV0) / DV0
    con[:, C_DIAG:C_DIAG + D] = p[:, None] // DK0 == np.arange(D)[None, :] // DV0
    con[:, C_RST:C_RST + T] = np.arange(T)[None, :] % P != 0
    con[:, C_EVEN] = ((p // DK0) % 2 == 0) * np.float32(DV0 ** -0.5)
    con[:, C_ODD] = ((p // DK0) % 2 == 1) * np.float32(DV0 ** -0.5)
    con[:, C_ODD + 1] = EPS
    rope = np.zeros((P, C_SEL + 16 * P), np.float32)
    i = p % HALF
    freq = (np.float32(10000.0) ** (i.astype(np.float32) * np.float32(-2.0 / DH1))).astype(np.float32)
    ang = (np.arange(T, dtype=np.float32)[None, :] * freq[:, None]).astype(np.float32)
    cos, sin = np.cos(ang), np.sin(ang)
    even = (i % 2 == 0)[:, None]
    rope[:, C_COS:C_COS + T] = np.where(even, cos, sin)
    rope[:, C_SIN:C_SIN + T] = np.where(even, -sin, cos)
    for t in range(NST):
        for which, parts in enumerate(((0, 0, 1, 1), (0, 1, 0, 1))):
            for part in range(2):
                m = np.zeros((P, P), np.float32)
                for hh in range(HPT):
                    for c in range(4):
                        if parts[c] == part:
                            for e in range(HALF):
                                m[HALF * (HPT * t + hh) + e, 32 * hh + 8 * c + e] = 1.0
                at = C_SEL + ((t * 2 + which) * 2 + part) * P
                rope[:, at:at + P] = m
    conb = np.zeros((P, 2 * P), np.float32)
    conb[:, 0:P] = np.eye(P)
    conb[:, P:2 * P] = np.where(p[None, :] > p[:, None], -BIG, 0.0)
    sel0 = np.zeros((WR, CH0, P), np.float32)
    sel1 = np.zeros((WR, CH1, P), np.float32)
    for sel, nch, e_n, f in ((sel0, CH0, E0, F0), (sel1, CH1, E1, F1)):
        for c in range(nch):
            for j in range(P):
                e = (c * P + j) // f
                if e < e_n:
                    for part in range(3):
                        sel[part * e_n + e, c, j] = 1.0
                elif e_n == E1 and c * P + j < E1 * F1 + SH1:
                    sel[3 * E1, c, j] = 1.0
    tie = np.zeros((P, E0 * E0 + E1 * E1 + G1 * G1), np.float32)
    at = 0
    for n in (E0, E1, G1):
        e = np.arange(n)
        tie[:, at:at + n * n] = (e[None, :] < e[:, None]).astype(np.float32).reshape(1, -1)
        at += n * n
    half = lambda c: (c.view(np.uint32) >> 16).astype(np.uint16)
    return {"con": con, "rope": rope, "conb": half(conb), "sel0": half(sel0), "sel1": half(sel1), "tie": tie}


def kernel(**inputs):
    import concourse.bacc as _bacc
    from concourse.bass_utils import run_bass_kernel_spmd as _run

    a = {k: np.asarray(v) for k, v in inputs.items()}
    by_rows = lambda w: np.ascontiguousarray(w.reshape(-1, P, w.shape[-1]).transpose(1, 0, 2))
    pad = lambda w, r, c: np.concatenate([np.concatenate([w, np.zeros((w.shape[0], c - w.shape[1]), w.dtype)], 1),
                                          np.zeros((r - w.shape[0], c), w.dtype)], 0)
    host = dict(host_constants())
    host["x"] = a["L0_attn_x"]
    host["w0"] = by_rows(np.concatenate([a["L0_attn_Wq"], a["L0_attn_Wk"], a["L0_attn_Wg"], pad(a["L0_attn_Wkg1"], D, P), a["L0_attn_Wv"]], 1))
    host["wr0"] = pad(a["L0_attn_Wkg2"], P, P)
    host["cols0"] = np.stack([a["L0_attn_bkg2"], a["L0_attn_bg"][:P], a["L0_attn_bg"][P:]], 1)
    host["wo0"] = by_rows(a["L0_attn_Wo"])

    def experts(gate, up, down, chunks):
        g = gate.reshape(KC, P, chunks, P).transpose(2, 1, 0, 3).reshape(chunks, P, KC * P)
        u = up.reshape(KC, P, chunks, P).transpose(2, 1, 0, 3).reshape(chunks, P, KC * P)
        return np.ascontiguousarray(np.concatenate([g, u, down.reshape(chunks, P, D)], 2))

    side = lambda w: w.transpose(1, 0, 2).reshape(D, -1)
    host["f0"] = experts(side(a["L0_ffn_Wg"]), side(a["L0_ffn_Wu"]), a["L0_ffn_Wd"].reshape(-1, D), CH0)
    n1 = CH1 * P
    host["f1"] = experts(pad(np.concatenate([side(a["L1_ffn_w1"]), a["L1_ffn_sw1"]], 1), D, n1),
                         pad(np.concatenate([side(a["L1_ffn_w3"]), a["L1_ffn_sw3"]], 1), D, n1),
                         pad(np.concatenate([a["L1_ffn_w2"].reshape(-1, D), a["L1_ffn_sw2"]], 0), n1, D), CH1)
    host["r0"] = by_rows(a["L0_ffn_Wr"])
    host["temp"] = a["L0_ffn_temperature"].reshape(1, 1)
    host["r1"] = by_rows(np.ascontiguousarray(a["L1_ffn_gate_w"].T))
    host["ebias"] = a["L1_ffn_expert_bias"].reshape(1, E1)
    even, odd = lambda w: w[..., 0::2], lambda w: w[..., 1::2]
    q, k = a["L1_attn_wq"], a["L1_attn_wk"]
    host["w1"] = by_rows(np.concatenate([even(q), odd(q), even(k), odd(k), a["L1_attn_wv"]], 1))
    bq, bk, rw = a["L1_attn_bq"], a["L1_attn_bk"], a["L1_attn_rms_w"]
    host["cols1"] = np.stack([even(bq), odd(bq), even(bk), odd(bk), rw[:P], rw[P:]], 1)
    host["rows1"] = np.stack([a["L1_attn_bv"], a["L1_attn_bo"]], 0).reshape(1, 2 * D)
    wo = a["L1_attn_wo"].reshape(NST, HPT, DH1, D)
    host["wo1"] = np.ascontiguousarray(np.concatenate([wo, np.zeros_like(wo)], 2).reshape(NST, P, D).transpose(1, 0, 2))

    nc = _bacc.Bacc("TRN2", target_bir_lowering=False, num_devices=1)
    arrays, dram = {}, {}
    for name, v in host.items():
        v = np.ascontiguousarray(v)
        arrays[f"in_{name}"] = v
        dram[name] = nc.dram_tensor(f"in_{name}", v.shape, mybir.dt.from_np(v.dtype), kind="ExternalInput").ap()
    out = nc.dram_tensor("out", (B, T, D), f32, kind="ExternalOutput").ap()
    build(nc, dram, out)
    r = _run(nc, [arrays], core_ids=[0])
    return r.results[0]["out"]
```

```python
import numpy as np
import concourse.bass as bass
from concourse import mybir
from contextlib import ExitStack

f32 = mybir.dt.float32
f32r = mybir.dt.float32r
bf16 = mybir.dt.bfloat16
u32 = mybir.dt.uint32
ALU = mybir.AluOpType
ACT = mybir.ActivationFunctionType
AX = mybir.AxisListType

P = 128
B, T, D = 4, 512, 256
KC = D // P
NT = T // P
EPS = 1e-5
LN_EXP_SET = "natural_log_exp_and_others"
H0, DK0, DV0 = 8, 16, 32
GATE_NORM = 16.0
H1, DH1 = 16, 16
HALF = DH1 // 2
HPT = P // 32
NST = H1 // HPT
E0, F0 = 8, 256
E1, F1, SH1 = 16, 176, 352
CH0 = E0 * F0 // P
CH1 = -(-(E1 * F1 + SH1) // P)
TOP0, TOP1, G1, TOPG1 = 2, 4, 4, 2
GROUP0, GROUP1 = 4, 5
WR = 128
CENTER = float(1.0 / np.e)
LOWER = float(np.float32(0.5 - np.log(4.0 / 3.0)))
UPPER = 0.5
BIG = 3.0e38

W0Q, W0K, W0G, W0R, W0V, W0N = 0, 128, 256, 512, 640, 896
W1QA, W1QB, W1KA, W1KB, W1V, W1N = 0, 128, 256, 384, 512, 768
C_ID, C_TRI, C_AVG, C_DIAG, C_RST, C_EVEN, C_ODD = 0, 128, 256, 384, 640, 1152, 1153
C_COS, C_SIN, C_SUM, C_HEAD, C_SEL = 0, 512, 1024, 1152, 1156


def mm3(pe, out, w_hi, w_lo, x_hi, x_lo, first, last):
    pe.matmul(out, w_hi, x_hi, start=first, stop=False, skip_group_check=True)
    pe.matmul(out, w_hi, x_lo, start=False, stop=False, skip_group_check=True)
    return pe.matmul(out, w_lo, x_hi, start=False, stop=last, skip_group_check=True)


def sems(nc, kept, prefix, names):
    named = {n: nc.alloc_semaphore(name=f"{prefix}_{n}") for n in names.split()}
    kept.extend(named.values())
    return named


def linear_attention(nc, kept, x, psum, con, conb, ident, dram):
    ctx = ExitStack()
    with ctx:
        def sb(name, shape, dt=f32):
            return ctx.enter_context(nc.sbuf_tensor(f"a0_{name}", shape, dt))

        s = sems(nc, kept, "a0", "x_in con_in w_in wo_in wr_in w_hi w_lo wo_hi wo_lo wr_hi wr_lo zeroed "
                 "stats moments var_eps ln_var rstd0 newton xhat xT_psum xT_hi xT_lo kg1_psum kg1_hi kg1_lo "
                 "q_psum k_psum kg2_psum v_psum g_psum gate_abs gate_min gate_exp gate_ln gate_log gate_cum "
                 "gate_last decay_q decay_k decay_end qd kn kdT kd_psum kd v_sb silu_g at_psum at_sb kv_psum "
                 "kv_sb state ot_psum o_sb mean_psum centered sq var_psum o_ln o_rstd c_gated y y_hi y_lo "
                 "wo_psum x_out")
        w_raw, w_hi, w_lo = sb("w_raw", [P, KC, W0N]), sb("w_hi", [P, KC, W0N], f32r), sb("w_lo", [P, KC, W0N], f32r)
        wo_raw, wo_hi, wo_lo = sb("wo_raw", [P, KC, D]), sb("wo_hi", [P, KC, D], f32r), sb("wo_lo", [P, KC, D], f32r)
        wr_raw, wr_hi, wr_lo = sb("wr_raw", [P, P]), sb("wr_hi", [P, P], f32r), sb("wr_lo", [P, P], f32r)
        cols = sb("cols", [P, 3])
        st, mv = sb("st", [P, NT, 6]), sb("mv", [P, NT, 2])
        ve, lnv, r0, n1, n2, rstd = (sb(n, [P, NT]) for n in ("ve", "lnv", "r0", "n1", "n2", "rstd"))
        held = sb("held", [P, 4])
        xhat = sb("xhat", [P, NT, D])
        xT_hi, xT_lo = sb("xT_hi", [P, KC, T], f32r), sb("xT_lo", [P, KC, T], f32r)
        kg1_hi, kg1_lo = sb("kg1_hi", [P, T], f32r), sb("kg1_lo", [P, T], f32r)
        g_abs, g_min, g_exp, g_ln, g_log, g_cum = (sb(n, [P, T]) for n in ("g_abs", "g_min", "g_exp", "g_ln", "g_log", "g_cum"))
        g_last = sb("g_last", [P, NT])
        dq, dk, de = sb("dq", [P, T]), sb("dk", [P, T]), sb("de", [P, T])
        qd, kne, kno, kdT = (sb(n, [P, T]) for n in ("qd", "kne", "kno", "kdT"))
        kd = sb("kd", [P, NT, P])
        v_sb = sb("v_sb", [P, NT, D])
        sg = sb("sg", [P, KC, T])
        at = [sb(f"at{i}", [P, 16, P]) for i in range(2)]
        kv = [sb(f"kv{i}", [P, D]) for i in range(3)]
        stt = [kv[0], sb("state2", [P, D]), sb("state3", [P, D])]
        o_sb, cen, sq, lv, rs, y = (sb(n, [P, KC, T]) for n in ("o_sb", "cen", "sq", "lv", "rs", "y"))
        y_hi, y_lo = sb("y_hi", [P, KC, T], f32r), sb("y_lo", [P, KC, T], f32r)
        tri = con[:, C_TRI:C_TRI + P]
        avg = con[:, C_AVG:C_AVG + P]
        diag = con[:, C_DIAG:C_DIAG + D]
        rst = con[:, C_RST:C_RST + T]
        eps_col = con[:, C_ODD + 1:C_ODD + 2]
        bank = lambda i, n=1: psum[:, 512 * i:512 * (i + n)]
        xb = lambda b: x[:, bass.ds(b * NT * D, NT * D)]

        def hold(dve, place):
            dve.tensor_copy(held[:, place:place + 1], con[:, 0:1])

        block = ctx.enter_context(nc.Block())

        @block.sync
        def _(sp):
            sp.dma_start(con[:, :], dram["con"]).then_inc(s["con_in"], 16)
            sp.dma_start(conb[:, :], dram["conb"].bitcast(bf16)).then_inc(s["con_in"], 16)
            for b in range(B):
                sp.dma_start(x[:, b * NT * D:(b + 1) * NT * D].rearrange("p (i d) -> p i d", i=NT),
                             dram["x"][b].rearrange("(i p) d -> p i d", p=P)).then_inc(s["x_in"], 16)
            sp.dma_start(w_raw[:, :, :], dram["w0"]).then_inc(s["w_in"], 16)
            sp.dma_start(wr_raw[:, :], dram["wr0"]).then_inc(s["wr_in"], 16)
            sp.dma_start(cols[:, :], dram["cols0"]).then_inc(s["wr_in"], 16)
            sp.dma_start(wo_raw[:, :, :], dram["wo0"]).then_inc(s["wo_in"], 16)

        @block.gpsimd
        def _(pool):
            for t in (at[0][:, :, :], at[1][:, :, :], kv[0][:, :], kv[1][:, :], kv[2][:, :]):
                pool.memset(t, 0.0).then_inc(s["zeroed"], 1)
            for raw, hi, lo, came, n, s_hi, s_lo in ((w_raw, w_hi, w_lo, "w_in", 16, "w_hi", "w_lo"),
                                                     (wr_raw, wr_hi, wr_lo, "wr_in", 32, "wr_hi", "wr_lo"),
                                                     (wo_raw, wo_hi, wo_lo, "wo_in", 16, "wo_hi", "wo_lo")):
                pool.wait_ge(s[came], n)
                pool.tensor_copy(hi[:], raw[:]).then_inc(s[s_hi], 1)
                pool.wait_ge(s[s_hi], 1)
                pool.tensor_tensor(lo[:], raw[:], hi[:].bitcast(f32), ALU.subtract).then_inc(s[s_lo], 1)

        @block.scalar
        def _(act):
            act.wait_ge(s["wr_in"], 32)
            with act.Fori(0, B) as b:
                act.preload_act_table_set(LN_EXP_SET)
                act.wait_ge(s["var_eps"], b + 1)
                act.activation(lnv[:, :], ve[:, :], ACT.Ln).then_inc(s["ln_var"], 1)
                act.wait_ge(s["ln_var"], b + 1)
                act.activation(r0[:, :], lnv[:, :], ACT.Exp, scale=-0.5).then_inc(s["rstd0"], 1)
                act.wait_ge(s["xT_psum"], b + 1)
                act.activation(xT_hi[:, :, :], bank(0, 2).rearrange("p (k t) -> p k t", k=KC), ACT.Copy).then_inc(s["xT_hi"], 1)
                act.wait_ge(s["kg1_psum"], b + 1)
                act.activation(kg1_hi[:, :], bank(6), ACT.Copy).then_inc(s["kg1_hi"], 1)
                act.wait_ge(s["gate_min"], b + 1)
                act.activation(g_abs[:, :], bank(7), ACT.Abs, bias=cols[:, 0:1]).then_inc(s["gate_abs"], 1)
                act.wait_ge(s["gate_abs"], b + 1)
                act.activation(g_exp[:, :], g_abs[:, :], ACT.Exp, scale=-1.0).then_inc(s["gate_exp"], 1)
                act.wait_ge(s["gate_exp"], b + 1)
                act.activation(g_ln[:, :], g_exp[:, :], ACT.Ln, bias=1.0).then_inc(s["gate_ln"], 1)
                act.wait_ge(s["gate_cum"], b + 1)
                act.activation(dq[:, :], g_cum[:, :], ACT.Exp, scale=1.0 / GATE_NORM).then_inc(s["decay_q"], 1)
                act.activation(dk[:, :], g_cum[:, :], ACT.Exp, scale=-1.0 / GATE_NORM).then_inc(s["decay_k"], 1)
                act.wait_ge(s["gate_last"], b + 1)
                for n in range(NT):
                    last = act.activation(de[:, n * P:(n + 1) * P], g_cum[:, n * P:(n + 1) * P], ACT.Exp,
                                          bias=g_last[:, n:n + 1], scale=-1.0 / GATE_NORM)
                last.then_inc(s["decay_end"], 1)
                act.wait_ge(s["v_psum"], b + 1)
                act.activation(v_sb[:, :, :], bank(0, 2).rearrange("p (i d) -> p i d", i=NT), ACT.Copy).then_inc(s["v_sb"], 1)
                act.wait_ge(s["kd_psum"], b + 1)
                act.activation(kd[:, :, :], bank(6).rearrange("p (i d) -> p i d", i=NT), ACT.Copy).then_inc(s["kd"], 1)
                act.wait_ge(s["g_psum"], b + 1)
                for h in range(KC):
                    last = act.activation(sg[:, h, :], bank(4 + h), ACT.Silu, bias=cols[:, 1 + h:2 + h])
                last.then_inc(s["silu_g"], 1)
                act.preload_act_table_set(LN_EXP_SET)
                act.wait_ge(s["ot_psum"], b + 1)
                act.activation(o_sb[:, :, :], bank(0, 2).rearrange("p (k t) -> p k t", k=KC), ACT.Copy).then_inc(s["o_sb"], 1)
                act.wait_ge(s["centered"], b + 1)
                act.activation(sq[:, :, :], cen[:, :, :], ACT.Square).then_inc(s["sq"], 1)
                act.wait_ge(s["var_psum"], b + 1)
                act.activation(lv[:, :, :], bank(4, 2).rearrange("p (k t) -> p k t", k=KC), ACT.Ln, bias=eps_col).then_inc(s["o_ln"], 1)
                act.wait_ge(s["o_ln"], b + 1)
                act.activation(rs[:, :, :], lv[:, :, :], ACT.Exp, scale=-0.5).then_inc(s["o_rstd"], 1)
                act.wait_ge(s["y"], b + 1)
                act.activation(y_hi[:, :, :], y[:, :, :], ACT.Copy).then_inc(s["y_hi"], 1)

        @block.vector
        def _(dve):
            dve.wait_ge(s["con_in"], 32)
            dve.wait_ge(s["x_in"], 16 * B)
            dve.wait_ge(s["zeroed"], 5)
            dve.wait_ge(s["wr_in"], 32)
            with dve.Fori(0, B) as b:
                for i in range(NT):
                    last = dve.bn_stats(st[:, i, :], x[:, bass.ds(b * NT * D + i * D, D)])
                last.then_inc(s["stats"], 1)
                dve.wait_ge(s["stats"], b + 1)
                hold(dve, 0)
                for i in range(NT):
                    last = dve.bn_aggr(mv[:, i, :], st[:, i, :])
                last.then_inc(s["moments"], 1)
                dve.wait_ge(s["moments"], b + 1)
                dve.tensor_scalar(ve[:, :], mv[:, :, 1], EPS, None, ALU.add).then_inc(s["var_eps"], 1)
                dve.wait_ge(s["rstd0"], b + 1)
                dve.scalar_tensor_tensor(n1[:, :], r0[:, :], -0.5, r0[:, :], ALU.mult, ALU.mult).then_inc(s["newton"], 1)
                dve.wait_ge(s["newton"], 3 * b + 1)
                dve.tensor_tensor(n2[:, :], n1[:, :], ve[:, :], ALU.mult).then_inc(s["newton"], 1)
                dve.wait_ge(s["newton"], 3 * b + 2)
                dve.scalar_tensor_tensor(rstd[:, :], n2[:, :], 1.5, r0[:, :], ALU.add, ALU.mult).then_inc(s["newton"], 1)
                dve.wait_ge(s["newton"], 3 * b + 3)
                for i in range(NT):
                    last = dve.tensor_scalar(xhat[:, i, :], x[:, bass.ds(b * NT * D + i * D, D)], mv[:, i, 0:1],
                                             rstd[:, i:i + 1], ALU.subtract, ALU.mult)
                last.then_inc(s["xhat"], 1)
                dve.wait_ge(s["xT_hi"], b + 1)
                dve.tensor_tensor(xT_lo[:, :, :], bank(0, 2).rearrange("p (k t) -> p k t", k=KC),
                                  xT_hi[:, :, :].bitcast(f32), ALU.subtract).then_inc(s["xT_lo"], 1)
                dve.wait_ge(s["kg1_hi"], b + 1)
                dve.tensor_tensor(kg1_lo[:, :], bank(6), kg1_hi[:, :].bitcast(f32), ALU.subtract).then_inc(s["kg1_lo"], 1)
                dve.wait_ge(s["kg2_psum"], b + 1)
                dve.tensor_scalar(g_min[:, :], bank(7), cols[:, 0:1], 0.0, ALU.add, ALU.min).then_inc(s["gate_min"], 1)
                dve.wait_ge(s["gate_ln"], b + 1)
                dve.wait_ge(s["gate_min"], b + 1)
                dve.tensor_tensor(g_log[:, :], g_min[:, :], g_ln[:, :], ALU.subtract).then_inc(s["gate_log"], 1)
                dve.wait_ge(s["gate_log"], b + 1)
                dve.tensor_tensor_scan(g_cum[:, :], rst, g_log[:, :], 0.0, ALU.mult, ALU.add).then_inc(s["gate_cum"], 1)
                dve.wait_ge(s["gate_cum"], b + 1)
                dve.tensor_scalar(g_last[:, :], g_cum[:, P - 1::P], 1.0 / GATE_NORM, None, ALU.mult).then_inc(s["gate_last"], 1)
                dve.wait_ge(s["decay_q"], b + 1)
                dve.wait_ge(s["q_psum"], b + 1)
                dve.tensor_tensor(qd[:, :], bank(2), dq[:, :], ALU.mult).then_inc(s["qd"], 1)
                dve.wait_ge(s["decay_k"], b + 1)
                dve.wait_ge(s["k_psum"], b + 1)
                dve.scalar_tensor_tensor(kne[:, :], bank(3), con[:, C_EVEN:C_EVEN + 1], dk[:, :], ALU.mult, ALU.mult).then_inc(s["kn"], 1)
                dve.scalar_tensor_tensor(kno[:, :], bank(3), con[:, C_ODD:C_ODD + 1], dk[:, :], ALU.mult, ALU.mult).then_inc(s["kn"], 1)
                dve.wait_ge(s["decay_end"], b + 1)
                dve.scalar_tensor_tensor(kdT[:, :], bank(3), float(DV0) ** -0.5, de[:, :], ALU.mult, ALU.mult).then_inc(s["kdT"], 1)

                def masked(r):
                    dve.wait_ge(s["at_psum"], 2 * b + r + 1)
                    hold(dve, 1 + r)
                    dve.copy_predicated(at[r][:, :, :], tri.unsqueeze(1).broadcast_to([P, 16, P]).bitcast(u32),
                                        bank(2, 4).rearrange("p (a t) -> p a t", t=P)).then_inc(s["at_sb"], 1)

                masked(0)
                dve.wait_ge(s["kv_psum"], b + 1)
                hold(dve, 3)
                for n in range(3):
                    last = dve.copy_predicated(kv[n][:, :], diag.bitcast(u32), (bank(7)[:, n * D:(n + 1) * D] if n < 2 else bank(6)[:, 0:D]))
                    last.then_inc(s["kv_sb"], 1)
                dve.wait_ge(s["kv_sb"], 3 * b + 3)
                dve.scalar_tensor_tensor(stt[1][:, :], stt[0][:, :], dq[:, 2 * P - 1:2 * P], kv[1][:, :], ALU.mult, ALU.add).then_inc(s["state"], 1)
                dve.wait_ge(s["state"], 2 * b + 1)
                dve.scalar_tensor_tensor(stt[2][:, :], stt[1][:, :], dq[:, 3 * P - 1:3 * P], kv[2][:, :], ALU.mult, ALU.add).then_inc(s["state"], 1)
                masked(1)
                dve.wait_ge(s["mean_psum"], b + 1)
                dve.tensor_tensor(cen[:, :, :], o_sb[:, :, :], bank(2, 2).rearrange("p (k t) -> p k t", k=KC), ALU.subtract).then_inc(s["centered"], 1)
                dve.wait_ge(s["centered"], b + 1)
                dve.wait_ge(s["silu_g"], b + 1)
                dve.tensor_tensor(sg[:, :, :], cen[:, :, :], sg[:, :, :], ALU.mult).then_inc(s["c_gated"], 1)
                dve.wait_ge(s["c_gated"], b + 1)
                dve.wait_ge(s["o_rstd"], b + 1)
                dve.tensor_tensor(y[:, :, :], sg[:, :, :], rs[:, :, :], ALU.mult).then_inc(s["y"], 1)
                dve.wait_ge(s["y_hi"], b + 1)
                dve.tensor_tensor(y_lo[:, :, :], y[:, :, :], y_hi[:, :, :].bitcast(f32), ALU.subtract).then_inc(s["y_lo"], 1)
                dve.wait_ge(s["wo_psum"], b + 1)
                dve.tensor_tensor(xb(b), xb(b), bank(6, 2), ALU.add).then_inc(s["x_out"], 1)
                dve.wait_ge(s["x_out"], b + 1)

        @block.tensor
        def _(pe):
            pe.wait_ge(s["con_in"], 32)
            with pe.Fori(0, B) as b:
                pe.wait_ge(s["xhat"], b + 1)
                for i in range(NT):
                    for k in range(KC):
                        last = pe.transpose(bank(k)[:, i * P:(i + 1) * P], xhat[:, i, k * P:(k + 1) * P], ident)
                last.then_inc(s["xT_psum"], 1)
                pe.wait_ge(s["xT_lo"], b + 1)
                pe.wait_ge(s["w_lo"], 1)

                def project(out, col):
                    for k in range(KC):
                        last = mm3(pe, out, w_hi[:, k, col:col + P], w_lo[:, k, col:col + P], xT_hi[:, k, :], xT_lo[:, k, :], k == 0, k == KC - 1)
                    return last

                project(bank(6), W0R).then_inc(s["kg1_psum"], 1)
                project(bank(2), W0Q).then_inc(s["q_psum"], 1)
                project(bank(3), W0K).then_inc(s["k_psum"], 1)
                pe.wait_ge(s["kg1_lo"], b + 1)
                pe.wait_ge(s["wr_lo"], 1)
                mm3(pe, bank(7), wr_hi[:, :], wr_lo[:, :], kg1_hi[:, :], kg1_lo[:, :], True, True).then_inc(s["kg2_psum"], 1)
                for i in range(NT):
                    for k in range(KC):
                        tt = slice(i * P, (i + 1) * P)
                        last = mm3(pe, bank(i // 2)[:, (i % 2) * D:(i % 2 + 1) * D], xT_hi[:, k, tt], xT_lo[:, k, tt],
                                   w_hi[:, k, W0V:W0V + D], w_lo[:, k, W0V:W0V + D], k == 0, k == KC - 1)
                last.then_inc(s["v_psum"], 1)
                project(bank(4), W0G)
                project(bank(5), W0G + P).then_inc(s["g_psum"], 1)
                pe.wait_ge(s["kdT"], b + 1)
                for n in range(NT):
                    last = pe.transpose(bank(6)[:, n * P:(n + 1) * P], kdT[:, n * P:(n + 1) * P], ident)
                last.then_inc(s["kd_psum"], 1)
                pe.wait_ge(s["kn"], 2 * b + 2)
                pe.wait_ge(s["qd"], b + 1)
                pe.wait_ge(s["silu_g"], b + 1)

                def scores(r):
                    for n in (2 * r, 2 * r + 1):
                        for par in range(2):
                            for pr in range(4):
                                row = slice(32 * pr, 32 * pr + 32)
                                col = ((n % 2) * 2 + par) * P
                                last = pe.matmul(bank(2 + pr)[:, col:col + P], (kne, kno)[par][row, n * P:(n + 1) * P],
                                                 qd[row, n * P:(n + 1) * P], start=True, stop=True, tile_position=(32 * pr, 0),
                                                 skip_group_check=True)
                    last.then_inc(s["at_psum"], 1)

                scores(0)
                pe.wait_ge(s["kd"], b + 1)
                pe.wait_ge(s["v_sb"], b + 1)
                for n in range(3):
                    last = pe.matmul(bank(7)[:, n * D:(n + 1) * D] if n < 2 else bank(6)[:, 0:D], kd[:, n, :], v_sb[:, n, :],
                                     start=True, stop=True, skip_group_check=True)
                last.then_inc(s["kv_psum"], 1)
                for n in range(NT):
                    if n == 0:
                        pe.wait_ge(s["at_sb"], 2 * b + 1)
                        scores(1)
                    if n == 2:
                        pe.wait_ge(s["at_sb"], 2 * b + 2)
                    if n > 0:
                        if n == 1:
                            pe.wait_ge(s["kv_sb"], 3 * b + 3)
                        else:
                            pe.wait_ge(s["state"], 2 * b + n - 1)
                        for h in range(KC):
                            pe.matmul(bank(h)[:, n * P:(n + 1) * P], stt[n - 1][:, h * P:(h + 1) * P], qd[:, n * P:(n + 1) * P],
                                      start=True, stop=False, skip_group_check=True)
                    for h in range(H0):
                        q = 32 * (h % 4)
                        last = pe.matmul(bank(h // 4)[q:q + 32, n * P:(n + 1) * P], v_sb[:, n, h * DV0:(h + 1) * DV0],
                                         at[n // 2][:, (h // 2) * 4 + (n % 2) * 2 + h % 2, :], start=(n == 0), stop=True,
                                         tile_position=(0, q), skip_group_check=True)
                last.then_inc(s["ot_psum"], 1)
                pe.wait_ge(s["o_sb"], b + 1)
                for h in range(KC):
                    last = pe.matmul(bank(2 + h), avg, o_sb[:, h, :], start=True, stop=True)
                last.then_inc(s["mean_psum"], 1)
                pe.wait_ge(s["sq"], b + 1)
                for h in range(KC):
                    last = pe.matmul(bank(4 + h), avg, sq[:, h, :], start=True, stop=True)
                last.then_inc(s["var_psum"], 1)
                pe.wait_ge(s["y_lo"], b + 1)
                pe.wait_ge(s["wo_lo"], 1)
                for i in range(NT):
                    for k in range(KC):
                        tt = slice(i * P, (i + 1) * P)
                        last = mm3(pe, bank(6 + i // 2)[:, (i % 2) * D:(i % 2 + 1) * D], y_hi[:, k, tt], y_lo[:, k, tt],
                                   wo_hi[:, k, :], wo_lo[:, k, :], k == 0, k == KC - 1)
                last.then_inc(s["wo_psum"], 1)


class Chain:

    def __init__(self, engine, sem):
        self.engine, self.sem, self.n = engine, sem, 0

    def __call__(self, ins):
        self.n += 1
        ins.then_inc(self.sem, 1)
        self.engine.wait_ge(self.sem, self.n)


def experts(nc, kept, tag, x, psum, con, conb, dram, weights, chunks, group, router, n_exp, sel_name, route_weights):
    groups = chunks // group
    per_group = B * group
    n = B * NT
    ctx = ExitStack()
    with ctx:
        def sb(name, shape, dt=f32):
            return ctx.enter_context(nc.sbuf_tensor(f"{tag}_{name}", shape, dt))

        s = sems(nc, kept, tag, "small_in stats moments var_eps chain ln_var rstd0 xhat xT_psum xT_hi xT_lo r_hi r_lo logits "
                 "z inh dist w0 fb wx wT_psum wT split_hi split_lo gate_psum up_psum silu gated scaled h_hi h_lo down y_added")
        raw_in = list(sems(nc, kept, tag, " ".join(f"raw_in{c}" for c in range(group))).values())
        WN = 2 * KC * P + D
        raw, w_hi, w_lo = sb("raw", [P, group, WN]), sb("w_hi", [P, group, WN], f32r), sb("w_lo", [P, group, WN], f32r)
        sel = sb("sel", [WR, chunks * P], bf16)
        r_raw, r_hi, r_lo = sb("r_raw", [P, KC, n_exp]), sb("r_hi", [P, KC, n_exp], f32r), sb("r_lo", [P, KC, n_exp], f32r)
        st, mv = sb("st", [P, n, 6]), sb("mv", [P, n, 2])
        ve, lnv, r0, n1, n2, rstd = (sb(k, [P, n]) for k in ("ve", "lnv", "r0", "n1", "n2", "rstd"))
        xT_hi, xT_lo = sb("xT_hi", [P, KC, B * T], f32r), sb("xT_lo", [P, KC, B * T], f32r)
        wx, wT = sb("wx", [P, NT, WR], bf16), sb("wT", [WR, B * T], bf16)
        sil, gat, h = ([sb(f"{k}{i}", [P, T]) for i in range(2)] for k in ("sil", "gat", "h"))
        h_hi, h_lo = ([sb(f"{k}{i}", [P, T], f32r) for i in range(2)] for k in ("h_hi", "h_lo"))
        side = sb("side", [P, E1 + E0 * E0 + E1 * E1 + G1 * G1])
        bank = lambda i, m=1: psum[:, 512 * i:512 * (i + m)]
        ident = con[:, C_ID:C_ID + P]
        zero = con[:, C_ODD + 2:C_ODD + 3]
        xhat = [sb(f"xhat{i}", [P, NT, D]) for i in range(2)]
        logits_read = "z" if n_exp == E0 else "inh"
        front_bank = lambda f, k: bank(7 if f else 6 + k)
        routing = route_weights(sb, s)
        block = ctx.enter_context(nc.Block())

        @block.sync
        def _(sp):
            sp.dma_start(r_raw[:, :, :], dram[router]).then_inc(s["small_in"], 16)
            if n_exp == E0:
                sp.dma_start(side[:, 0:1], dram["temp"].broadcast_to([P, 1])).then_inc(s["small_in"], 16)
            else:
                sp.dma_start(side[:, 0:E1], dram["ebias"].broadcast_to([P, E1])).then_inc(s["small_in"], 16)
            sp.dma_start(side[:, E1:], dram["tie"]).then_inc(s["small_in"], 16)
            sp.dma_start(sel[:, :], dram[sel_name].rearrange("r c p -> r (c p)").bitcast(bf16)).then_inc(s["small_in"], 16)

            for c in range(group):
                sp.dma_start(raw[:, c, :], dram[weights][c]).then_inc(raw_in[c], 16)
            with sp.Fori(1, groups) as g:
                for c in range(group):
                    sp.wait_ge(s["split_lo"], (g - 1) * group + c + 1)
                    sp.dma_start(raw[:, c, :], dram[weights][bass.ds(g * group + c, 1), :, :].rearrange("a p n -> (a p) n")).then_inc(raw_in[c], 16)

        @block.gpsimd
        def _(pool):
            pool.wait_ge(s["small_in"], 64)
            pool.tensor_copy(r_hi[:, :, :], r_raw[:, :, :]).then_inc(s["r_hi"], 1)
            pool.wait_ge(s["r_hi"], 1)
            pool.tensor_tensor(r_lo[:, :, :], r_raw[:, :, :], r_hi[:, :, :].bitcast(f32), ALU.subtract).then_inc(s["r_lo"], 1)

            def split_chunk(g, c, first):
                k = g * group + c
                pool.wait_ge(raw_in[c], (g + 1) * 16)
                if not first:
                    pool.wait_ge(s["down"], (g - 1) * per_group + (B - 1) * group + c + 1)
                pool.tensor_tensor(w_hi[:, c, :], raw[:, c, :], zero.broadcast_to([P, WN]), ALU.add).then_inc(s["split_hi"], 1)
                pool.wait_ge(s["split_hi"], k + 1)
                pool.tensor_tensor(w_lo[:, c, :], raw[:, c, :], w_hi[:, c, :].bitcast(f32), ALU.subtract).then_inc(s["split_lo"], 1)

            for c in range(group):
                split_chunk(0, c, True)
            with pool.Fori(1, groups) as g:
                for c in range(group):
                    split_chunk(g, c, False)

        @block.scalar
        def _(act):
            def guess(f):
                nt = slice(f * NT, (f + 1) * NT)
                act.preload_act_table_set(LN_EXP_SET)
                act.wait_ge(s["var_eps"], f + 1)
                act.activation(lnv[:, nt], ve[:, nt], ACT.Ln).then_inc(s["ln_var"], 1)
                act.wait_ge(s["ln_var"], f + 1)
                act.activation(r0[:, nt], lnv[:, nt], ACT.Exp, scale=-0.5).then_inc(s["rstd0"], 1)

            def turned(f, k):
                act.wait_ge(s["xT_psum"], KC * f + k + 1)
                act.activation(xT_hi[:, k, f * T:(f + 1) * T], front_bank(f, k), ACT.Copy).then_inc(s["xT_hi"], 1)

            def weights_turned(f):
                act.wait_ge(s["wT_psum"], f + 1)
                act.activation(wT[:, f * T:(f + 1) * T], bank(7)[0:WR, :].bitcast(bf16)[:, 0:T], ACT.Copy).then_inc(s["wT"], 1)

            def pieces(b, c):
                if c == 0 and b + 1 < B:
                    routing["scalar"](act, bank(7)[:, 0:NT * n_exp], b + 1)
                if c in (1, 2) and b + 2 < B:
                    turned(b + 2, c - 1)
                if c == 3 and b + 1 < B:
                    weights_turned(b + 1)

            def unit(u, i, first):
                q = i % 2
                act.wait_ge(s["gate_psum"], u + 1)
                if not (first and i < 2):
                    act.wait_ge(s["gated"], u - 1)
                act.activation(sil[q][:, :], bank(2 + q), ACT.Silu).then_inc(s["silu"], 1)
                act.wait_ge(s["scaled"], u + 1)
                if not (first and i < 2):
                    act.wait_ge(s["down"], u - 1)
                act.activation(h_hi[q][:, :], h[q][:, :], ACT.Copy).then_inc(s["h_hi"], 1)

            guess(0)
            guess(1)
            for k in range(KC):
                turned(0, k)
            routing["scalar"](act, bank(7)[:, 0:NT * n_exp], 0)
            for k in range(KC):
                turned(1, k)
            weights_turned(0)
            for f in range(2, B):
                guess(f)
            for i in range(per_group):
                unit(i, i, True)
                pieces(i // group, i % group)
            with act.Fori(1, groups) as g:
                for i in range(per_group):
                    unit(g * per_group + i, i, False)

        @block.vector
        def _(dve):
            step = Chain(dve, s["chain"])

            def moments(f):
                nt = slice(f * NT, (f + 1) * NT)
                for i in range(f * NT, (f + 1) * NT):
                    last = dve.bn_stats(st[:, i, :], x[:, i * D:(i + 1) * D])
                last.then_inc(s["stats"], 1)
                dve.wait_ge(s["stats"], f + 1)
                for i in range(f * NT, (f + 1) * NT):
                    last = dve.bn_aggr(mv[:, i, :], st[:, i, :])
                last.then_inc(s["moments"], 1)
                dve.wait_ge(s["moments"], f + 1)
                dve.tensor_scalar(ve[:, nt], mv[:, nt, 1], EPS, None, ALU.add).then_inc(s["var_eps"], 1)

            def normal(f):
                nt = slice(f * NT, (f + 1) * NT)
                dve.wait_ge(s["rstd0"], f + 1)
                step(dve.scalar_tensor_tensor(n1[:, nt], r0[:, nt], -0.5, r0[:, nt], ALU.mult, ALU.mult))
                step(dve.tensor_tensor(n2[:, nt], n1[:, nt], ve[:, nt], ALU.mult))
                step(dve.scalar_tensor_tensor(rstd[:, nt], n2[:, nt], 1.5, r0[:, nt], ALU.add, ALU.mult))
                if f >= 2:
                    dve.wait_ge(s["xT_psum"], KC * (f - 1))
                for i in range(NT):
                    j = f * NT + i
                    last = dve.tensor_scalar(xhat[f % 2][:, i, :], x[:, j * D:(j + 1) * D], mv[:, j, 0:1], rstd[:, j:j + 1], ALU.subtract, ALU.mult)
                last.then_inc(s["xhat"], 1)

            def turned(f, k):
                dve.wait_ge(s["xT_hi"], KC * f + k + 1)
                tt = slice(f * T, (f + 1) * T)
                dve.tensor_tensor(xT_lo[:, k, tt], front_bank(f, k), xT_hi[:, k, tt].bitcast(f32), ALU.subtract).then_inc(s["xT_lo"], 1)

            def split_weights(f, w):
                parts = [wx[:, :, k * n_exp:(k + 1) * n_exp] for k in range(3)]
                rest = (routing["rest0"], routing["rest1"])
                if f > 0:
                    dve.wait_ge(s["wT_psum"], f)
                step(dve.tensor_copy(parts[0], w))
                step(dve.tensor_tensor(rest[0][:, :, :], w, parts[0], ALU.subtract))
                step(dve.tensor_copy(parts[1], rest[0][:, :, :]))
                step(dve.tensor_tensor(rest[1][:, :, :], rest[0][:, :, :], parts[1], ALU.subtract))
                dve.tensor_copy(parts[2], rest[1][:, :, :]).then_inc(s["wx"], 1)
                dve.wait_ge(s["wx"], f + 1)

            def pieces(b, c):
                if b + 1 < B:
                    if c == 0:
                        routing["ranks"](dve, step, bank(7)[:, 0:NT * n_exp], side, b + 1)
                    if c == 1:
                        routed[b + 1] = routing["weights"](dve, step, b + 1)
                    if c == 2:
                        split_weights(b + 1, routed[b + 1])
                if b + 2 < B and c in (1, 2):
                    turned(b + 2, c - 1)
                if b + 3 < B and c == 3:
                    normal(b + 3)

            routed = {}
            step(dve.memset(wx[:, :, 3 * n_exp:], 0.0))
            if n_exp == E1:
                step(dve.memset(wx[:, :, 3 * E1:3 * E1 + 1], 1.0))
            moments(0)
            normal(0)
            moments(1)
            for k in range(KC):
                turned(0, k)
            normal(1)
            dve.wait_ge(s["small_in"], 64)
            routing["ranks"](dve, step, bank(7)[:, 0:NT * n_exp], side, 0)
            for k in range(KC):
                turned(1, k)
            split_weights(0, routing["weights"](dve, step, 0))
            for f in range(2, B):
                moments(f)
            normal(2)

            def unit(u, i, first):
                q = i % 2
                dve.wait_ge(s["up_psum"], u + 1)
                dve.wait_ge(s["silu"], u + 1)
                dve.tensor_tensor(gat[q][:, :], bank(4 + q), sil[q][:, :], ALU.mult).then_inc(s["gated"], 1)
                if not (first and i < 2):
                    dve.wait_ge(s["h_lo"], u - 1)
                dve.wait_ge(s["gated"], u + 1)
                dve.tensor_tensor(h[q][:, :], bank(6 + (0 if first else q)), gat[q][:, :], ALU.mult).then_inc(s["scaled"], 1)
                dve.wait_ge(s["h_hi"], u + 1)
                dve.tensor_tensor(h_lo[q][:, :], h[q][:, :], h_hi[q][:, :].bitcast(f32), ALU.subtract).then_inc(s["h_lo"], 1)

            def gather(y, b):
                dve.wait_ge(s["down"], (y + 1) * group)
                xs = x[:, b * NT * D:(b + 1) * NT * D]
                dve.tensor_tensor(xs, xs, bank(0, 2), ALU.add).then_inc(s["y_added"], 1)

            def run(g, first):
                for b in range(B):
                    for c in range(group):
                        i = b * group + c
                        unit(g * per_group + i, i, first)
                        if c == 0 and not (first and b == 0):
                            gather(g * B + b - 1, (b - 1) % B)
                        if first:
                            pieces(b, c)

            run(0, True)
            with dve.Fori(1, groups) as g:
                run(g, False)
            gather(groups * B - 1, B - 1)

        @block.tensor
        def _(pe):
            def turned(f, k):
                if k == 0:
                    pe.wait_ge(s["xhat"], f + 1)
                    if f > 0:
                        pe.wait_ge(s[logits_read], f)
                elif f > 0:
                    pe.wait_ge(s["xT_lo"], KC * f + 1)
                for i in range(NT):
                    last = pe.transpose(front_bank(f, k)[:, i * P:(i + 1) * P], xhat[f % 2][:, i, k * P:(k + 1) * P], ident)
                last.then_inc(s["xT_psum"], 1)

            def logits(f):
                pe.wait_ge(s["r_lo"], 1)
                pe.wait_ge(s["xT_lo"], KC * (f + 1))
                if f > 0:
                    pe.wait_ge(s["wT"], f)
                for i in range(NT):
                    for k in range(KC):
                        tt = slice(f * T + i * P, f * T + (i + 1) * P)
                        last = mm3(pe, bank(7)[:, i * n_exp:(i + 1) * n_exp], xT_hi[:, k, tt], xT_lo[:, k, tt], r_hi[:, k, :], r_lo[:, k, :], k == 0, k == KC - 1)
                last.then_inc(s["logits"], 1)

            def weights_turned(f):
                pe.wait_ge(s["wx"], f + 1)
                if f + 1 < B:
                    pe.wait_ge(s["xT_lo"], KC * (f + 2))
                for i in range(NT):
                    last = pe.transpose(bank(7)[0:WR, :].bitcast(bf16)[:, i * P:(i + 1) * P], wx[:, i, :], conb[:, 0:P])
                last.then_inc(s["wT_psum"], 1)

            def pieces(b, c):
                if c == 0 and b + 1 < B:
                    logits(b + 1)
                if c in (1, 2) and b + 2 < B:
                    turned(b + 2, c - 1)
                if c == 3 and b + 1 < B:
                    weights_turned(b + 1)

            for k in range(KC):
                turned(0, k)
            logits(0)
            for k in range(KC):
                turned(1, k)
            weights_turned(0)

            def up(u, i, first, fresh):
                b, c, q = i // group, i % group, i % 2
                tt = slice(b * T, (b + 1) * T)
                if fresh is not None:
                    pe.wait_ge(s["split_lo"], fresh)
                for name, at, out, used in (("gate_psum", 0, bank(2 + q), "silu"), ("up_psum", KC * P, bank(4 + q), "gated")):
                    if not (first and i < 2):
                        pe.wait_ge(s[used], u - 1)
                    for k in range(KC):
                        cc = slice(at + k * P, at + (k + 1) * P)
                        last = mm3(pe, out, w_hi[:, c, cc], w_lo[:, c, cc], xT_hi[:, k, tt], xT_lo[:, k, tt], k == 0, k == KC - 1)
                    if name == "gate_psum":
                        last.then_inc(s[name], 1)

            def spread(u, i, first, chunk):
                b, q = i // group, i % 2
                tt = slice(b * T, (b + 1) * T)
                if first and i > 0 or not first and i == 0:
                    pe.wait_ge(s["scaled"], u)
                elif not first:
                    pe.wait_ge(s["scaled"], u - 1)
                pe.matmul(bank(6 + (0 if first else q)), sel[:, chunk * P:(chunk + 1) * P] if isinstance(chunk, int) else sel[:, bass.ds(chunk * P, P)], wT[:, tt], start=True, stop=True).then_inc(s["up_psum"], 1)

            def down(u, i, y):
                c, q = i % group, i % 2
                pe.wait_ge(s["h_lo"], u + 1)
                if c == 0 and y is not None:
                    pe.wait_ge(s["y_added"], y)
                for t in range(NT):
                    out = bank(t // 2)[:, (t % 2) * D:(t % 2 + 1) * D]
                    dn = slice(2 * KC * P, 2 * KC * P + D)
                    tt = slice(t * P, (t + 1) * P)
                    last = mm3(pe, out, h_hi[q][:, tt], h_lo[q][:, tt], w_hi[:, c, dn], w_lo[:, c, dn], c == 0 and t % 2 == 0, c == group - 1)
                last.then_inc(s["down"], 1)

            def run(g, first):
                for i in range(per_group):
                    u = g * per_group + i
                    c = i % group
                    up(u, i, first, g * group + c + 1 if i < group else None)
                    if first and c == 0:
                        pe.wait_ge(s["wT"], i // group + 1)
                    spread(u, i, first, g * group + c)
                    if not (first and i == 0):
                        j = (i - 1) % per_group
                        bj = (i - 1) // group
                        y = None if first and bj == 0 else g * B + bj
                        down(u - 1, j, y)
                    if first:
                        pieces(i // group, c)

            run(0, True)
            with pe.Fori(1, groups) as g:
                run(g, False)
            down(groups * per_group - 1, per_group - 1, groups * B - 1)


def golden_route(sb, s):
    n = NT
    inv = sb("inv_temp", [P, 1])
    z, inh, off, dist, w0, fb, zone, w1, rank, fw, rest0, rest1 = (
        sb(k, [P, n, E0]) for k in ("z", "inh", "off", "dist", "w0", "fb", "zone", "w1", "rank", "fw", "rest0", "rest1"))
    less, same = sb("less", [P, n, E0, E0]), sb("same", [P, n, E0, E0])
    wsum, none, some, fsum, finv, total, tinv = (sb(k, [P, n]) for k in ("wsum", "none", "some", "fsum", "finv", "total", "tinv"))
    flat = lambda t: t[:, :, :].rearrange("p i e -> p (i e)")
    wide = lambda t: t[:, :].unsqueeze(2).broadcast_to([P, n, E0])

    def scalar(act, logits, f):
        act.wait_ge(s["z"], f + 1)
        act.activation(flat(inh), flat(z), ACT.Sigmoid).then_inc(s["inh"], 1)
        act.wait_ge(s["dist"], f + 1)
        act.activation(flat(w0), flat(dist), ACT.Exp, scale=-1.0 / 0.1).then_inc(s["w0"], 1)
        act.activation(flat(fb), flat(dist), ACT.Exp, scale=-1.0 / 0.3).then_inc(s["fb"], 1)

    def ranks(dve, step, logits, side, f):
        tie = side[:, E1:E1 + E0 * E0].rearrange("p (a c) -> p a c", a=E0).unsqueeze(1).broadcast_to([P, n, E0, E0])
        step(dve.reciprocal(inv[:, :], side[:, 0:1]))
        dve.wait_ge(s["logits"], f + 1)
        dve.tensor_scalar(flat(z), logits, inv[:, 0:1], None, ALU.mult).then_inc(s["z"], 1)
        dve.wait_ge(s["inh"], f + 1)
        step(dve.tensor_scalar(flat(off), flat(inh), CENTER, None, ALU.subtract))
        dve.scalar_tensor_tensor(flat(dist), flat(off), -1.0, flat(off), ALU.mult, ALU.max).then_inc(s["dist"], 1)
        dve.wait_ge(s["dist"], f + 1)
        step(dve.tensor_scalar(flat(zone), flat(inh), LOWER, None, ALU.is_ge))
        step(dve.scalar_tensor_tensor(flat(off), flat(inh), UPPER, flat(zone), ALU.is_le, ALU.mult))
        step(dve.tensor_tensor(less[:, :, :, :], dist[:, :, :].unsqueeze(2).broadcast_to([P, n, E0, E0]),
                               dist[:, :, :].unsqueeze(3).broadcast_to([P, n, E0, E0]), ALU.is_lt))
        step(dve.tensor_tensor(same[:, :, :, :], dist[:, :, :].unsqueeze(2).broadcast_to([P, n, E0, E0]),
                               dist[:, :, :].unsqueeze(3).broadcast_to([P, n, E0, E0]), ALU.is_equal))
        step(dve.tensor_tensor(same[:, :, :, :], same[:, :, :, :], tie, ALU.mult))
        step(dve.tensor_tensor(less[:, :, :, :], less[:, :, :, :], same[:, :, :, :], ALU.add))
        step(dve.tensor_reduce(rank[:, :, :], less[:, :, :, :], AX.X, ALU.add))

    def weights(dve, step, f):
        dve.wait_ge(s["fb"], f + 1)
        step(dve.scalar_tensor_tensor(flat(fw), flat(rank), float(TOP0), flat(fb), ALU.is_lt, ALU.mult))
        step(dve.tensor_reduce(fsum[:, :], fw[:, :, :], AX.X, ALU.add))
        step(dve.tensor_scalar(fsum[:, :], fsum[:, :], 1e-8, None, ALU.max))
        step(dve.reciprocal(finv[:, :], fsum[:, :]))
        step(dve.tensor_tensor(fw[:, :, :], fw[:, :, :], wide(finv), ALU.mult))
        step(dve.tensor_tensor(flat(w1), flat(w0), flat(off), ALU.mult))
        step(dve.tensor_reduce(wsum[:, :], w1[:, :, :], AX.X, ALU.add))
        step(dve.tensor_scalar(none[:, :], wsum[:, :], 1e-8, None, ALU.is_lt))
        step(dve.tensor_scalar(some[:, :], none[:, :], -1.0, 1.0, ALU.mult, ALU.add))
        step(dve.tensor_tensor(fw[:, :, :], fw[:, :, :], wide(none), ALU.mult))
        step(dve.tensor_tensor(w1[:, :, :], w1[:, :, :], wide(some), ALU.mult))
        step(dve.tensor_tensor(flat(w1), flat(w1), flat(fw), ALU.add))
        step(dve.tensor_reduce(total[:, :], w1[:, :, :], AX.X, ALU.add))
        step(dve.tensor_scalar(total[:, :], total[:, :], 1e-8, None, ALU.max))
        step(dve.reciprocal(tinv[:, :], total[:, :]))
        step(dve.tensor_tensor(w1[:, :, :], w1[:, :, :], wide(tinv), ALU.mult))
        return w1[:, :, :]

    return {"scalar": scalar, "ranks": ranks, "weights": weights, "rest0": rest0, "rest1": rest1}


def top_route(sb, s):
    n, m = NT, E1 // G1
    sig, sc, ms, rank, w1, rest0, rest1 = (sb(k, [P, n, E1]) for k in ("sig", "sc", "ms", "rank", "w1", "rest0", "rest1"))
    less, same = sb("less", [P, NT, E1, E1]), sb("same", [P, NT, E1, E1])
    gmax, grank, gm, pen = (sb(k, [P, n, G1]) for k in ("gmax", "grank", "gm", "pen"))
    gless, gsame = sb("gless", [P, n, G1, G1]), sb("gsame", [P, n, G1, G1])
    total, tinv = sb("total", [P, n]), sb("tinv", [P, n])
    flat = lambda t: t[:, :, :].rearrange("p i e -> p (i e)")
    grouped = lambda t: t[:, :, :].rearrange("p i (g e) -> p (i g) e", g=G1)
    spread = lambda t: t[:, :, :].rearrange("p i g -> p (i g)").unsqueeze(2).broadcast_to([P, n * G1, m])

    def scalar(act, logits, f):
        act.wait_ge(s["logits"], f + 1)
        act.activation(flat(sig), logits, ACT.Sigmoid).then_inc(s["inh"], 1)

    def ranks(dve, step, logits, side, f):
        t0 = E1 + E0 * E0
        tie = side[:, t0:t0 + E1 * E1].rearrange("p (a c) -> p a c", a=E1).unsqueeze(1).broadcast_to([P, NT, E1, E1])
        gtie = side[:, t0 + E1 * E1:].rearrange("p (a c) -> p a c", a=G1).unsqueeze(1).broadcast_to([P, n, G1, G1])
        dve.wait_ge(s["inh"], f + 1)
        step(dve.tensor_tensor(sc[:, :, :], sig[:, :, :], side[:, 0:E1].unsqueeze(1).broadcast_to([P, n, E1]), ALU.add))
        step(dve.tensor_reduce(gmax[:, :, :].rearrange("p i g -> p (i g)"), grouped(sc), AX.X, ALU.max))
        a, c = gmax[:, :, :].unsqueeze(2).broadcast_to([P, n, G1, G1]), gmax[:, :, :].unsqueeze(3).broadcast_to([P, n, G1, G1])
        step(dve.tensor_tensor(gless[:, :, :, :], a, c, ALU.is_gt))
        step(dve.tensor_tensor(gsame[:, :, :, :], a, c, ALU.is_equal))
        step(dve.tensor_tensor(gsame[:, :, :, :], gsame[:, :, :, :], gtie, ALU.mult))
        step(dve.tensor_tensor(gless[:, :, :, :], gless[:, :, :, :], gsame[:, :, :, :], ALU.add))
        step(dve.tensor_reduce(grank[:, :, :], gless[:, :, :, :], AX.X, ALU.add))
        step(dve.tensor_scalar(flat(gm), flat(grank), float(TOPG1), None, ALU.is_lt))
        step(dve.tensor_scalar(flat(pen), flat(gm), -1.0, BIG, ALU.add, ALU.mult))
        step(dve.tensor_tensor(grouped(ms), grouped(sc), spread(gm), ALU.mult))
        step(dve.tensor_tensor(grouped(ms), grouped(ms), spread(pen), ALU.add))
        a, c = ms[:, :, :].unsqueeze(2).broadcast_to([P, NT, E1, E1]), ms[:, :, :].unsqueeze(3).broadcast_to([P, NT, E1, E1])
        step(dve.tensor_tensor(less[:, :, :, :], a, c, ALU.is_gt))
        step(dve.tensor_tensor(same[:, :, :, :], a, c, ALU.is_equal))
        step(dve.tensor_tensor(same[:, :, :, :], same[:, :, :, :], tie, ALU.mult))

    def weights(dve, step, f):
        step(dve.tensor_tensor(less[:, :, :, :], less[:, :, :, :], same[:, :, :, :], ALU.add))
        step(dve.tensor_reduce(rank[:, :, :], less[:, :, :, :], AX.X, ALU.add))
        step(dve.scalar_tensor_tensor(flat(w1), flat(rank), float(TOP1), flat(sig), ALU.is_lt, ALU.mult))
        step(dve.tensor_reduce(total[:, :], w1[:, :, :], AX.X, ALU.add))
        step(dve.reciprocal(tinv[:, :], total[:, :]))
        step(dve.tensor_tensor(w1[:, :, :], w1[:, :, :], tinv[:, :].unsqueeze(2).broadcast_to([P, n, E1]), ALU.mult))
        return w1[:, :, :]

    return {"scalar": scalar, "ranks": ranks, "weights": weights, "rest0": rest0, "rest1": rest1}


FRONT_AT = {
    "dve": (6, 9, 12, 20, 14, 16, 19, 21, 23, 24, 25, 26, 27, 29),
    "act": (8, 11, 18, 20, 26, 28, 27, 29),
    "pe": (13, 15, 17, 19, 22, 23, 24, 25, 26, 28),
}
UNITS = tuple((4, (h,)) for h in range(4)) + tuple((3, (h,)) for h in range(4)) + ((2, (0, 1)), (2, (2, 3)), (1, (0, 1)), (1, (2, 3)))
NU = len(UNITS)
MAX_STEP = (1, 1, 2, 2, 3, 3, 4, 4, 5, 5, 6, 6)
VALUE_STEP = (4, 8, 10, NU)
KEY_BANKS = 3


def after(engine, sem, count):
    if not isinstance(count, int) or count > 0:
        engine.wait_ge(sem, count)


def rotary_attention(nc, kept, x, psum, con, conb, dram):
    ctx = ExitStack()
    with ctx:
        def sb(name, shape, dt=f32):
            return ctx.enter_context(nc.sbuf_tensor(f"a1_{name}", shape, dt))

        s = sems(nc, kept, "a1", "rope_in w_in wo_in small_in w_hi w_lo wo_hi wo_lo sel_r v_pad "
                 "stats moments var_eps ln_var rstd0 newton ln_ms rms0 rms_newton xhat xr xT_psum xw xT_hi xT_lo residual "
                 "qk_psum v_psum v_raw v_sb rot q_rot k_rot rot_hi rot_lo k_psum k_stack q_psum q_stack q_stack_too "
                 "score_psum max max_parts mT_psum mT key_psum prob_ready ot_psum o_raw sum_psum sum_sb recip o_t o_hi o_lo wo_psum x_out")
        w_hi, w_lo = sb("w_hi", [P, KC, W1N], f32r), sb("w_lo", [P, KC, W1N], f32r)
        wo_hi, wo_lo = sb("wo_hi", [P, NST, D], f32r), sb("wo_lo", [P, NST, D], f32r)
        rope = sb("rope", [P, C_SEL])
        sel = sb("sel", [P, 16 * P], f32r)
        cols, rows = sb("cols", [P, 6]), sb("rows", [P, 2 * D])
        st, mv = sb("st", [P, NT, 6]), sb("mv", [P, NT, 2])
        ve, lnv, r0, n1, n2, rstd, ms, lnm, m0, m1, m2, rms = (
            sb(k, [P, NT]) for k in ("ve", "lnv", "r0", "n1", "n2", "rstd", "ms", "lnm", "m0", "m1", "m2", "rms"))
        xhat, xr = sb("xhat", [P, NT, D]), sb("xr", [P, NT, D])
        xw = sb("xw", [P, KC, T])
        xT_hi, xT_lo = sb("xT_hi", [P, KC, T], f32r), sb("xT_lo", [P, KC, T], f32r)
        ra, rb_ = sb("ra", [P, 2, T]), sb("rb_", [P, 2, T])
        rot = sb("rot", [P, 2, T])
        rot_hi, rot_lo = sb("rot_hi", [P, 2, T], f32r), sb("rot_lo", [P, 2, T], f32r)
        k_stack = [sb(f"k_stack{i}", [P, T], f32r) for i in range(2)]
        q_stack = [sb(f"q_stack{i}", [P, HPT, T], f32r) for i in range(2)]
        vs = sb("vs", [P, NT, H1, 32])
        v_raw = sb("v_raw", [P, NT, D])
        prob = [sb(f"prob{i}", [P, HPT, T]) for i in range(2)]
        mx, mrest = sb("mx", [P, NT, HPT]), sb("mrest", [P, NT, HPT])
        mparts = sb("mparts", [P, NT, HPT, 32], bf16)
        mT = [sb(f"mT{i}", [P, T], bf16) for i in range(2)]
        o_raw, o_sum, rinv, o_t = (sb(k, [P, T]) for k in ("o_raw", "o_sum", "rinv", "o_t"))
        o_hi, o_lo = sb("o_hi", [P, NST, T], f32r), sb("o_lo", [P, NST, T], f32r)
        held = sb("held", [P, 4])
        bank = lambda i, m=1: psum[:, 512 * i:512 * (i + m)]
        ident = con[:, C_ID:C_ID + P]
        xb = lambda b: x[:, b * NT * D:(b + 1) * NT * D] if isinstance(b, int) else x[:, bass.ds(b * NT * D, NT * D)]

        def heads(one, unit):
            blocks, hh = unit
            return one[:, 0:len(hh) * blocks * P].rearrange("p (h t) -> p h t", h=len(hh))

        misc = bank(7)

        def hold(dve, place):
            dve.tensor_copy(held[:, place:place + 1], con[:, 0:1])

        w_raw, wo_raw, sel_raw = sb("w_raw", [P, KC, W1N]), sb("wo_raw", [P, NST, D]), sb("sel_raw", [P, 16 * P])

        block = ctx.enter_context(nc.Block())

        @block.sync
        def _(sp):
            sp.dma_start(w_raw[:, :, :], dram["w1"]).then_inc(s["w_in"], 16)
            sp.dma_start(cols[:, :], dram["cols1"]).then_inc(s["small_in"], 16)
            sp.dma_start(rows[:, :], dram["rows1"].broadcast_to([P, 2 * D])).then_inc(s["small_in"], 16)
            sp.dma_start(rope[:, :], dram["rope"][:, 0:C_SEL]).then_inc(s["small_in"], 16)
            sp.dma_start(sel_raw[:, :], dram["rope"][:, C_SEL:]).then_inc(s["rope_in"], 16)
            sp.dma_start(wo_raw[:, :, :], dram["wo1"]).then_inc(s["wo_in"], 16)

        @block.gpsimd
        def _(pool):
            pool.memset(vs[:, :, :, DH1 + 1:], 0.0)
            pool.memset(mparts[:, :, :, :], 0.0)
            pool.memset(vs[:, :, :, DH1:DH1 + 1], 1.0).then_inc(s["v_pad"], 1)
            for raw, hi, lo, came, s_hi, s_lo in ((w_raw, w_hi, w_lo, "w_in", "w_hi", "w_lo"), (wo_raw, wo_hi, wo_lo, "wo_in", "wo_hi", "wo_lo")):
                pool.wait_ge(s[came], 16)
                pool.tensor_copy(hi[:], raw[:]).then_inc(s[s_hi], 1)
                pool.wait_ge(s[s_hi], 1)
                pool.tensor_tensor(lo[:], raw[:], hi[:].bitcast(f32), ALU.subtract).then_inc(s[s_lo], 1)
                if came == "w_in":
                    pool.wait_ge(s["rope_in"], 16)
                    pool.tensor_copy(sel[:, :], sel_raw[:, :]).then_inc(s["sel_r"], 1)

        def every_step(pieces, engine_name):
            assert len(pieces) == len(FRONT_AT[engine_name])
            return dict(zip(FRONT_AT[engine_name], pieces))

        @block.scalar
        def _(act):
            act.wait_ge(s["small_in"], 48)
            act.preload_act_table_set(LN_EXP_SET)

            def front(f):
                def guess():
                    act.wait_ge(s["var_eps"], f + 1)
                    act.activation(lnv[:, :], ve[:, :], ACT.Ln).then_inc(s["ln_var"], 1)
                    act.wait_ge(s["ln_var"], f + 1)
                    act.activation(r0[:, :], lnv[:, :], ACT.Exp, scale=-0.5).then_inc(s["rstd0"], 1)

                def guess_rms():
                    act.wait_ge(s["newton"], 6 * f + 6)
                    act.activation(lnm[:, :], ms[:, :], ACT.Ln).then_inc(s["ln_ms"], 1)
                    act.wait_ge(s["ln_ms"], f + 1)
                    act.activation(m0[:, :], lnm[:, :], ACT.Exp, scale=-0.5).then_inc(s["rms0"], 1)

                def turned(k):
                    act.wait_ge(s["xT_psum"], KC * f + k + 1)
                    act.activation(xw[:, k, :], bank(1), ACT.Copy, scale=cols[:, 4 + k:5 + k]).then_inc(s["xw"], 1)
                    act.wait_ge(s["xw"], KC * f + k + 1)
                    act.activation(xT_hi[:, k, :], xw[:, k, :], ACT.Copy).then_inc(s["xT_hi"], 1)

                def rotated(w):
                    act.wait_ge(s[("q_rot", "k_rot")[w]], f + 1)
                    act.activation(rot_hi[:, w, :], rot[:, w, :], ACT.Copy).then_inc(s["rot_hi"], 1)

                def values(m):
                    act.wait_ge(s["v_psum"], 2 * f + m + 1)
                    act.activation(v_raw[:, 2 * m:2 * m + 2, :], bank(1).rearrange("p (i d) -> p i d", i=2), ACT.Copy).then_inc(s["v_raw"], 1)

                return every_step([guess, guess_rms, lambda: turned(0), lambda: turned(1), lambda: rotated(0), lambda: rotated(1),
                                   lambda: values(0), lambda: values(1)], "act")

            def k_stacked(tau, t):
                act.wait_ge(s["k_psum"], tau + 1)
                act.activation(k_stack[t % 2][:, :], misc, ACT.Copy).then_inc(s["k_stack"], 1)

            def q_stacked(tau, t):
                act.wait_ge(s["q_psum"], tau + 1)
                for hh in range(HPT // 2):
                    last = act.activation(q_stack[t % 2][:, hh, :], misc, ACT.Copy, scale=rope[:, C_HEAD + hh:C_HEAD + hh + 1])
                last.then_inc(s["q_stack"], 1)

            def maxima_turned(tau, t):
                act.wait_ge(s["mT_psum"], tau + 1)
                act.activation(mT[t % 2][:, :], misc.bitcast(bf16)[:, 0:T], ACT.Copy).then_inc(s["mT"], 1)

            def exps(tau, n):
                blocks, hh = UNITS[n]
                j = NT - blocks
                act.wait_ge(s["key_psum"], NU * tau + n + 1)
                after(act, s["ot_psum"], NT * tau + j - 1)
                act.activation(prob[j % 2][:, hh[0]:hh[-1] + 1, 0:blocks * P], heads(bank(4 + n % KEY_BANKS), UNITS[n]), ACT.Exp,
                               scale=0.5).then_inc(s["prob_ready"], 1)

            def finished_raw(tau):
                act.wait_ge(s["ot_psum"], NT * (tau + 1))
                after(act, s["o_t"], tau)
                act.activation(o_raw[:, :], bank(0), ACT.Copy).then_inc(s["o_raw"], 1)

            def finished_sums(tau):
                act.wait_ge(s["sum_psum"], tau + 1)
                act.activation(o_sum[:, :], misc, ACT.Copy).then_inc(s["sum_sb"], 1)

            def finished_hi(tau, t, b):
                act.wait_ge(s["o_t"], tau + 1)
                if t == 0:
                    after(act, s["wo_psum"], 2 * b)
                act.activation(o_hi[:, t, :], o_t[:, :], ACT.Copy).then_inc(s["o_hi"], 1)

            def turn(b, ahead):
                pieces = front(b + 1) if ahead else {}
                for t in range(NST):
                    tau = NST * b + t
                    one, two = ahead or t < NST - 1, ahead or t < NST - 2
                    before = t > 0 or not isinstance(b, int) or b > 0
                    for n in range(NU):
                        exps(tau, n)
                        if n == 1 and before:
                            finished_raw(tau - 1)
                        if n == 3 and before:
                            finished_sums(tau - 1)
                        if n == 8 and one:
                            maxima_turned(tau + 1, t + 1)
                        if n == 10 and two:
                            k_stacked(tau + 2, t + 2)
                        if n == 10 and two:
                            q_stacked(tau + 2, t + 2)
                        if n == 10 and before:
                            finished_hi(tau - 1, (t - 1) % NST, b)
                        if NU * t + n in pieces:
                            pieces[NU * t + n]()

            for piece in front(0).values():
                piece()
            k_stacked(0, 0)
            q_stacked(0, 0)
            maxima_turned(0, 0)
            k_stacked(1, 1)
            q_stacked(1, 1)
            turn(0, True)
            with act.Fori(1, B - 1) as b:
                turn(b, True)
            turn(B - 1, False)
            finished_raw(B * NST - 1)
            finished_sums(B * NST - 1)
            finished_hi(B * NST - 1, NST - 1, B - 1)

        @block.vector
        def _(dve):
            dve.wait_ge(s["small_in"], 48)
            dve.wait_ge(s["v_pad"], 1)

            def front(f):
                xf = lambda i: x[:, f * NT * D + i * D:f * NT * D + (i + 1) * D] if isinstance(f, int) else x[:, bass.ds(f * NT * D + i * D, D)]

                def moments():
                    for i in range(NT):
                        last = dve.bn_stats(st[:, i, :], xf(i))
                    last.then_inc(s["stats"], 1)
                    dve.wait_ge(s["stats"], f + 1)
                    hold(dve, 0)
                    for i in range(NT):
                        last = dve.bn_aggr(mv[:, i, :], st[:, i, :])
                    last.then_inc(s["moments"], 1)
                    dve.wait_ge(s["moments"], f + 1)
                    dve.tensor_scalar(ve[:, :], mv[:, :, 1], EPS, None, ALU.add).then_inc(s["var_eps"], 1)

                def refine():
                    def newton(k, ins):
                        ins.then_inc(s["newton"], 1)
                        dve.wait_ge(s["newton"], 6 * f + k)

                    dve.wait_ge(s["rstd0"], f + 1)
                    newton(1, dve.scalar_tensor_tensor(n1[:, :], r0[:, :], -0.5, r0[:, :], ALU.mult, ALU.mult))
                    newton(2, dve.tensor_tensor(n2[:, :], n1[:, :], ve[:, :], ALU.mult))
                    newton(3, dve.scalar_tensor_tensor(rstd[:, :], n2[:, :], 1.5, r0[:, :], ALU.add, ALU.mult))
                    newton(4, dve.tensor_tensor(m1[:, :], rstd[:, :], rstd[:, :], ALU.mult))
                    newton(5, dve.tensor_tensor(m2[:, :], m1[:, :], mv[:, :, 1], ALU.mult))
                    newton(6, dve.tensor_scalar(ms[:, :], m2[:, :], EPS, None, ALU.add))

                def normal():
                    for i in range(NT):
                        last = dve.tensor_scalar(xhat[:, i, :], xf(i), mv[:, i, 0:1], rstd[:, i:i + 1], ALU.subtract, ALU.mult)
                    last.then_inc(s["xhat"], 1)
                    dve.wait_ge(s["rms0"], f + 1)
                    dve.scalar_tensor_tensor(m1[:, :], m0[:, :], -0.5, m0[:, :], ALU.mult, ALU.mult).then_inc(s["rms_newton"], 1)
                    dve.wait_ge(s["rms_newton"], 3 * f + 1)
                    dve.tensor_tensor(m2[:, :], m1[:, :], ms[:, :], ALU.mult).then_inc(s["rms_newton"], 1)
                    dve.wait_ge(s["rms_newton"], 3 * f + 2)
                    dve.scalar_tensor_tensor(rms[:, :], m2[:, :], 1.5, m0[:, :], ALU.add, ALU.mult).then_inc(s["rms_newton"], 1)
                    dve.wait_ge(s["rms_newton"], 3 * f + 3)
                    dve.wait_ge(s["xhat"], f + 1)
                    for i in range(NT):
                        last = dve.tensor_scalar(xr[:, i, :], xhat[:, i, :], rms[:, i:i + 1], None, ALU.mult)
                    last.then_inc(s["xr"], 1)

                def residual():
                    dve.wait_ge(s["xr"], f + 1)
                    wide_bo = rows[:, D:2 * D].unsqueeze(1).broadcast_to([P, NT, D])
                    dve.tensor_tensor(xhat[:, :, :], xhat[:, :, :], wide_bo, ALU.add).then_inc(s["residual"], 1)
                    dve.wait_ge(s["residual"], 2 * f + 1)
                    xx = x[:, f * NT * D:(f + 1) * NT * D] if isinstance(f, int) else xb(f)
                    dve.tensor_tensor(xx, xx, xhat[:, :, :].rearrange("p i d -> p (i d)"), ALU.add).then_inc(s["residual"], 1)

                def turned(k):
                    dve.wait_ge(s["xT_hi"], KC * f + k + 1)
                    dve.tensor_tensor(xT_lo[:, k, :], xw[:, k, :], xT_hi[:, k, :].bitcast(f32), ALU.subtract).then_inc(s["xT_lo"], 1)

                cos, sin = rope[:, C_COS:C_COS + T], rope[:, C_SIN:C_SIN + T]

                def product(w, m):
                    dve.wait_ge(s["qk_psum"], 4 * f + 2 * w + m + 1)
                    dve.scalar_tensor_tensor((ra, rb_)[m][:, w, :], bank(1), cols[:, 2 * w + m:2 * w + m + 1], (cos, sin)[m],
                                             ALU.add, ALU.mult).then_inc(s["rot"], 1)
                    if m == 1:
                        dve.wait_ge(s["rot"], 4 * f + 2 * w + 2)
                        dve.tensor_tensor(rot[:, w, :], ra[:, w, :], rb_[:, w, :], ALU.add).then_inc(s[("q_rot", "k_rot")[w]], 1)

                def rotated(w):
                    dve.wait_ge(s["rot_hi"], 2 * f + w + 1)
                    dve.tensor_tensor(rot_lo[:, w, :], rot[:, w, :], rot_hi[:, w, :].bitcast(f32), ALU.subtract).then_inc(s["rot_lo"], 1)

                return every_step([moments, refine, normal, residual, lambda: output(f - 2, 0), lambda: output(f - 2, 1),
                                   lambda: turned(0), lambda: turned(1), lambda: product(0, 0), lambda: product(0, 1),
                                   lambda: product(1, 0), lambda: product(1, 1), lambda: rotated(0), lambda: rotated(1)], "dve")

            def output(b, m):
                if isinstance(b, int) and b < 0:
                    return
                dve.wait_ge(s["wo_psum"], 2 * b + m + 1)
                half = NT * D // 2
                at = b * NT * D + m * half
                xx = x[:, at:at + half] if isinstance(b, int) else x[:, bass.ds(at, half)]
                dve.tensor_tensor(xx, xx, bank(1), ALU.add).then_inc(s["x_out"], 1)

            def maxima(tau, m):
                blocks, hh = UNITS[m]
                dve.wait_ge(s["score_psum"], NU * tau + m + 1)
                dve.tensor_reduce(mx[:, blocks - 1, hh[0]:hh[-1] + 1], heads(bank(2 + m % 2), UNITS[m]), AX.X, ALU.max).then_inc(s["max"], 1)
                if m == NU - 1:
                    parts = [mparts[:, :, :, k] for k in range(3)]
                    dve.wait_ge(s["max"], NU * (tau + 1))
                    dve.tensor_scalar(parts[0], mx[:, :, :], -1.0, None, ALU.mult).then_inc(s["max_parts"], 1)
                    dve.wait_ge(s["max_parts"], 4 * tau + 1)
                    dve.scalar_tensor_tensor(mrest[:, :, :], mx[:, :, :], -1.0, parts[0], ALU.mult, ALU.subtract).then_inc(s["max_parts"], 1)
                    dve.wait_ge(s["max_parts"], 4 * tau + 2)
                    dve.tensor_copy(parts[1], mrest[:, :, :]).then_inc(s["max_parts"], 1)
                    dve.wait_ge(s["max_parts"], 4 * tau + 3)
                    dve.tensor_tensor(parts[2], mrest[:, :, :], parts[1], ALU.subtract).then_inc(s["max_parts"], 1)

            def q_stacked(tau, t):
                dve.wait_ge(s["q_stack"], tau + 1)
                for hh in range(HPT // 2, HPT):
                    last = dve.tensor_scalar(q_stack[t % 2][:, hh, :], misc, rope[:, C_HEAD + hh:C_HEAD + hh + 1], None, ALU.mult)
                last.then_inc(s["q_stack_too"], 1)

            def scaled(tau):
                dve.wait_ge(s["sum_sb"], tau + 1)
                dve.reciprocal(rinv[:, :], o_sum[:, :]).then_inc(s["recip"], 1)
                dve.wait_ge(s["recip"], tau + 1)
                after(dve, s["o_lo"], tau)
                dve.tensor_tensor(o_t[:, :], o_raw[:, :], rinv[:, :], ALU.mult).then_inc(s["o_t"], 1)

            def rest(tau, t):
                dve.wait_ge(s["o_hi"], tau + 1)
                dve.tensor_tensor(o_lo[:, t, :], o_t[:, :], o_hi[:, t, :].bitcast(f32), ALU.subtract).then_inc(s["o_lo"], 1)

            def turn(b, ahead):
                pieces = front(b + 1) if ahead else {FRONT_AT["dve"][4 + m]: (lambda m=m: output(b - 1, m)) for m in range(2)}
                for t in range(NST):
                    tau = NST * b + t
                    more = ahead or t < NST - 1
                    finished = t > 0 or not isinstance(b, int) or b > 0
                    for n in range(NU):
                        for m in range(NU):
                            if more and MAX_STEP[m] == n:
                                maxima(tau + 1, m)
                        if n == 2 and t == 0:
                            dve.wait_ge(s["v_raw"], 2 * b + 2)
                            after(dve, s["ot_psum"], NT * NST * b)
                            for i in range(NT):
                                last = dve.tensor_tensor(vs[:, i, :, 0:DH1], v_raw[:, i, :].rearrange("p (h v) -> p h v", h=H1),
                                                         rows[:, 0:D].rearrange("p (h v) -> p h v", h=H1), ALU.add)
                            last.then_inc(s["v_sb"], 1)
                        if n == 7 and finished:
                            scaled(tau - 1)
                        if n == 10 and (ahead or t < NST - 2):
                            q_stacked(tau + 2, t + 2)
                        if n == 10 and finished:
                            rest(tau - 1, (t - 1) % NST)
                        if NU * t + n in pieces:
                            pieces[NU * t + n]()

            for piece in front(0).values():
                piece()
            q_stacked(0, 0)
            for m in range(NU):
                maxima(0, m)
            q_stacked(1, 1)
            turn(0, True)
            with dve.Fori(1, B - 1) as b:
                turn(b, True)
            turn(B - 1, False)
            scaled(B * NST - 1)
            rest(B * NST - 1, NST - 1)
            for m in range(2):
                output(B - 1, m)

        @block.tensor
        def _(pe):
            def output(b, m):
                if isinstance(b, int) and b < 0:
                    return
                if m == 0:
                    pe.wait_ge(s["wo_lo"], 1)
                    pe.wait_ge(s["o_lo"], NST * (b + 1))
                else:
                    pe.wait_ge(s["x_out"], 2 * b + 1)
                for i in (2 * m, 2 * m + 1):
                    for k in range(NST):
                        tt = slice(i * P, (i + 1) * P)
                        last = mm3(pe, bank(1)[:, (i % 2) * D:(i % 2 + 1) * D], o_hi[:, k, tt], o_lo[:, k, tt],
                                   wo_hi[:, k, :], wo_lo[:, k, :], k == 0, k == NST - 1)
                last.then_inc(s["wo_psum"], 1)

            def front(f):
                def turned(k):
                    pe.wait_ge(s["xr"], f + 1)
                    if k == 1:
                        pe.wait_ge(s["xT_hi"], KC * f + 1)
                    elif not isinstance(f, int) or f > 1:
                        pe.wait_ge(s["x_out"], 2 * f - 2)
                    elif f == 1:
                        pe.wait_ge(s["v_raw"], 2)
                    for i in range(NT):
                        last = pe.transpose(bank(1)[:, i * P:(i + 1) * P], xr[:, i, k * P:(k + 1) * P], ident)
                    last.then_inc(s["xT_psum"], 1)

                def project(m):
                    if m == 0:
                        pe.wait_ge(s["w_lo"], 1)
                        pe.wait_ge(s["xT_lo"], KC * f + KC)
                    else:
                        pe.wait_ge(s["rot"], 4 * f + m)
                    for k in range(KC):
                        col = m * P
                        last = mm3(pe, bank(1), w_hi[:, k, col:col + P], w_lo[:, k, col:col + P], xT_hi[:, k, :], xT_lo[:, k, :], k == 0, k == KC - 1)
                    last.then_inc(s["qk_psum"], 1)

                def values(m):
                    if m == 0:
                        pe.wait_ge(s["rot"], 4 * f + 4)
                    else:
                        pe.wait_ge(s["v_raw"], 2 * f + 1)
                    for i in (2 * m, 2 * m + 1):
                        for k in range(KC):
                            tt = slice(i * P, (i + 1) * P)
                            last = mm3(pe, bank(1)[:, (i % 2) * D:(i % 2 + 1) * D], xT_hi[:, k, tt], xT_lo[:, k, tt],
                                       w_hi[:, k, W1V:W1V + D], w_lo[:, k, W1V:W1V + D], k == 0, k == KC - 1)
                    last.then_inc(s["v_psum"], 1)

                return every_step([lambda: output(f - 2, 0), lambda: output(f - 2, 1), lambda: turned(0), lambda: turned(1), lambda: project(0),
                                   lambda: project(1), lambda: project(2), lambda: project(3), lambda: values(0), lambda: values(1)], "pe")

            def stack(tau, t, w):
                if w == 1:
                    after(pe, s["mT"], tau)
                else:
                    pe.wait_ge(s["k_stack"], tau + 1)
                at = (t * 2 + w) * 2 * P
                pe.matmul(misc, sel[:, at:at + P], rot_hi[:, w, :], start=True, stop=False, skip_group_check=True)
                pe.matmul(misc, sel[:, at + P:at + 2 * P], rot_lo[:, w, :], start=False, stop=True, skip_group_check=True).then_inc(
                    s[("q_psum", "k_psum")[w]], 1)

            def scores(tau, t, m):
                blocks, hh = UNITS[m]
                i = blocks - 1
                if m == 0:
                    pe.wait_ge(s["q_stack_too"], tau + 1)
                after(pe, s["max"], NU * tau + m - 1 if m > 1 else NU * tau)
                out = heads(bank(2 + m % 2), UNITS[m])
                for e, h in enumerate(hh):
                    pe.matmul(out[:, e, :], q_stack[t % 2][:, h, i * P:(i + 1) * P], k_stack[t % 2][:, 0:(i + 1) * P],
                              start=True, stop=False, skip_group_check=True)
                    last = pe.matmul(out[:, e, i * P:(i + 1) * P], conb[:, 0:P], conb[:, P:2 * P],
                                     start=False, stop=True, skip_group_check=True)
                last.then_inc(s["score_psum"], 1)

            def maxima_turned(tau):
                pe.wait_ge(s["max_parts"], 4 * tau + 4)
                after(pe, s["sum_sb"], tau - 1)
                for i in range(NT):
                    last = pe.transpose(misc.bitcast(bf16)[:, i * P:(i + 1) * P], mparts[:, i, :, :].rearrange("p h k -> p (h k)"), conb[:, 0:P])
                last.then_inc(s["mT_psum"], 1)

            def keys(tau, t, n):
                blocks, hh = UNITS[n]
                j = NT - blocks
                if n == 0:
                    pe.wait_ge(s["mT"], tau + 1)
                after(pe, s["prob_ready"], NU * tau + n + 1 - KEY_BANKS)
                out = heads(bank(4 + n % KEY_BANKS), UNITS[n])
                for e, h in enumerate(hh):
                    pe.matmul(out[:, e, :], k_stack[t % 2][:, j * P:(j + 1) * P], q_stack[t % 2][:, h, j * P:],
                              start=True, stop=False, skip_group_check=True)
                    pe.matmul(out[:, e, :], conb[:, (2 + h) * P:(3 + h) * P], mT[t % 2][:, j * P:], start=False, stop=False, skip_group_check=True)
                    last = pe.matmul(out[:, e, 0:P], conb[:, P:2 * P], conb[:, 0:P], start=False, stop=True, skip_group_check=True)
                last.then_inc(s["key_psum"], 1)

            def weighted(tau, t, j):
                pe.wait_ge(s["prob_ready"], NU * tau + (4, 8, 10, 12)[j])
                if j == 0:
                    after(pe, s["o_raw"], tau)
                for hh in range(HPT):
                    q = 32 * hh
                    last = pe.matmul(bank(0)[q:q + 32, j * P:], vs[:, j, t * HPT + hh, :], prob[j % 2][:, hh, 0:T - j * P],
                                     start=(j == 0), stop=(j == NT - 1), tile_position=(0, q), skip_group_check=True)
                last.then_inc(s["ot_psum"], 1)

            def sums(tau):
                pe.wait_ge(s["o_raw"], tau + 1)
                after(pe, s["q_stack_too"], tau + 3 if not isinstance(tau, int) else min(tau + 3, B * NST))
                pe.matmul(misc, rope[:, C_SUM:C_SUM + P], o_raw[:, :], start=True, stop=True, skip_group_check=True).then_inc(s["sum_psum"], 1)

            def turn(b, ahead):
                pieces = front(b + 1) if ahead else {FRONT_AT["pe"][m]: (lambda m=m: output(b - 1, m)) for m in range(2)}
                for t in range(NST):
                    tau = NST * b + t
                    one, two = ahead or t < NST - 1, ahead or t < NST - 2
                    before = t > 0 or not isinstance(b, int) or b > 0
                    for n in range(NU):
                        if n + 2 < NU:
                            keys(tau, t, n + 2)
                        elif one:
                            keys(tau + 1, t + 1, n + 2 - NU)
                        for m in range(NU):
                            if one and MAX_STEP[m] == n:
                                scores(tau + 1, (t + 1) % NST, m)
                        if n == 3 and before:
                            sums(tau - 1)
                        if n == 8 and one:
                            maxima_turned(tau + 1)
                        if n == 9 and two:
                            if t == NST - 2:
                                pe.wait_ge(s["rot_lo"], 2 * (b + 1) + 2)
                            stack(tau + 2, (t + 2) % NST, 1)
                        if n == 4 and t == 0:
                            pe.wait_ge(s["v_sb"], b + 1)
                        if n == 0 and before:
                            weighted(tau - 1, (t - 1) % NST, NT - 1)
                        if n in VALUE_STEP:
                            weighted(tau, t, VALUE_STEP.index(n))
                        if n == 10 and two:
                            stack(tau + 2, (t + 2) % NST, 0)
                        if NU * t + n in pieces:
                            pieces[NU * t + n]()

            for piece in front(0).values():
                piece()
            pe.wait_ge(s["sel_r"], 1)
            pe.wait_ge(s["rot_lo"], 2)
            stack(0, 0, 1)
            stack(0, 0, 0)
            for m in range(NU):
                scores(0, 0, m)
            pe.wait_ge(s["q_stack_too"], 1)
            maxima_turned(0)
            stack(1, 1, 1)
            stack(1, 1, 0)
            keys(0, 0, 0)
            keys(0, 0, 1)
            turn(0, True)
            with pe.Fori(1, B - 1) as b:
                turn(b, True)
            turn(B - 1, False)
            weighted(B * NST - 1, NST - 1, NT - 1)
            sums(B * NST - 1)
            for m in range(2):
                output(B - 1, m)


def build(nc, dram, out):
    ctx = ExitStack()
    with ctx:
        x = ctx.enter_context(nc.sbuf_tensor("x", [P, B * NT * D], f32))
        con = ctx.enter_context(nc.sbuf_tensor("con", [P, C_ODD + 3], f32))
        conb = ctx.enter_context(nc.sbuf_tensor("conb", [P, (2 + HPT) * P], bf16))
        psum = ctx.enter_context(nc.psum_tensor("psum", [P, 8 * 512], f32))
        ident = con[:, C_ID:C_ID + P]
        kept = []
        linear_attention(nc, kept, x, psum, con, conb, ident, dram)
        experts(nc, kept, "e0", x, psum, con, conb, dram, "f0", CH0, GROUP0, "r0", E0, "sel0", golden_route)
        nc.clear_and_free_semaphores(kept)
        nc.all_engine_barrier()
        kept = []
        rotary_attention(nc, kept, x, psum, con, conb, dram)
        experts(nc, kept, "e1", x, psum, con, conb, dram, "f1", CH1, GROUP1, "r1", E1, "sel1", top_route)
        stored = ctx.enter_context(nc.semaphore("stored"))
        with nc.Block() as block:
            @block.sync
            def _(sp):
                for b in range(B):
                    sp.dma_start(out[b].rearrange("(i p) d -> p i d", p=P),
                                 x[:, b * NT * D:(b + 1) * NT * D].rearrange("p (i d) -> p i d", i=NT)).then_inc(stored, 16)
                sp.wait_ge(stored, 16 * B)


def host_constants():
    p = np.arange(P)
    con = np.zeros((P, C_ODD + 3), np.float32)
    con[:, C_ID:C_ID + P] = np.eye(P)
    con[:, C_TRI:C_TRI + P] = p[:, None] <= p[None, :]
    con[:, C_AVG:C_AVG + P] = (p[:, None] // DV0 == p[None, :] // DV0) / DV0
    con[:, C_DIAG:C_DIAG + D] = p[:, None] // DK0 == np.arange(D)[None, :] // DV0
    con[:, C_RST:C_RST + T] = np.arange(T)[None, :] % P != 0
    con[:, C_EVEN] = ((p // DK0) % 2 == 0) * np.float32(DV0 ** -0.5)
    con[:, C_ODD] = ((p // DK0) % 2 == 1) * np.float32(DV0 ** -0.5)
    con[:, C_ODD + 1] = EPS
    rope = np.zeros((P, C_SEL + 16 * P), np.float32)
    i = p % HALF
    freq = (np.float32(10000.0) ** (i.astype(np.float32) * np.float32(-2.0 / DH1))).astype(np.float32)
    ang = (np.arange(T, dtype=np.float32)[None, :] * freq[:, None]).astype(np.float32)
    cos, sin = np.cos(ang), np.sin(ang)
    even = (i % 2 == 0)[:, None]
    rope[:, C_COS:C_COS + T] = np.where(even, cos, sin)
    rope[:, C_SIN:C_SIN + T] = np.where(even, -sin, cos)
    for t in range(NST):
        for which, parts in enumerate(((0, 0, 1, 1), (0, 1, 0, 1))):
            for part in range(2):
                m = np.zeros((P, P), np.float32)
                for hh in range(HPT):
                    for c in range(4):
                        if parts[c] == part:
                            for e in range(HALF):
                                m[HALF * (HPT * t + hh) + e, 32 * hh + 8 * c + e] = 1.0
                at = C_SEL + ((t * 2 + which) * 2 + part) * P
                rope[:, at:at + P] = m
    rope[:, C_SUM:C_SUM + P] = p[:, None] == p[None, :] // 32 * 32 + DH1
    rope[:, C_HEAD:C_HEAD + HPT] = p[:, None] // 32 == np.arange(HPT)
    conb = np.zeros((P, (2 + HPT) * P), np.float32)
    for h in range(HPT):
        conb[32 * h:32 * h + 3, (2 + h) * P:(3 + h) * P] = 1.0
    conb[:, 0:P] = np.eye(P)
    conb[:, P:2 * P] = np.where(p[None, :] > p[:, None], -BIG, 0.0)
    sel0 = np.zeros((WR, CH0, P), np.float32)
    sel1 = np.zeros((WR, CH1, P), np.float32)
    for sel, nch, e_n, f in ((sel0, CH0, E0, F0), (sel1, CH1, E1, F1)):
        for c in range(nch):
            for j in range(P):
                e = (c * P + j) // f
                if e < e_n:
                    for part in range(3):
                        sel[part * e_n + e, c, j] = 1.0
                elif e_n == E1 and c * P + j < E1 * F1 + SH1:
                    sel[3 * E1, c, j] = 1.0
    tie = np.zeros((P, E0 * E0 + E1 * E1 + G1 * G1), np.float32)
    at = 0
    for n in (E0, E1, G1):
        e = np.arange(n)
        tie[:, at:at + n * n] = (e[None, :] < e[:, None]).astype(np.float32).reshape(1, -1)
        at += n * n
    half = lambda c: (c.view(np.uint32) >> 16).astype(np.uint16)
    return {"con": con, "rope": rope, "conb": half(conb), "sel0": half(sel0), "sel1": half(sel1), "tie": tie}


def kernel(**inputs):
    import concourse.bacc as _bacc
    from concourse.bass_utils import run_bass_kernel_spmd as _run

    a = {k: np.asarray(v) for k, v in inputs.items()}
    by_rows = lambda w: np.ascontiguousarray(w.reshape(-1, P, w.shape[-1]).transpose(1, 0, 2))
    pad = lambda w, r, c: np.concatenate([np.concatenate([w, np.zeros((w.shape[0], c - w.shape[1]), w.dtype)], 1),
                                          np.zeros((r - w.shape[0], c), w.dtype)], 0)
    host = dict(host_constants())
    host["x"] = a["L0_attn_x"]
    host["w0"] = by_rows(np.concatenate([a["L0_attn_Wq"], a["L0_attn_Wk"], a["L0_attn_Wg"], pad(a["L0_attn_Wkg1"], D, P), a["L0_attn_Wv"]], 1))
    host["wr0"] = pad(a["L0_attn_Wkg2"], P, P)
    host["cols0"] = np.stack([a["L0_attn_bkg2"], a["L0_attn_bg"][:P], a["L0_attn_bg"][P:]], 1)
    host["wo0"] = by_rows(a["L0_attn_Wo"])

    def experts(gate, up, down, chunks):
        g = gate.reshape(KC, P, chunks, P).transpose(2, 1, 0, 3).reshape(chunks, P, KC * P)
        u = up.reshape(KC, P, chunks, P).transpose(2, 1, 0, 3).reshape(chunks, P, KC * P)
        return np.ascontiguousarray(np.concatenate([g, u, down.reshape(chunks, P, D)], 2))

    side = lambda w: w.transpose(1, 0, 2).reshape(D, -1)
    host["f0"] = experts(side(a["L0_ffn_Wg"]), side(a["L0_ffn_Wu"]), a["L0_ffn_Wd"].reshape(-1, D), CH0)
    n1 = CH1 * P
    host["f1"] = experts(pad(np.concatenate([side(a["L1_ffn_w1"]), a["L1_ffn_sw1"]], 1), D, n1),
                         pad(np.concatenate([side(a["L1_ffn_w3"]), a["L1_ffn_sw3"]], 1), D, n1),
                         pad(np.concatenate([a["L1_ffn_w2"].reshape(-1, D), a["L1_ffn_sw2"]], 0), n1, D), CH1)
    host["r0"] = by_rows(a["L0_ffn_Wr"])
    host["temp"] = a["L0_ffn_temperature"].reshape(1, 1)
    host["r1"] = by_rows(np.ascontiguousarray(a["L1_ffn_gate_w"].T))
    host["ebias"] = a["L1_ffn_expert_bias"].reshape(1, E1)
    even, odd = lambda w: w[..., 0::2], lambda w: w[..., 1::2]
    q, k = a["L1_attn_wq"], a["L1_attn_wk"]
    host["w1"] = by_rows(np.concatenate([even(q), odd(q), even(k), odd(k), a["L1_attn_wv"]], 1))
    bq, bk, rw = a["L1_attn_bq"], a["L1_attn_bk"], a["L1_attn_rms_w"]
    host["cols1"] = np.stack([even(bq), odd(bq), even(bk), odd(bk), rw[:P], rw[P:]], 1)
    host["rows1"] = np.stack([a["L1_attn_bv"], a["L1_attn_bo"]], 0).reshape(1, 2 * D)
    wo = a["L1_attn_wo"].reshape(NST, HPT, DH1, D)
    host["wo1"] = np.ascontiguousarray(np.concatenate([wo, np.zeros_like(wo)], 2).reshape(NST, P, D).transpose(1, 0, 2))

    nc = _bacc.Bacc("TRN2", target_bir_lowering=False, num_devices=1)
    arrays, dram = {}, {}
    for name, v in host.items():
        v = np.ascontiguousarray(v)
        arrays[f"in_{name}"] = v
        dram[name] = nc.dram_tensor(f"in_{name}", v.shape, mybir.dt.from_np(v.dtype), kind="ExternalInput").ap()
    out = nc.dram_tensor("out", (B, T, D), f32, kind="ExternalOutput").ap()
    build(nc, dram, out)
    r = _run(nc, [arrays], core_ids=[0])
    return r.results[0]["out"]
```

```python
import numpy as np
import concourse.bass as bass
from concourse import mybir
from contextlib import ExitStack

f32 = mybir.dt.float32
f32r = mybir.dt.float32r
bf16 = mybir.dt.bfloat16
u32 = mybir.dt.uint32
ALU = mybir.AluOpType
ACT = mybir.ActivationFunctionType
AX = mybir.AxisListType

P = 128
B, T, D = 4, 512, 256
KC = D // P
NT = T // P
EPS = 1e-5
LN_EXP_SET = "natural_log_exp_and_others"
H0, DK0, DV0 = 8, 16, 32
GATE_NORM = 16.0
H1, DH1 = 16, 16
HALF = DH1 // 2
HPT = P // 32
NST = H1 // HPT
E0, F0 = 8, 256
E1, F1, SH1 = 16, 176, 352
CH0 = E0 * F0 // P
CH1 = -(-(E1 * F1 + SH1) // P)
TOP0, TOP1, G1, TOPG1 = 2, 4, 4, 2
GROUP0, GROUP1 = 4, 5
WR = 128
CENTER = float(1.0 / np.e)
LOWER = float(np.float32(0.5 - np.log(4.0 / 3.0)))
UPPER = 0.5
BIG = 3.0e38

W0Q, W0K, W0G, W0R, W0V, W0N = 0, 128, 256, 512, 640, 896
W1QA, W1QB, W1KA, W1KB, W1V, W1N = 0, 128, 256, 384, 512, 768
C_ID, C_TRI, C_AVG, C_DIAG, C_RST, C_EVEN, C_ODD = 0, 128, 256, 384, 640, 1152, 1153
C_COS, C_SIN, C_SUM, C_HEAD, C_SEL = 0, 512, 1024, 1152, 1156


def mm3(pe, out, w_hi, w_lo, x_hi, x_lo, first, last):
    pe.matmul(out, w_hi, x_hi, start=first, stop=False, skip_group_check=True)
    pe.matmul(out, w_hi, x_lo, start=False, stop=False, skip_group_check=True)
    return pe.matmul(out, w_lo, x_hi, start=False, stop=last, skip_group_check=True)


def sems(nc, kept, prefix, names):
    named = {n: nc.alloc_semaphore(name=f"{prefix}_{n}") for n in names.split()}
    kept.extend(named.values())
    return named


def linear_attention(nc, kept, x, psum, con, conb, ident, dram):
    ctx = ExitStack()
    with ctx:
        def sb(name, shape, dt=f32):
            return ctx.enter_context(nc.sbuf_tensor(f"a0_{name}", shape, dt))

        s = sems(nc, kept, "a0", "x0_in x_in con_in w_in wo_in wr_in w_hi w_lo wo_hi wo_lo wr_hi wr_lo zeroed "
                 "stats moments var_eps ln_var rstd0 newton xhat xT_psum xT_hi xT_lo kg1_psum kg1_hi kg1_lo "
                 "q_psum k_psum kg2_psum v_psum g_psum gate_abs gate_min gate_exp gate_ln gate_log gate_cum "
                 "gate_last decay_q decay_k decay_end qd kn kdT kd_psum kd v_sb silu_g at_psum at_sb kv_psum "
                 "kv_sb state ot_psum o_sb mean_psum centered sq var_psum o_ln o_rstd c_gated y y_hi y_lo "
                 "wo_psum x_out")
        w_raw, w_hi, w_lo = sb("w_raw", [P, KC, W0N]), sb("w_hi", [P, KC, W0N], f32r), sb("w_lo", [P, KC, W0N], f32r)
        wo_raw, wo_hi, wo_lo = sb("wo_raw", [P, KC, D]), sb("wo_hi", [P, KC, D], f32r), sb("wo_lo", [P, KC, D], f32r)
        wr_raw, wr_hi, wr_lo = sb("wr_raw", [P, P]), sb("wr_hi", [P, P], f32r), sb("wr_lo", [P, P], f32r)
        cols = sb("cols", [P, 3])
        st, mv = sb("st", [P, NT, 6]), sb("mv", [P, NT, 2])
        ve, lnv, r0, n1, n2, rstd = (sb(n, [P, NT]) for n in ("ve", "lnv", "r0", "n1", "n2", "rstd"))
        held = sb("held", [P, 4])
        xhat = sb("xhat", [P, NT, D])
        xT_hi, xT_lo = sb("xT_hi", [P, KC, T], f32r), sb("xT_lo", [P, KC, T], f32r)
        kg1_hi, kg1_lo = sb("kg1_hi", [P, T], f32r), sb("kg1_lo", [P, T], f32r)
        g_abs, g_min, g_exp, g_ln, g_log, g_cum = (sb(n, [P, T]) for n in ("g_abs", "g_min", "g_exp", "g_ln", "g_log", "g_cum"))
        g_last = sb("g_last", [P, NT])
        dq, dk, de = sb("dq", [P, T]), sb("dk", [P, T]), sb("de", [P, T])
        qd, kne, kno, kdT = (sb(n, [P, T]) for n in ("qd", "kne", "kno", "kdT"))
        kd = sb("kd", [P, NT, P])
        v_sb = sb("v_sb", [P, NT, D])
        sg = sb("sg", [P, KC, T])
        at = [sb(f"at{i}", [P, 16, P]) for i in range(2)]
        kv = [sb(f"kv{i}", [P, D]) for i in range(3)]
        stt = [kv[0], sb("state2", [P, D]), sb("state3", [P, D])]
        o_sb, cen, sq, lv, rs, y = (sb(n, [P, KC, T]) for n in ("o_sb", "cen", "sq", "lv", "rs", "y"))
        y_hi, y_lo = sb("y_hi", [P, KC, T], f32r), sb("y_lo", [P, KC, T], f32r)
        tri = con[:, C_TRI:C_TRI + P]
        avg = con[:, C_AVG:C_AVG + P]
        diag = con[:, C_DIAG:C_DIAG + D]
        rst = con[:, C_RST:C_RST + T]
        eps_col = con[:, C_ODD + 1:C_ODD + 2]
        bank = lambda i, n=1: psum[:, 512 * i:512 * (i + n)]
        xb = lambda b, at=0, m=NT * D: (x[:, b * NT * D + at:b * NT * D + at + m] if isinstance(b, int)
                                        else x[:, bass.ds(b * NT * D + at, m)])

        def hold(dve, place):
            dve.tensor_copy(held[:, place:place + 1], con[:, 0:1])

        block = ctx.enter_context(nc.Block())

        @block.sync
        def _(sp):
            for b in range(B):
                sp.dma_start(x[:, b * NT * D:(b + 1) * NT * D].rearrange("p (i d) -> p i d", i=NT),
                             dram["x"][b].rearrange("(i p) d -> p i d", p=P)).then_inc(s["x0_in" if b == 0 else "x_in"], 16)
                if b == 0:
                    sp.dma_start(con[:, :], dram["con"]).then_inc(s["con_in"], 16)
                    sp.dma_start(conb[:, :], dram["conb"].bitcast(bf16)).then_inc(s["con_in"], 16)
                    sp.dma_start(wr_raw[:, :], dram["wr0"]).then_inc(s["wr_in"], 16)
                    sp.dma_start(cols[:, :], dram["cols0"]).then_inc(s["wr_in"], 16)
                    sp.dma_start(w_raw[:, :, :], dram["w0"]).then_inc(s["w_in"], 16)
            sp.dma_start(wo_raw[:, :, :], dram["wo0"]).then_inc(s["wo_in"], 16)

        @block.gpsimd
        def _(pool):
            def split(raw, hi, lo, came, n, s_hi, s_lo):
                pool.wait_ge(s[came], n)
                if came != "w_in":
                    pool.tensor_copy(hi[:], raw[:]).then_inc(s[s_hi], 1)
                pool.wait_ge(s[s_hi], 1)
                pool.tensor_tensor(lo[:], raw[:], hi[:].bitcast(f32), ALU.subtract).then_inc(s[s_lo], 1)

            split(wr_raw, wr_hi, wr_lo, "wr_in", 32, "wr_hi", "wr_lo")
            split(w_raw, w_hi, w_lo, "w_in", 16, "w_hi", "w_lo")
            for t in (at[0][:, :, :], at[1][:, :, :], kv[0][:, :], kv[1][:, :], kv[2][:, :]):
                pool.memset(t, 0.0).then_inc(s["zeroed"], 1)
            split(wo_raw, wo_hi, wo_lo, "wo_in", 16, "wo_hi", "wo_lo")

        @block.scalar
        def _(act):
            act.preload_act_table_set(LN_EXP_SET)

            def guess(f):
                act.wait_ge(s["var_eps"], f + 1)
                act.activation(lnv[:, :], ve[:, :], ACT.Ln).then_inc(s["ln_var"], 1)
                act.wait_ge(s["ln_var"], f + 1)
                act.activation(r0[:, :], lnv[:, :], ACT.Exp, scale=-0.5).then_inc(s["rstd0"], 1)

            def turned(f):
                act.wait_ge(s["xT_psum"], f + 1)
                act.activation(xT_hi[:, :, :], bank(0, 2).rearrange("p (k t) -> p k t", k=KC), ACT.Copy).then_inc(s["xT_hi"], 1)

            def low_rank(f):
                act.wait_ge(s["kg1_psum"], f + 1)
                act.activation(kg1_hi[:, :], bank(6), ACT.Copy).then_inc(s["kg1_hi"], 1)

            def decays(f):
                act.wait_ge(s["gate_min"], f + 1)
                act.activation(g_abs[:, :], bank(7), ACT.Abs, bias=cols[:, 0:1]).then_inc(s["gate_abs"], 1)
                act.wait_ge(s["gate_abs"], f + 1)
                act.activation(g_exp[:, :], g_abs[:, :], ACT.Exp, scale=-1.0).then_inc(s["gate_exp"], 1)
                act.wait_ge(s["gate_exp"], f + 1)
                act.activation(g_ln[:, :], g_exp[:, :], ACT.Ln, bias=1.0).then_inc(s["gate_ln"], 1)
                act.wait_ge(s["gate_cum"], f + 1)
                act.activation(dq[:, :], g_cum[:, :], ACT.Exp, scale=1.0 / GATE_NORM).then_inc(s["decay_q"], 1)
                act.activation(dk[:, :], g_cum[:, :], ACT.Exp, scale=-1.0 / GATE_NORM).then_inc(s["decay_k"], 1)
                act.wait_ge(s["gate_last"], f + 1)
                for n in range(NT):
                    last = act.activation(de[:, n * P:(n + 1) * P], g_cum[:, n * P:(n + 1) * P], ACT.Exp,
                                          bias=g_last[:, n:n + 1], scale=-1.0 / GATE_NORM)
                last.then_inc(s["decay_end"], 1)

            def values_and_gate(f):
                act.wait_ge(s["v_psum"], f + 1)
                act.activation(v_sb[:, :, :], bank(0, 2).rearrange("p (i d) -> p i d", i=NT), ACT.Copy).then_inc(s["v_sb"], 1)
                act.wait_ge(s["g_psum"], f + 1)
                for h in range(KC):
                    last = act.activation(sg[:, h, :], bank(4 + h), ACT.Silu, bias=cols[:, 1 + h:2 + h])
                last.then_inc(s["silu_g"], 1)
                act.preload_act_table_set(LN_EXP_SET)
                act.wait_ge(s["kd_psum"], f + 1)
                act.activation(kd[:, :, :], bank(6).rearrange("p (i d) -> p i d", i=NT), ACT.Copy).then_inc(s["kd"], 1)

            def turn(b, ahead):
                f = b + 1
                if ahead:
                    guess(f)
                act.wait_ge(s["ot_psum"], b + 1)
                act.activation(o_sb[:, :, :], bank(0, 2).rearrange("p (k t) -> p k t", k=KC), ACT.Copy).then_inc(s["o_sb"], 1)
                act.wait_ge(s["centered"], b + 1)
                act.activation(sq[:, :, :], cen[:, :, :], ACT.Square).then_inc(s["sq"], 1)
                if ahead:
                    turned(f)
                act.wait_ge(s["var_psum"], b + 1)
                act.activation(lv[:, :, :], bank(4, 2).rearrange("p (k t) -> p k t", k=KC), ACT.Ln, bias=eps_col).then_inc(s["o_ln"], 1)
                act.wait_ge(s["o_ln"], b + 1)
                act.activation(rs[:, :, :], lv[:, :, :], ACT.Exp, scale=-0.5).then_inc(s["o_rstd"], 1)
                if ahead:
                    low_rank(f)
                act.wait_ge(s["y"], b + 1)
                act.activation(y_hi[:, :, :], y[:, :, :], ACT.Copy).then_inc(s["y_hi"], 1)
                if ahead:
                    decays(f)
                    values_and_gate(f)

            guess(0)
            act.wait_ge(s["w_in"], 16)
            act.activation(w_hi[:, :, :], w_raw[:, :, :], ACT.Copy).then_inc(s["w_hi"], 1)
            turned(0)
            low_rank(0)
            act.wait_ge(s["wr_in"], 32)
            decays(0)
            values_and_gate(0)
            with act.Fori(0, B - 1) as b:
                turn(b, True)
            turn(B - 1, False)

        @block.vector
        def _(dve):
            dve.wait_ge(s["x0_in"], 16)

            def normal(f):
                for i in range(NT):
                    last = dve.bn_stats(st[:, i, :], xb(f, i * D, D))
                last.then_inc(s["stats"], 1)
                if isinstance(f, int) and f == 0:
                    dve.wait_ge(s["con_in"], 32)
                dve.wait_ge(s["stats"], f + 1)
                hold(dve, 0)
                for i in range(NT):
                    last = dve.bn_aggr(mv[:, i, :], st[:, i, :])
                last.then_inc(s["moments"], 1)
                dve.wait_ge(s["moments"], f + 1)
                dve.tensor_scalar(ve[:, :], mv[:, :, 1], EPS, None, ALU.add).then_inc(s["var_eps"], 1)
                dve.wait_ge(s["rstd0"], f + 1)
                dve.scalar_tensor_tensor(n1[:, :], r0[:, :], -0.5, r0[:, :], ALU.mult, ALU.mult).then_inc(s["newton"], 1)
                dve.wait_ge(s["newton"], 3 * f + 1)
                dve.tensor_tensor(n2[:, :], n1[:, :], ve[:, :], ALU.mult).then_inc(s["newton"], 1)
                dve.wait_ge(s["newton"], 3 * f + 2)
                dve.scalar_tensor_tensor(rstd[:, :], n2[:, :], 1.5, r0[:, :], ALU.add, ALU.mult).then_inc(s["newton"], 1)
                dve.wait_ge(s["newton"], 3 * f + 3)
                for i in range(NT):
                    last = dve.tensor_scalar(xhat[:, i, :], xb(f, i * D, D), mv[:, i, 0:1],
                                             rstd[:, i:i + 1], ALU.subtract, ALU.mult)
                last.then_inc(s["xhat"], 1)

            def turned(f):
                dve.wait_ge(s["xT_hi"], f + 1)
                dve.tensor_tensor(xT_lo[:, :, :], bank(0, 2).rearrange("p (k t) -> p k t", k=KC),
                                  xT_hi[:, :, :].bitcast(f32), ALU.subtract).then_inc(s["xT_lo"], 1)

            def low_rank(f):
                dve.wait_ge(s["kg1_hi"], f + 1)
                dve.tensor_tensor(kg1_lo[:, :], bank(6), kg1_hi[:, :].bitcast(f32), ALU.subtract).then_inc(s["kg1_lo"], 1)

            def gate_min(f):
                dve.wait_ge(s["kg2_psum"], f + 1)
                dve.tensor_scalar(g_min[:, :], bank(7), cols[:, 0:1], 0.0, ALU.add, ALU.min).then_inc(s["gate_min"], 1)

            def decays(f):
                dve.wait_ge(s["gate_ln"], f + 1)
                dve.wait_ge(s["gate_min"], f + 1)
                dve.tensor_tensor(g_log[:, :], g_min[:, :], g_ln[:, :], ALU.subtract).then_inc(s["gate_log"], 1)
                dve.wait_ge(s["gate_log"], f + 1)
                dve.tensor_tensor_scan(g_cum[:, :], rst, g_log[:, :], 0.0, ALU.mult, ALU.add).then_inc(s["gate_cum"], 1)
                dve.wait_ge(s["gate_cum"], f + 1)
                dve.tensor_scalar(g_last[:, :], g_cum[:, P - 1::P], 1.0 / GATE_NORM, None, ALU.mult).then_inc(s["gate_last"], 1)

            def decayed(f):
                dve.wait_ge(s["decay_q"], f + 1)
                dve.wait_ge(s["q_psum"], f + 1)
                dve.tensor_tensor(qd[:, :], bank(2), dq[:, :], ALU.mult).then_inc(s["qd"], 1)
                dve.wait_ge(s["decay_k"], f + 1)
                dve.wait_ge(s["k_psum"], f + 1)
                dve.scalar_tensor_tensor(kne[:, :], bank(3), con[:, C_EVEN:C_EVEN + 1], dk[:, :], ALU.mult, ALU.mult).then_inc(s["kn"], 1)
                dve.scalar_tensor_tensor(kno[:, :], bank(3), con[:, C_ODD:C_ODD + 1], dk[:, :], ALU.mult, ALU.mult).then_inc(s["kn"], 1)
                dve.wait_ge(s["decay_end"], f + 1)
                dve.scalar_tensor_tensor(kdT[:, :], bank(3), float(DV0) ** -0.5, de[:, :], ALU.mult, ALU.mult).then_inc(s["kdT"], 1)

            def turn(b, ahead):
                f = b + 1

                def masked(r):
                    dve.wait_ge(s["at_psum"], 2 * b + r + 1)
                    hold(dve, 1 + r)
                    dve.copy_predicated(at[r][:, :, :], tri.unsqueeze(1).broadcast_to([P, 16, P]).bitcast(u32),
                                        bank(2, 4).rearrange("p (a t) -> p a t", t=P)).then_inc(s["at_sb"], 1)

                masked(0)
                dve.wait_ge(s["kv_psum"], b + 1)
                hold(dve, 3)
                for n in range(3):
                    last = dve.copy_predicated(kv[n][:, :], diag.bitcast(u32), (bank(7)[:, n * D:(n + 1) * D] if n < 2 else bank(6)[:, 0:D]))
                    last.then_inc(s["kv_sb"], 1)
                dve.wait_ge(s["kv_sb"], 3 * b + 3)
                dve.scalar_tensor_tensor(stt[1][:, :], stt[0][:, :], dq[:, 2 * P - 1:2 * P], kv[1][:, :], ALU.mult, ALU.add).then_inc(s["state"], 1)
                dve.wait_ge(s["state"], 2 * b + 1)
                dve.scalar_tensor_tensor(stt[2][:, :], stt[1][:, :], dq[:, 3 * P - 1:3 * P], kv[2][:, :], ALU.mult, ALU.add).then_inc(s["state"], 1)
                masked(1)
                if ahead:
                    normal(f)
                dve.wait_ge(s["mean_psum"], b + 1)
                dve.tensor_tensor(cen[:, :, :], o_sb[:, :, :], bank(2, 2).rearrange("p (k t) -> p k t", k=KC), ALU.subtract).then_inc(s["centered"], 1)
                dve.wait_ge(s["centered"], b + 1)
                dve.wait_ge(s["silu_g"], b + 1)
                dve.tensor_tensor(sg[:, :, :], cen[:, :, :], sg[:, :, :], ALU.mult).then_inc(s["c_gated"], 1)
                if ahead:
                    turned(f)
                dve.wait_ge(s["c_gated"], b + 1)
                dve.wait_ge(s["o_rstd"], b + 1)
                dve.tensor_tensor(y[:, :, :], sg[:, :, :], rs[:, :, :], ALU.mult).then_inc(s["y"], 1)
                if ahead:
                    low_rank(f)
                dve.wait_ge(s["y_hi"], b + 1)
                dve.tensor_tensor(y_lo[:, :, :], y[:, :, :], y_hi[:, :, :].bitcast(f32), ALU.subtract).then_inc(s["y_lo"], 1)
                if ahead:
                    gate_min(f)
                    decays(f)
                dve.wait_ge(s["wo_psum"], b + 1)
                dve.tensor_tensor(xb(b), xb(b), bank(4, 2), ALU.add).then_inc(s["x_out"], 1)
                if ahead:
                    decayed(f)

            normal(0)
            turned(0)
            low_rank(0)
            dve.wait_ge(s["wr_in"], 32)
            gate_min(0)
            decays(0)
            decayed(0)
            dve.wait_ge(s["zeroed"], 5)
            dve.wait_ge(s["x_in"], 16 * (B - 1))
            with dve.Fori(0, B - 1) as b:
                turn(b, True)
            turn(B - 1, False)

        @block.tensor
        def _(pe):
            pe.wait_ge(s["con_in"], 32)

            def project(out, col):
                for k in range(KC):
                    last = mm3(pe, out, w_hi[:, k, col:col + P], w_lo[:, k, col:col + P], xT_hi[:, k, :], xT_lo[:, k, :], k == 0, k == KC - 1)
                return last

            def turned(f):
                pe.wait_ge(s["xhat"], f + 1)
                for i in range(NT):
                    for k in range(KC):
                        last = pe.transpose(bank(k)[:, i * P:(i + 1) * P], xhat[:, i, k * P:(k + 1) * P], ident)
                last.then_inc(s["xT_psum"], 1)

            def qk(f):
                pe.wait_ge(s["xT_lo"], f + 1)
                pe.wait_ge(s["w_lo"], 1)
                project(bank(6), W0R).then_inc(s["kg1_psum"], 1)
                project(bank(2), W0Q).then_inc(s["q_psum"], 1)
                project(bank(3), W0K).then_inc(s["k_psum"], 1)
                pe.wait_ge(s["kg1_lo"], f + 1)
                pe.wait_ge(s["wr_lo"], 1)
                mm3(pe, bank(7), wr_hi[:, :], wr_lo[:, :], kg1_hi[:, :], kg1_lo[:, :], True, True).then_inc(s["kg2_psum"], 1)

            def values(f):
                for i in range(NT):
                    for k in range(KC):
                        tt = slice(i * P, (i + 1) * P)
                        last = mm3(pe, bank(i // 2)[:, (i % 2) * D:(i % 2 + 1) * D], xT_hi[:, k, tt], xT_lo[:, k, tt],
                                   w_hi[:, k, W0V:W0V + D], w_lo[:, k, W0V:W0V + D], k == 0, k == KC - 1)
                last.then_inc(s["v_psum"], 1)

            def gate(f):
                project(bank(4), W0G)
                project(bank(5), W0G + P).then_inc(s["g_psum"], 1)

            def turn(b, ahead):
                f = b + 1
                pe.wait_ge(s["kdT"], b + 1)
                for n in range(NT):
                    last = pe.transpose(bank(6)[:, n * P:(n + 1) * P], kdT[:, n * P:(n + 1) * P], ident)
                last.then_inc(s["kd_psum"], 1)
                pe.wait_ge(s["kn"], 2 * b + 2)
                pe.wait_ge(s["qd"], b + 1)
                pe.wait_ge(s["silu_g"], b + 1)

                def scores(r):
                    for n in (2 * r, 2 * r + 1):
                        for par in range(2):
                            for pr in range(4):
                                row = slice(32 * pr, 32 * pr + 32)
                                col = ((n % 2) * 2 + par) * P
                                last = pe.matmul(bank(2 + pr)[:, col:col + P], (kne, kno)[par][row, n * P:(n + 1) * P],
                                                 qd[row, n * P:(n + 1) * P], start=True, stop=True, tile_position=(32 * pr, 0),
                                                 skip_group_check=True)
                    last.then_inc(s["at_psum"], 1)

                scores(0)
                pe.wait_ge(s["kd"], b + 1)
                pe.wait_ge(s["v_sb"], b + 1)
                for n in range(3):
                    last = pe.matmul(bank(7)[:, n * D:(n + 1) * D] if n < 2 else bank(6)[:, 0:D], kd[:, n, :], v_sb[:, n, :],
                                     start=True, stop=True, skip_group_check=True)
                last.then_inc(s["kv_psum"], 1)
                for n in range(NT):
                    if n == 0:
                        pe.wait_ge(s["at_sb"], 2 * b + 1)
                        scores(1)
                    if n == 2:
                        pe.wait_ge(s["at_sb"], 2 * b + 2)
                    if n > 0:
                        if n == 1:
                            pe.wait_ge(s["kv_sb"], 3 * b + 3)
                        else:
                            pe.wait_ge(s["state"], 2 * b + n - 1)
                        for h in range(KC):
                            pe.matmul(bank(h)[:, n * P:(n + 1) * P], stt[n - 1][:, h * P:(h + 1) * P], qd[:, n * P:(n + 1) * P],
                                      start=True, stop=False, skip_group_check=True)
                    for h in range(H0):
                        q = 32 * (h % 4)
                        last = pe.matmul(bank(h // 4)[q:q + 32, n * P:(n + 1) * P], v_sb[:, n, h * DV0:(h + 1) * DV0],
                                         at[n // 2][:, (h // 2) * 4 + (n % 2) * 2 + h % 2, :], start=(n == 0), stop=True,
                                         tile_position=(0, q), skip_group_check=True)
                last.then_inc(s["ot_psum"], 1)
                pe.wait_ge(s["o_sb"], b + 1)
                for h in range(KC):
                    last = pe.matmul(bank(2 + h), avg, o_sb[:, h, :], start=True, stop=True)
                last.then_inc(s["mean_psum"], 1)
                if ahead:
                    turned(f)
                pe.wait_ge(s["sq"], b + 1)
                for h in range(KC):
                    last = pe.matmul(bank(4 + h), avg, sq[:, h, :], start=True, stop=True)
                last.then_inc(s["var_psum"], 1)
                if ahead:
                    qk(f)
                    values(f)
                pe.wait_ge(s["y_lo"], b + 1)
                pe.wait_ge(s["wo_lo"], 1)
                for i in range(NT):
                    for k in range(KC):
                        tt = slice(i * P, (i + 1) * P)
                        last = mm3(pe, bank(4 + i // 2)[:, (i % 2) * D:(i % 2 + 1) * D], y_hi[:, k, tt], y_lo[:, k, tt],
                                   wo_hi[:, k, :], wo_lo[:, k, :], k == 0, k == KC - 1)
                last.then_inc(s["wo_psum"], 1)
                if ahead:
                    pe.wait_ge(s["x_out"], b + 1)
                    gate(f)

            turned(0)
            qk(0)
            values(0)
            gate(0)
            with pe.Fori(0, B - 1) as b:
                turn(b, True)
            turn(B - 1, False)


class Chain:

    def __init__(self, engine, sem):
        self.engine, self.sem, self.n = engine, sem, 0

    def __call__(self, ins):
        self.n += 1
        ins.then_inc(self.sem, 1)
        self.engine.wait_ge(self.sem, self.n)

    def beside(self, ins):
        self.n += 1
        ins.then_inc(self.sem, 1)


def experts(nc, kept, tag, x, psum, con, conb, dram, weights, chunks, group, router, n_exp, sel_name, route_weights):
    groups = chunks // group
    per_group = B * group
    n = B * NT
    ctx = ExitStack()
    with ctx:
        def sb(name, shape, dt=f32):
            return ctx.enter_context(nc.sbuf_tensor(f"{tag}_{name}", shape, dt))

        s = sems(nc, kept, tag, "small_in stats moments var_eps chain ln_var rstd0 xhat xT_psum xT_hi xT_lo r_hi r_lo logits "
                 "z inh dist w0 fb wx wT_psum wT split_hi split_lo gate_psum up_psum spread_psum silu gated scaled h_hi h_lo down y_added")
        raw_in = list(sems(nc, kept, tag, " ".join(f"raw_in{c}" for c in range(group))).values())
        WN = 2 * KC * P + D
        raw, w_hi, w_lo = sb("raw", [P, group, WN]), sb("w_hi", [P, group, WN], f32r), sb("w_lo", [P, group, WN], f32r)
        sel = sb("sel", [WR, chunks * P], bf16)
        r_raw, r_hi, r_lo = sb("r_raw", [P, KC, n_exp]), sb("r_hi", [P, KC, n_exp], f32r), sb("r_lo", [P, KC, n_exp], f32r)
        st, mv = sb("st", [P, n, 6]), sb("mv", [P, n, 2])
        ve, lnv, r0, n1, n2, rstd = (sb(k, [P, n]) for k in ("ve", "lnv", "r0", "n1", "n2", "rstd"))
        xT_hi, xT_lo = sb("xT_hi", [P, KC, B * T], f32r), sb("xT_lo", [P, KC, B * T], f32r)
        wx, wT = sb("wx", [P, NT, WR], bf16), sb("wT", [WR, B * T], bf16)
        sil, gat, h = ([sb(f"{k}{i}", [P, T]) for i in range(2)] for k in ("sil", "gat", "h"))
        h_hi, h_lo = ([sb(f"{k}{i}", [P, T], f32r) for i in range(2)] for k in ("h_hi", "h_lo"))
        side = sb("side", [P, E1 + E0 * E0 + E1 * E1 + G1 * G1])
        bank = lambda i, m=1: psum[:, 512 * i:512 * (i + m)]
        ident = con[:, C_ID:C_ID + P]
        zero = con[:, C_ODD + 2:C_ODD + 3]
        xhat = [sb(f"xhat{i}", [P, NT, D]) for i in range(2)]
        routing = route_weights(sb, s)
        lag = 1 if "groups" in routing else 0
        logits_read = "z" if n_exp == E0 else "inh"
        front_bank = lambda f, k: bank(7 if f else 6 + k)
        block = ctx.enter_context(nc.Block())

        @block.sync
        def _(sp):
            sp.dma_start(r_raw[:, :, :], dram[router]).then_inc(s["small_in"], 16)
            if n_exp == E0:
                sp.dma_start(side[:, 0:1], dram["temp"].broadcast_to([P, 1])).then_inc(s["small_in"], 16)
            else:
                sp.dma_start(side[:, 0:E1], dram["ebias"].broadcast_to([P, E1])).then_inc(s["small_in"], 16)
            sp.dma_start(side[:, E1:], dram["tie"]).then_inc(s["small_in"], 16)
            sp.dma_start(sel[:, :], dram[sel_name].rearrange("r c p -> r (c p)").bitcast(bf16)).then_inc(s["small_in"], 16)

            for c in range(group):
                sp.dma_start(raw[:, c, :], dram[weights][c]).then_inc(raw_in[c], 16)
            with sp.Fori(1, groups) as g:
                for c in range(group):
                    sp.wait_ge(s["split_lo"], (g - 1) * group + c + 1)
                    sp.dma_start(raw[:, c, :], dram[weights][bass.ds(g * group + c, 1), :, :].rearrange("a p n -> (a p) n")).then_inc(raw_in[c], 16)

        @block.gpsimd
        def _(pool):
            pool.wait_ge(s["small_in"], 64)
            pool.tensor_copy(r_hi[:, :, :], r_raw[:, :, :]).then_inc(s["r_hi"], 1)
            pool.wait_ge(s["r_hi"], 1)
            pool.tensor_tensor(r_lo[:, :, :], r_raw[:, :, :], r_hi[:, :, :].bitcast(f32), ALU.subtract).then_inc(s["r_lo"], 1)

            def split_chunk(g, c, first):
                k = g * group + c
                pool.wait_ge(raw_in[c], (g + 1) * 16)
                if not first:
                    pool.wait_ge(s["down"], (g - 1) * per_group + (B - 1) * group + c + 1)
                pool.tensor_tensor(w_hi[:, c, :], raw[:, c, :], zero.broadcast_to([P, WN]), ALU.add).then_inc(s["split_hi"], 1)
                pool.wait_ge(s["split_hi"], k + 1)
                pool.tensor_tensor(w_lo[:, c, :], raw[:, c, :], w_hi[:, c, :].bitcast(f32), ALU.subtract).then_inc(s["split_lo"], 1)

            for c in range(group):
                split_chunk(0, c, True)
            with pool.Fori(1, groups) as g:
                for c in range(group):
                    split_chunk(g, c, False)

        @block.scalar
        def _(act):
            def guess(f):
                nt = slice(f * NT, (f + 1) * NT)
                act.preload_act_table_set(LN_EXP_SET)
                act.wait_ge(s["var_eps"], f + 1)
                act.activation(lnv[:, nt], ve[:, nt], ACT.Ln).then_inc(s["ln_var"], 1)
                act.wait_ge(s["ln_var"], f + 1)
                act.activation(r0[:, nt], lnv[:, nt], ACT.Exp, scale=-0.5).then_inc(s["rstd0"], 1)

            def turned(f, k):
                act.wait_ge(s["xT_psum"], KC * f + k + 1)
                act.activation(xT_hi[:, k, f * T:(f + 1) * T], front_bank(f, k), ACT.Copy).then_inc(s["xT_hi"], 1)

            def weights_turned(f):
                act.wait_ge(s["wT_psum"], f + 1)
                act.activation(wT[:, f * T:(f + 1) * T], bank(7)[0:WR, :].bitcast(bf16)[:, 0:T], ACT.Copy).then_inc(s["wT"], 1)

            def pieces(b, c):
                if c == 0 and b + 1 < B:
                    routing["scalar"](act, bank(7)[:, 0:NT * n_exp], b + 1)
                if c in (1, 2) and b + 2 < B:
                    turned(b + 2, c - 1)
                if c == 3 + lag and b + 1 < B:
                    weights_turned(b + 1)

            def unit(u, i, first):
                q = i % 2
                act.wait_ge(s["gate_psum"], u + 1)
                if not (first and i < 2):
                    act.wait_ge(s["gated"], u - 1)
                act.activation(sil[q][:, :], bank(2 + q), ACT.Silu).then_inc(s["silu"], 1)
                act.wait_ge(s["scaled"], u + 1)
                if not (first and i < 2):
                    act.wait_ge(s["down"], u - 1)
                act.activation(h_hi[q][:, :], h[q][:, :], ACT.Copy).then_inc(s["h_hi"], 1)

            guess(0)
            guess(1)
            for k in range(KC):
                turned(0, k)
            routing["scalar"](act, bank(7)[:, 0:NT * n_exp], 0)
            for k in range(KC):
                turned(1, k)
            weights_turned(0)
            for f in range(2, B):
                guess(f)
            for i in range(per_group):
                unit(i, i, True)
                pieces(i // group, i % group)
            with act.Fori(1, groups) as g:
                for i in range(per_group):
                    unit(g * per_group + i, i, False)

        @block.vector
        def _(dve):
            step = Chain(dve, s["chain"])

            def moments(f):
                nt = slice(f * NT, (f + 1) * NT)
                for i in range(f * NT, (f + 1) * NT):
                    last = dve.bn_stats(st[:, i, :], x[:, i * D:(i + 1) * D])
                last.then_inc(s["stats"], 1)
                dve.wait_ge(s["stats"], f + 1)
                for i in range(f * NT, (f + 1) * NT):
                    last = dve.bn_aggr(mv[:, i, :], st[:, i, :])
                last.then_inc(s["moments"], 1)
                dve.wait_ge(s["moments"], f + 1)
                dve.tensor_scalar(ve[:, nt], mv[:, nt, 1], EPS, None, ALU.add).then_inc(s["var_eps"], 1)

            def normal(f):
                nt = slice(f * NT, (f + 1) * NT)
                dve.wait_ge(s["rstd0"], f + 1)
                step(dve.scalar_tensor_tensor(n1[:, nt], r0[:, nt], -0.5, r0[:, nt], ALU.mult, ALU.mult))
                step(dve.tensor_tensor(n2[:, nt], n1[:, nt], ve[:, nt], ALU.mult))
                step(dve.scalar_tensor_tensor(rstd[:, nt], n2[:, nt], 1.5, r0[:, nt], ALU.add, ALU.mult))
                if f >= 2:
                    dve.wait_ge(s["xT_psum"], KC * (f - 1))
                for i in range(NT):
                    j = f * NT + i
                    last = dve.tensor_scalar(xhat[f % 2][:, i, :], x[:, j * D:(j + 1) * D], mv[:, j, 0:1], rstd[:, j:j + 1], ALU.subtract, ALU.mult)
                last.then_inc(s["xhat"], 1)

            def turned(f, k):
                dve.wait_ge(s["xT_hi"], KC * f + k + 1)
                tt = slice(f * T, (f + 1) * T)
                dve.tensor_tensor(xT_lo[:, k, tt], front_bank(f, k), xT_hi[:, k, tt].bitcast(f32), ALU.subtract).then_inc(s["xT_lo"], 1)

            def split_weights(f, w):
                parts = [wx[:, :, k * n_exp:(k + 1) * n_exp] for k in range(3)]
                rest = (routing["rest0"], routing["rest1"])
                if f > 0:
                    dve.wait_ge(s["wT_psum"], f)
                step(dve.tensor_copy(parts[0], w))
                step(dve.tensor_tensor(rest[0][:, :, :], w, parts[0], ALU.subtract))
                step(dve.tensor_copy(parts[1], rest[0][:, :, :]))
                step(dve.tensor_tensor(rest[1][:, :, :], rest[0][:, :, :], parts[1], ALU.subtract))
                dve.tensor_copy(parts[2], rest[1][:, :, :]).then_inc(s["wx"], 1)
                dve.wait_ge(s["wx"], f + 1)

            def pieces(b, c):
                if b + 1 < B:
                    if c == 0 and lag:
                        routing["groups"](dve, step, side, b + 1)
                    if c == lag:
                        routing["ranks"](dve, step, bank(7)[:, 0:NT * n_exp], side, b + 1)
                    if c == 1 + lag:
                        routed[b + 1] = routing["weights"](dve, step, b + 1)
                    if c == 2 + lag:
                        split_weights(b + 1, routed[b + 1])
                if b + 2 < B and c in (1, 2):
                    turned(b + 2, c - 1)
                if b + 3 < B and c == 3:
                    normal(b + 3)

            routed = {}
            step(dve.memset(wx[:, :, 3 * n_exp:], 0.0))
            if n_exp == E1:
                step(dve.memset(wx[:, :, 3 * E1:3 * E1 + 1], 1.0))
            moments(0)
            normal(0)
            moments(1)
            for k in range(KC):
                turned(0, k)
            normal(1)
            dve.wait_ge(s["small_in"], 64)
            if lag:
                routing["groups"](dve, step, side, 0)
            routing["ranks"](dve, step, bank(7)[:, 0:NT * n_exp], side, 0)
            for k in range(KC):
                turned(1, k)
            split_weights(0, routing["weights"](dve, step, 0))
            for f in range(2, B):
                moments(f)
            normal(2)

            def unit(u, i, first):
                q = i % 2
                dve.wait_ge(s["up_psum"], u + 1)
                dve.wait_ge(s["silu"], u + 1)
                dve.tensor_tensor(gat[q][:, :], bank(4 + q), sil[q][:, :], ALU.mult).then_inc(s["gated"], 1)
                if not (first and i < 2):
                    dve.wait_ge(s["h_lo"], u - 1)
                dve.wait_ge(s["gated"], u + 1)
                dve.wait_ge(s["spread_psum"], u + 1)
                dve.tensor_tensor(h[q][:, :], bank(6 + (0 if first else q)), gat[q][:, :], ALU.mult).then_inc(s["scaled"], 1)
                dve.wait_ge(s["h_hi"], u + 1)
                dve.tensor_tensor(h_lo[q][:, :], h[q][:, :], h_hi[q][:, :].bitcast(f32), ALU.subtract).then_inc(s["h_lo"], 1)

            def gather(y, b):
                dve.wait_ge(s["down"], (y + 1) * group)
                xs = x[:, b * NT * D:(b + 1) * NT * D]
                dve.tensor_tensor(xs, xs, bank(0, 2), ALU.add).then_inc(s["y_added"], 1)

            def run(g, first):
                for b in range(B):
                    for c in range(group):
                        i = b * group + c
                        unit(g * per_group + i, i, first)
                        if c == 0 and not (first and b == 0):
                            gather(g * B + b - 1, (b - 1) % B)
                        if first:
                            pieces(b, c)

            run(0, True)
            with dve.Fori(1, groups) as g:
                run(g, False)
            gather(groups * B - 1, B - 1)

        @block.tensor
        def _(pe):
            def turned(f, k):
                if k == 0:
                    pe.wait_ge(s["xhat"], f + 1)
                    if f > 0:
                        pe.wait_ge(s[logits_read], f)
                elif f > 0:
                    pe.wait_ge(s["xT_lo"], KC * f + 1)
                for i in range(NT):
                    last = pe.transpose(front_bank(f, k)[:, i * P:(i + 1) * P], xhat[f % 2][:, i, k * P:(k + 1) * P], ident)
                last.then_inc(s["xT_psum"], 1)

            def logits(f, tiles):
                if 0 in tiles:
                    pe.wait_ge(s["r_lo"], 1)
                    pe.wait_ge(s["xT_lo"], KC * (f + 1))
                    if f > 0:
                        pe.wait_ge(s["wT"], f)
                for i in tiles:
                    for k in range(KC):
                        tt = slice(f * T + i * P, f * T + (i + 1) * P)
                        last = mm3(pe, bank(7)[:, i * n_exp:(i + 1) * n_exp], xT_hi[:, k, tt], xT_lo[:, k, tt], r_hi[:, k, :], r_lo[:, k, :], k == 0, k == KC - 1)
                if NT - 1 in tiles:
                    last.then_inc(s["logits"], 1)

            def weights_turned(f):
                pe.wait_ge(s["wx"], f + 1)
                if f + 1 < B:
                    pe.wait_ge(s["xT_lo"], KC * (f + 2))
                for i in range(NT):
                    last = pe.transpose(bank(7)[0:WR, :].bitcast(bf16)[:, i * P:(i + 1) * P], wx[:, i, :], conb[:, 0:P])
                last.then_inc(s["wT_psum"], 1)

            def pieces(b, c):
                if c in (1, 2) and b + 2 < B:
                    turned(b + 2, c - 1)
                if c == 3 + lag and b + 1 < B:
                    weights_turned(b + 1)

            for k in range(KC):
                turned(0, k)
            logits(0, range(NT))
            for k in range(KC):
                turned(1, k)

            def up(u, i, first, fresh):
                b, c, q = i // group, i % group, i % 2
                tt = slice(b * T, (b + 1) * T)
                if fresh is not None:
                    pe.wait_ge(s["split_lo"], fresh)
                for name, at, out, used in (("gate_psum", 0, bank(2 + q), "silu"), ("up_psum", KC * P, bank(4 + q), "gated")):
                    if not (first and i < 2):
                        pe.wait_ge(s[used], u - 1)
                    for k in range(KC):
                        cc = slice(at + k * P, at + (k + 1) * P)
                        last = mm3(pe, out, w_hi[:, c, cc], w_lo[:, c, cc], xT_hi[:, k, tt], xT_lo[:, k, tt], k == 0, k == KC - 1)
                    last.then_inc(s[name], 1)

            def spread(u, i, first, chunk):
                b, q = i // group, i % 2
                tt = slice(b * T, (b + 1) * T)
                if first and i > 0 or not first and i == 0:
                    pe.wait_ge(s["scaled"], u)
                elif not first:
                    pe.wait_ge(s["scaled"], u - 1)
                pe.matmul(bank(6 + (0 if first else q)), sel[:, chunk * P:(chunk + 1) * P] if isinstance(chunk, int) else sel[:, bass.ds(chunk * P, P)], wT[:, tt], start=True, stop=True).then_inc(s["spread_psum"], 1)

            def down(u, i, y):
                c, q = i % group, i % 2
                pe.wait_ge(s["h_lo"], u + 1)
                if c == 0 and y is not None:
                    pe.wait_ge(s["y_added"], y)
                for t in range(NT):
                    out = bank(t // 2)[:, (t % 2) * D:(t % 2 + 1) * D]
                    dn = slice(2 * KC * P, 2 * KC * P + D)
                    tt = slice(t * P, (t + 1) * P)
                    last = mm3(pe, out, h_hi[q][:, tt], h_lo[q][:, tt], w_hi[:, c, dn], w_lo[:, c, dn], c == 0 and t % 2 == 0, c == group - 1)
                last.then_inc(s["down"], 1)

            def run(g, first):
                for i in range(per_group):
                    u = g * per_group + i
                    c, f = i % group, i // group + 1
                    j, bj = (i - 1) % per_group, (i - 1) // group
                    if not (first and i < 2):
                        up(u, i, first, g * group + c + 1 if i < group else None)
                    if first:
                        if c == 0:
                            pe.wait_ge(s["wT"], f)
                            if f < B:
                                logits(f, (0, 1))
                        if i > 0:
                            down(u - 1, j, None if bj == 0 else bj)
                        spread(u, i, first, c)
                        if c == 0 and f < B:
                            logits(f, (2, 3))
                        pieces(f - 1, c)
                    else:
                        spread(u, i, first, g * group + c)
                        down(u - 1, j, g * B + bj)

            for c in range(2):
                up(c, c, True, c + 1)
            weights_turned(0)
            run(0, True)
            with pe.Fori(1, groups) as g:
                run(g, False)
            down(groups * per_group - 1, per_group - 1, groups * B - 1)


def golden_route(sb, s):
    n = NT
    inv = sb("inv_temp", [P, 1])
    z, inh, off, dist, w0, fb, zone, w1, rank, fw, rest0, rest1 = (
        sb(k, [P, n, E0]) for k in ("z", "inh", "off", "dist", "w0", "fb", "zone", "w1", "rank", "fw", "rest0", "rest1"))
    less, same = sb("less", [P, n, E0, E0]), sb("same", [P, n, E0, E0])
    wsum, none, some, fsum, finv, total, tinv = (sb(k, [P, n]) for k in ("wsum", "none", "some", "fsum", "finv", "total", "tinv"))
    flat = lambda t: t[:, :, :].rearrange("p i e -> p (i e)")
    wide = lambda t: t[:, :].unsqueeze(2).broadcast_to([P, n, E0])

    def scalar(act, logits, f):
        act.wait_ge(s["z"], f + 1)
        act.activation(flat(inh), flat(z), ACT.Sigmoid).then_inc(s["inh"], 1)
        act.wait_ge(s["dist"], f + 1)
        act.activation(flat(w0), flat(dist), ACT.Exp, scale=-1.0 / 0.1).then_inc(s["w0"], 1)
        act.activation(flat(fb), flat(dist), ACT.Exp, scale=-1.0 / 0.3).then_inc(s["fb"], 1)

    def ranks(dve, step, logits, side, f):
        tie = side[:, E1:E1 + E0 * E0].rearrange("p (a c) -> p a c", a=E0).unsqueeze(1).broadcast_to([P, n, E0, E0])
        step(dve.reciprocal(inv[:, :], side[:, 0:1]))
        dve.wait_ge(s["logits"], f + 1)
        dve.tensor_scalar(flat(z), logits, inv[:, 0:1], None, ALU.mult).then_inc(s["z"], 1)
        dve.wait_ge(s["inh"], f + 1)
        step(dve.tensor_scalar(flat(off), flat(inh), CENTER, None, ALU.subtract))
        dve.scalar_tensor_tensor(flat(dist), flat(off), -1.0, flat(off), ALU.mult, ALU.max).then_inc(s["dist"], 1)
        dve.wait_ge(s["dist"], f + 1)
        step(dve.tensor_scalar(flat(zone), flat(inh), LOWER, None, ALU.is_ge))
        step(dve.scalar_tensor_tensor(flat(off), flat(inh), UPPER, flat(zone), ALU.is_le, ALU.mult))
        step.beside(dve.tensor_tensor(less[:, :, :, :], dist[:, :, :].unsqueeze(2).broadcast_to([P, n, E0, E0]),
                               dist[:, :, :].unsqueeze(3).broadcast_to([P, n, E0, E0]), ALU.is_lt))
        step(dve.tensor_tensor(same[:, :, :, :], dist[:, :, :].unsqueeze(2).broadcast_to([P, n, E0, E0]),
                               dist[:, :, :].unsqueeze(3).broadcast_to([P, n, E0, E0]), ALU.is_equal))
        step(dve.tensor_tensor(same[:, :, :, :], same[:, :, :, :], tie, ALU.mult))
        step(dve.tensor_tensor(less[:, :, :, :], less[:, :, :, :], same[:, :, :, :], ALU.add))
        step(dve.tensor_reduce(rank[:, :, :], less[:, :, :, :], AX.X, ALU.add))

    def weights(dve, step, f):
        dve.wait_ge(s["fb"], f + 1)
        step.beside(dve.scalar_tensor_tensor(flat(fw), flat(rank), float(TOP0), flat(fb), ALU.is_lt, ALU.mult))
        step(dve.tensor_tensor(flat(w1), flat(w0), flat(off), ALU.mult))
        step.beside(dve.tensor_reduce(fsum[:, :], fw[:, :, :], AX.X, ALU.add))
        step(dve.tensor_reduce(wsum[:, :], w1[:, :, :], AX.X, ALU.add))
        step.beside(dve.tensor_scalar(fsum[:, :], fsum[:, :], 1e-8, None, ALU.max))
        step(dve.tensor_scalar(none[:, :], wsum[:, :], 1e-8, None, ALU.is_lt))
        step.beside(dve.reciprocal(finv[:, :], fsum[:, :]))
        step(dve.tensor_scalar(some[:, :], none[:, :], -1.0, 1.0, ALU.mult, ALU.add))
        step.beside(dve.tensor_tensor(fw[:, :, :], fw[:, :, :], wide(finv), ALU.mult))
        step(dve.tensor_tensor(w1[:, :, :], w1[:, :, :], wide(some), ALU.mult))
        step(dve.tensor_tensor(fw[:, :, :], fw[:, :, :], wide(none), ALU.mult))
        step(dve.tensor_tensor(flat(w1), flat(w1), flat(fw), ALU.add))
        step(dve.tensor_reduce(total[:, :], w1[:, :, :], AX.X, ALU.add))
        step(dve.tensor_scalar(total[:, :], total[:, :], 1e-8, None, ALU.max))
        step(dve.reciprocal(tinv[:, :], total[:, :]))
        step(dve.tensor_tensor(w1[:, :, :], w1[:, :, :], wide(tinv), ALU.mult))
        return w1[:, :, :]

    return {"scalar": scalar, "ranks": ranks, "weights": weights, "rest0": rest0, "rest1": rest1}


def top_route(sb, s):
    n, m = NT, E1 // G1
    sig, sc, ms, rank, w1, rest0, rest1 = (sb(k, [P, n, E1]) for k in ("sig", "sc", "ms", "rank", "w1", "rest0", "rest1"))
    less, same = sb("less", [P, NT, E1, E1]), sb("same", [P, NT, E1, E1])
    gmax, grank, gm, pen = (sb(k, [P, n, G1]) for k in ("gmax", "grank", "gm", "pen"))
    gless, gsame = sb("gless", [P, n, G1, G1]), sb("gsame", [P, n, G1, G1])
    total, tinv = sb("total", [P, n]), sb("tinv", [P, n])
    flat = lambda t: t[:, :, :].rearrange("p i e -> p (i e)")
    grouped = lambda t: t[:, :, :].rearrange("p i (g e) -> p (i g) e", g=G1)
    spread = lambda t: t[:, :, :].rearrange("p i g -> p (i g)").unsqueeze(2).broadcast_to([P, n * G1, m])

    def scalar(act, logits, f):
        act.wait_ge(s["logits"], f + 1)
        act.activation(flat(sig), logits, ACT.Sigmoid).then_inc(s["inh"], 1)

    def groups(dve, step, side, f):
        t0 = E1 + E0 * E0
        gtie = side[:, t0 + E1 * E1:].rearrange("p (a c) -> p a c", a=G1).unsqueeze(1).broadcast_to([P, n, G1, G1])
        dve.wait_ge(s["inh"], f + 1)
        step(dve.tensor_tensor(sc[:, :, :], sig[:, :, :], side[:, 0:E1].unsqueeze(1).broadcast_to([P, n, E1]), ALU.add))
        step(dve.tensor_reduce(gmax[:, :, :].rearrange("p i g -> p (i g)"), grouped(sc), AX.X, ALU.max))
        a, c = gmax[:, :, :].unsqueeze(2).broadcast_to([P, n, G1, G1]), gmax[:, :, :].unsqueeze(3).broadcast_to([P, n, G1, G1])
        step.beside(dve.tensor_tensor(gless[:, :, :, :], a, c, ALU.is_gt))
        step(dve.tensor_tensor(gsame[:, :, :, :], a, c, ALU.is_equal))
        step(dve.tensor_tensor(gsame[:, :, :, :], gsame[:, :, :, :], gtie, ALU.mult))
        step(dve.tensor_tensor(gless[:, :, :, :], gless[:, :, :, :], gsame[:, :, :, :], ALU.add))
        step(dve.tensor_reduce(grank[:, :, :], gless[:, :, :, :], AX.X, ALU.add))
        step(dve.tensor_scalar(flat(gm), flat(grank), float(TOPG1), None, ALU.is_lt))
        step(dve.tensor_scalar(flat(pen), flat(gm), -1.0, BIG, ALU.add, ALU.mult))
        step(dve.tensor_tensor(grouped(ms), grouped(sc), spread(gm), ALU.mult))
        step(dve.tensor_tensor(grouped(ms), grouped(ms), spread(pen), ALU.add))

    def ranks(dve, step, logits, side, f):
        t0 = E1 + E0 * E0
        tie = side[:, t0:t0 + E1 * E1].rearrange("p (a c) -> p a c", a=E1).unsqueeze(1).broadcast_to([P, NT, E1, E1])
        a, c = ms[:, :, :].unsqueeze(2).broadcast_to([P, NT, E1, E1]), ms[:, :, :].unsqueeze(3).broadcast_to([P, NT, E1, E1])
        step.beside(dve.tensor_tensor(less[:, :, :, :], a, c, ALU.is_gt))
        step(dve.tensor_tensor(same[:, :, :, :], a, c, ALU.is_equal))
        step(dve.tensor_tensor(same[:, :, :, :], same[:, :, :, :], tie, ALU.mult))

    def weights(dve, step, f):
        step(dve.tensor_tensor(less[:, :, :, :], less[:, :, :, :], same[:, :, :, :], ALU.add))
        step(dve.tensor_reduce(rank[:, :, :], less[:, :, :, :], AX.X, ALU.add))
        step(dve.scalar_tensor_tensor(flat(w1), flat(rank), float(TOP1), flat(sig), ALU.is_lt, ALU.mult))
        step(dve.tensor_reduce(total[:, :], w1[:, :, :], AX.X, ALU.add))
        step(dve.reciprocal(tinv[:, :], total[:, :]))
        step(dve.tensor_tensor(w1[:, :, :], w1[:, :, :], tinv[:, :].unsqueeze(2).broadcast_to([P, n, E1]), ALU.mult))
        return w1[:, :, :]

    return {"scalar": scalar, "groups": groups, "ranks": ranks, "weights": weights, "rest0": rest0, "rest1": rest1}


FRONT_AT = {
    "dve": (6, 9, 12, 33, 14, 16, 18, 20, 23, 25, 27, 29, 28, 31),
    "act": (8, 11, 17, 19, 26, 30, 31, 32),
    "pe": (13, 15, 16, 18, 22, 24, 26, 28, 30, 31),
}
UNITS = tuple((4, (h,)) for h in range(4)) + tuple((3, (h,)) for h in range(4)) + ((2, (0, 1)), (2, (2, 3)), (1, (0, 1)), (1, (2, 3)))
NU = len(UNITS)
MAX_STEP = (1, 1, 2, 2, 3, 3, 4, 4, 5, 5, 6, 6)
VALUE_STEP = (4, 8, 10, NU)
KEY_BANKS = 3


def after(engine, sem, count):
    if not isinstance(count, int) or count > 0:
        engine.wait_ge(sem, count)


def rotary_attention(nc, kept, x, psum, con, conb, dram):
    ctx = ExitStack()
    with ctx:
        def sb(name, shape, dt=f32):
            return ctx.enter_context(nc.sbuf_tensor(f"a1_{name}", shape, dt))

        s = sems(nc, kept, "a1", "rope_in w_in wo_in small_in w_hi w_lo wo_hi wo_lo sel_r v_pad "
                 "stats moments var_eps ln_var rstd0 newton ln_ms rms0 rms_newton xhat xr xT_psum xw xT_hi xT_lo residual "
                 "qk_psum v_psum v_raw v_sb rot q_rot k_rot rot_hi rot_lo k_psum k_stack q_psum q_stack q_stack_too "
                 "score_psum max max_parts mT_psum mT key_psum prob_ready ot_psum o_raw sum_psum sum_sb recip o_t o_hi o_lo wo_psum x_out")
        w_hi, w_lo = sb("w_hi", [P, KC, W1N], f32r), sb("w_lo", [P, KC, W1N], f32r)
        wo_hi, wo_lo = sb("wo_hi", [P, NST, D], f32r), sb("wo_lo", [P, NST, D], f32r)
        rope = sb("rope", [P, C_SEL])
        sel = sb("sel", [P, 16 * P], f32r)
        cols, rows = sb("cols", [P, 6]), sb("rows", [P, 2 * D])
        st, mv = sb("st", [P, NT, 6]), sb("mv", [P, NT, 2])
        ve, lnv, r0, n1, n2, rstd, ms, lnm, m0, m1, m2, rms = (
            sb(k, [P, NT]) for k in ("ve", "lnv", "r0", "n1", "n2", "rstd", "ms", "lnm", "m0", "m1", "m2", "rms"))
        xhat, xr = sb("xhat", [P, NT, D]), sb("xr", [P, NT, D])
        xw = sb("xw", [P, KC, T])
        xT_hi, xT_lo = sb("xT_hi", [P, KC, T], f32r), sb("xT_lo", [P, KC, T], f32r)
        ra, rb_ = sb("ra", [P, 2, T]), sb("rb_", [P, 2, T])
        rot = sb("rot", [P, 2, T])
        rot_hi, rot_lo = sb("rot_hi", [P, 2, T], f32r), sb("rot_lo", [P, 2, T], f32r)
        k_stack = [sb(f"k_stack{i}", [P, T], f32r) for i in range(2)]
        q_stack = [sb(f"q_stack{i}", [P, HPT, T], f32r) for i in range(2)]
        vs = sb("vs", [P, NT, H1, 32])
        v_raw = sb("v_raw", [P, NT, D])
        prob = [sb(f"prob{i}", [P, HPT, T]) for i in range(2)]
        mx, mrest = sb("mx", [P, NT, HPT]), sb("mrest", [P, NT, HPT])
        mparts = sb("mparts", [P, NT, HPT, 32], bf16)
        mT = [sb(f"mT{i}", [P, T], bf16) for i in range(2)]
        o_raw, o_sum, rinv, o_t = (sb(k, [P, T]) for k in ("o_raw", "o_sum", "rinv", "o_t"))
        o_hi, o_lo = sb("o_hi", [P, NST, T], f32r), sb("o_lo", [P, NST, T], f32r)
        held = sb("held", [P, 4])
        bank = lambda i, m=1: psum[:, 512 * i:512 * (i + m)]
        ident = con[:, C_ID:C_ID + P]
        xb = lambda b: x[:, b * NT * D:(b + 1) * NT * D] if isinstance(b, int) else x[:, bass.ds(b * NT * D, NT * D)]

        def heads(one, unit):
            blocks, hh = unit
            return one[:, 0:len(hh) * blocks * P].rearrange("p (h t) -> p h t", h=len(hh))

        def front_bank(f, k):
            return bank((k + 1) % 8) if isinstance(f, int) and f == 0 else bank(1)

        def output_bank(b, m):
            return bank(2) if isinstance(b, int) and b == B - 1 and m == 1 else bank(1)

        misc = bank(7)

        def hold(dve, place):
            dve.tensor_copy(held[:, place:place + 1], con[:, 0:1])

        w_raw, wo_raw, sel_raw = sb("w_raw", [P, KC, W1N]), sb("wo_raw", [P, NST, D]), sb("sel_raw", [P, 16 * P])

        block = ctx.enter_context(nc.Block())

        @block.sync
        def _(sp):
            sp.dma_start(cols[:, :], dram["cols1"]).then_inc(s["small_in"], 16)
            sp.dma_start(w_raw[:, :, :], dram["w1"]).then_inc(s["w_in"], 16)
            sp.dma_start(rows[:, :], dram["rows1"].broadcast_to([P, 2 * D])).then_inc(s["small_in"], 16)
            sp.dma_start(rope[:, :], dram["rope"][:, 0:C_SEL]).then_inc(s["small_in"], 16)
            sp.dma_start(sel_raw[:, :], dram["rope"][:, C_SEL:]).then_inc(s["rope_in"], 16)
            sp.dma_start(wo_raw[:, :, :], dram["wo1"]).then_inc(s["wo_in"], 16)

        @block.gpsimd
        def _(pool):
            pool.memset(vs[:, :, :, DH1 + 1:], 0.0)
            pool.memset(mparts[:, :, :, :], 0.0)
            pool.memset(vs[:, :, :, DH1:DH1 + 1], 1.0).then_inc(s["v_pad"], 1)
            for raw, hi, lo, came, s_hi, s_lo in ((w_raw, w_hi, w_lo, "w_in", "w_hi", "w_lo"), (wo_raw, wo_hi, wo_lo, "wo_in", "wo_hi", "wo_lo")):
                pool.wait_ge(s[came], 16)
                if came == "wo_in":
                    pool.tensor_copy(hi[:], raw[:]).then_inc(s[s_hi], 1)
                pool.wait_ge(s[s_hi], 1)
                pool.tensor_tensor(lo[:], raw[:], hi[:].bitcast(f32), ALU.subtract).then_inc(s[s_lo], 1)
                if came == "w_in":
                    pool.wait_ge(s["rope_in"], 16)
                    pool.tensor_copy(sel[:, :], sel_raw[:, :]).then_inc(s["sel_r"], 1)

        def every_step(pieces, engine_name):
            assert len(pieces) == len(FRONT_AT[engine_name])
            return dict(zip(FRONT_AT[engine_name], pieces))

        @block.scalar
        def _(act):
            act.preload_act_table_set(LN_EXP_SET)

            def front(f):
                def guess():
                    act.wait_ge(s["var_eps"], f + 1)
                    act.activation(lnv[:, :], ve[:, :], ACT.Ln).then_inc(s["ln_var"], 1)
                    act.wait_ge(s["ln_var"], f + 1)
                    act.activation(r0[:, :], lnv[:, :], ACT.Exp, scale=-0.5).then_inc(s["rstd0"], 1)

                def guess_rms():
                    act.wait_ge(s["newton"], 6 * f + 6)
                    act.activation(lnm[:, :], ms[:, :], ACT.Ln).then_inc(s["ln_ms"], 1)
                    act.wait_ge(s["ln_ms"], f + 1)
                    act.activation(m0[:, :], lnm[:, :], ACT.Exp, scale=-0.5).then_inc(s["rms0"], 1)

                def turned(k):
                    if isinstance(f, int) and f == 0 and k == 0:
                        act.wait_ge(s["small_in"], 48)
                    act.wait_ge(s["xT_psum"], KC * f + k + 1)
                    act.activation(xw[:, k, :], front_bank(f, k), ACT.Copy, scale=cols[:, 4 + k:5 + k]).then_inc(s["xw"], 1)
                    act.wait_ge(s["xw"], KC * f + k + 1)
                    act.activation(xT_hi[:, k, :], xw[:, k, :], ACT.Copy).then_inc(s["xT_hi"], 1)

                def rotated(w):
                    act.wait_ge(s[("q_rot", "k_rot")[w]], f + 1)
                    act.activation(rot_hi[:, w, :], rot[:, w, :], ACT.Copy).then_inc(s["rot_hi"], 1)

                def values(m):
                    act.wait_ge(s["v_psum"], 2 * f + m + 1)
                    act.activation(v_raw[:, 2 * m:2 * m + 2, :], front_bank(f, 6 + m).rearrange("p (i d) -> p i d", i=2), ACT.Copy).then_inc(s["v_raw"], 1)

                return every_step([guess, guess_rms, lambda: turned(0), lambda: turned(1), lambda: rotated(0), lambda: rotated(1),
                                   lambda: values(0), lambda: values(1)], "act")

            def k_stacked(tau, t):
                act.wait_ge(s["k_psum"], tau + 1)
                act.activation(k_stack[t % 2][:, :], misc, ACT.Copy).then_inc(s["k_stack"], 1)

            def q_stacked(tau, t):
                act.wait_ge(s["q_psum"], tau + 1)
                for hh in range(HPT // 2):
                    last = act.activation(q_stack[t % 2][:, hh, :], misc, ACT.Copy, scale=rope[:, C_HEAD + hh:C_HEAD + hh + 1])
                last.then_inc(s["q_stack"], 1)

            def maxima_turned(tau, t):
                act.wait_ge(s["mT_psum"], tau + 1)
                act.activation(mT[t % 2][:, :], misc.bitcast(bf16)[:, 0:T], ACT.Copy).then_inc(s["mT"], 1)

            def exps(tau, n):
                blocks, hh = UNITS[n]
                j = NT - blocks
                act.wait_ge(s["key_psum"], NU * tau + n + 1)
                after(act, s["ot_psum"], NT * tau + j - 1)
                act.activation(prob[j % 2][:, hh[0]:hh[-1] + 1, 0:blocks * P], heads(bank(4 + n % KEY_BANKS), UNITS[n]), ACT.Exp,
                               scale=0.5).then_inc(s["prob_ready"], 1)

            def finished_raw(tau):
                act.wait_ge(s["ot_psum"], NT * (tau + 1))
                after(act, s["o_t"], tau)
                act.activation(o_raw[:, :], bank(0), ACT.Copy).then_inc(s["o_raw"], 1)

            def finished_sums(tau):
                act.wait_ge(s["sum_psum"], tau + 1)
                act.activation(o_sum[:, :], misc, ACT.Copy).then_inc(s["sum_sb"], 1)

            def finished_hi(tau, t, b):
                act.wait_ge(s["o_t"], tau + 1)
                if t == 0:
                    after(act, s["wo_psum"], 2 * b)
                act.activation(o_hi[:, t, :], o_t[:, :], ACT.Copy).then_inc(s["o_hi"], 1)

            def turn(b, ahead):
                pieces = front(b + 1) if ahead else {}
                for t in range(NST):
                    tau = NST * b + t
                    one, two = ahead or t < NST - 1, ahead or t < NST - 2
                    before = t > 0 or not isinstance(b, int) or b > 0
                    for n in range(NU):
                        exps(tau, n)
                        if n == 1 and before:
                            finished_raw(tau - 1)
                        if n == 3 and before:
                            finished_sums(tau - 1)
                        if n == 8 and one:
                            maxima_turned(tau + 1, t + 1)
                        if n == 9 and two:
                            k_stacked(tau + 2, t + 2)
                        if n == 10 and before:
                            finished_hi(tau - 1, (t - 1) % NST, b)
                        if n == 11 and two:
                            q_stacked(tau + 2, t + 2)
                        if NU * t + n in pieces:
                            pieces[NU * t + n]()

            for k, piece in enumerate(front(0).values()):
                piece()
                if k == 1:
                    act.wait_ge(s["w_in"], 16)
                    act.activation(w_hi[:, :, :], w_raw[:, :, :], ACT.Copy).then_inc(s["w_hi"], 1)
            k_stacked(0, 0)
            q_stacked(0, 0)
            maxima_turned(0, 0)
            k_stacked(1, 1)
            q_stacked(1, 1)
            turn(0, True)
            with act.Fori(1, B - 1) as b:
                turn(b, True)
            turn(B - 1, False)
            finished_raw(B * NST - 1)
            finished_sums(B * NST - 1)
            finished_hi(B * NST - 1, NST - 1, B - 1)

        @block.vector
        def _(dve):
            def front(f):
                xf = lambda i: x[:, f * NT * D + i * D:f * NT * D + (i + 1) * D] if isinstance(f, int) else x[:, bass.ds(f * NT * D + i * D, D)]

                def moments():
                    for i in range(NT):
                        last = dve.bn_stats(st[:, i, :], xf(i))
                    last.then_inc(s["stats"], 1)
                    dve.wait_ge(s["stats"], f + 1)
                    hold(dve, 0)
                    for i in range(NT):
                        last = dve.bn_aggr(mv[:, i, :], st[:, i, :])
                    last.then_inc(s["moments"], 1)
                    dve.wait_ge(s["moments"], f + 1)
                    dve.tensor_scalar(ve[:, :], mv[:, :, 1], EPS, None, ALU.add).then_inc(s["var_eps"], 1)

                def refine():
                    def newton(k, ins):
                        ins.then_inc(s["newton"], 1)
                        dve.wait_ge(s["newton"], 6 * f + k)

                    dve.wait_ge(s["rstd0"], f + 1)
                    newton(1, dve.scalar_tensor_tensor(n1[:, :], r0[:, :], -0.5, r0[:, :], ALU.mult, ALU.mult))
                    newton(2, dve.tensor_tensor(n2[:, :], n1[:, :], ve[:, :], ALU.mult))
                    newton(3, dve.scalar_tensor_tensor(rstd[:, :], n2[:, :], 1.5, r0[:, :], ALU.add, ALU.mult))
                    newton(4, dve.tensor_tensor(m1[:, :], rstd[:, :], rstd[:, :], ALU.mult))
                    newton(5, dve.tensor_tensor(m2[:, :], m1[:, :], mv[:, :, 1], ALU.mult))
                    newton(6, dve.tensor_scalar(ms[:, :], m2[:, :], EPS, None, ALU.add))

                def normal():
                    for i in range(NT):
                        last = dve.tensor_scalar(xhat[:, i, :], xf(i), mv[:, i, 0:1], rstd[:, i:i + 1], ALU.subtract, ALU.mult)
                    last.then_inc(s["xhat"], 1)
                    dve.wait_ge(s["rms0"], f + 1)
                    dve.scalar_tensor_tensor(m1[:, :], m0[:, :], -0.5, m0[:, :], ALU.mult, ALU.mult).then_inc(s["rms_newton"], 1)
                    dve.wait_ge(s["rms_newton"], 3 * f + 1)
                    dve.tensor_tensor(m2[:, :], m1[:, :], ms[:, :], ALU.mult).then_inc(s["rms_newton"], 1)
                    dve.wait_ge(s["rms_newton"], 3 * f + 2)
                    dve.scalar_tensor_tensor(rms[:, :], m2[:, :], 1.5, m0[:, :], ALU.add, ALU.mult).then_inc(s["rms_newton"], 1)
                    dve.wait_ge(s["rms_newton"], 3 * f + 3)
                    dve.wait_ge(s["xhat"], f + 1)
                    for i in range(NT):
                        last = dve.tensor_scalar(xr[:, i, :], xhat[:, i, :], rms[:, i:i + 1], None, ALU.mult)
                    last.then_inc(s["xr"], 1)

                def residual():
                    if isinstance(f, int) and f == 0:
                        dve.wait_ge(s["small_in"], 48)
                    dve.wait_ge(s["xr"], f + 1)
                    wide_bo = rows[:, D:2 * D].unsqueeze(1).broadcast_to([P, NT, D])
                    dve.tensor_tensor(xhat[:, :, :], xhat[:, :, :], wide_bo, ALU.add).then_inc(s["residual"], 1)
                    dve.wait_ge(s["residual"], 2 * f + 1)
                    xx = x[:, f * NT * D:(f + 1) * NT * D] if isinstance(f, int) else xb(f)
                    dve.tensor_tensor(xx, xx, xhat[:, :, :].rearrange("p i d -> p (i d)"), ALU.add).then_inc(s["residual"], 1)

                def turned(k):
                    dve.wait_ge(s["xT_hi"], KC * f + k + 1)
                    dve.tensor_tensor(xT_lo[:, k, :], xw[:, k, :], xT_hi[:, k, :].bitcast(f32), ALU.subtract).then_inc(s["xT_lo"], 1)

                cos, sin = rope[:, C_COS:C_COS + T], rope[:, C_SIN:C_SIN + T]

                def product(w, m):
                    dve.wait_ge(s["qk_psum"], 4 * f + 2 * w + m + 1)
                    dve.scalar_tensor_tensor((ra, rb_)[m][:, w, :], front_bank(f, 2 + 2 * w + m), cols[:, 2 * w + m:2 * w + m + 1], (cos, sin)[m],
                                             ALU.add, ALU.mult).then_inc(s["rot"], 1)
                    if m == 1:
                        dve.wait_ge(s["rot"], 4 * f + 2 * w + 2)
                        dve.tensor_tensor(rot[:, w, :], ra[:, w, :], rb_[:, w, :], ALU.add).then_inc(s[("q_rot", "k_rot")[w]], 1)

                def rotated(w):
                    dve.wait_ge(s["rot_hi"], 2 * f + w + 1)
                    dve.tensor_tensor(rot_lo[:, w, :], rot[:, w, :], rot_hi[:, w, :].bitcast(f32), ALU.subtract).then_inc(s["rot_lo"], 1)

                return every_step([moments, refine, normal, residual, lambda: output(f - 2, 0), lambda: output(f - 2, 1),
                                   lambda: turned(0), lambda: turned(1), lambda: product(0, 0), lambda: product(0, 1),
                                   lambda: product(1, 0), lambda: product(1, 1), lambda: rotated(0), lambda: rotated(1)], "dve")

            def output(b, m):
                if isinstance(b, int) and b < 0:
                    return
                dve.wait_ge(s["wo_psum"], 2 * b + m + 1)
                half = NT * D // 2
                at = b * NT * D + m * half
                xx = x[:, at:at + half] if isinstance(b, int) else x[:, bass.ds(at, half)]
                dve.tensor_tensor(xx, xx, output_bank(b, m), ALU.add).then_inc(s["x_out"], 1)

            def maxima(tau, m):
                blocks, hh = UNITS[m]
                dve.wait_ge(s["score_psum"], NU * tau + m + 1)
                dve.tensor_reduce(mx[:, blocks - 1, hh[0]:hh[-1] + 1], heads(bank(2 + m % 2), UNITS[m]), AX.X, ALU.max).then_inc(s["max"], 1)
                if m == NU - 1:
                    parts = [mparts[:, :, :, k] for k in range(3)]
                    dve.wait_ge(s["max"], NU * (tau + 1))
                    dve.tensor_scalar(parts[0], mx[:, :, :], -1.0, None, ALU.mult).then_inc(s["max_parts"], 1)
                    dve.wait_ge(s["max_parts"], 4 * tau + 1)
                    dve.scalar_tensor_tensor(mrest[:, :, :], mx[:, :, :], -1.0, parts[0], ALU.mult, ALU.subtract).then_inc(s["max_parts"], 1)
                    dve.wait_ge(s["max_parts"], 4 * tau + 2)
                    dve.tensor_copy(parts[1], mrest[:, :, :]).then_inc(s["max_parts"], 1)
                    dve.wait_ge(s["max_parts"], 4 * tau + 3)
                    dve.tensor_tensor(parts[2], mrest[:, :, :], parts[1], ALU.subtract).then_inc(s["max_parts"], 1)

            def q_stacked(tau, t):
                dve.wait_ge(s["q_stack"], tau + 1)
                for hh in range(HPT // 2, HPT):
                    last = dve.tensor_scalar(q_stack[t % 2][:, hh, :], misc, rope[:, C_HEAD + hh:C_HEAD + hh + 1], None, ALU.mult)
                last.then_inc(s["q_stack_too"], 1)

            def scaled(tau):
                dve.wait_ge(s["sum_sb"], tau + 1)
                dve.reciprocal(rinv[:, :], o_sum[:, :]).then_inc(s["recip"], 1)
                dve.wait_ge(s["recip"], tau + 1)
                after(dve, s["o_lo"], tau)
                dve.tensor_tensor(o_t[:, :], o_raw[:, :], rinv[:, :], ALU.mult).then_inc(s["o_t"], 1)

            def rest(tau, t):
                dve.wait_ge(s["o_hi"], tau + 1)
                dve.tensor_tensor(o_lo[:, t, :], o_t[:, :], o_hi[:, t, :].bitcast(f32), ALU.subtract).then_inc(s["o_lo"], 1)

            def turn(b, ahead):
                pieces = front(b + 1) if ahead else {FRONT_AT["dve"][4 + m]: (lambda m=m: output(b - 1, m)) for m in range(2)}
                for t in range(NST):
                    tau = NST * b + t
                    more = ahead or t < NST - 1
                    finished = t > 0 or not isinstance(b, int) or b > 0
                    for n in range(NU):
                        for m in range(NU):
                            if more and MAX_STEP[m] == n:
                                maxima(tau + 1, m)
                        if n == 2 and t == 0:
                            dve.wait_ge(s["v_raw"], 2 * b + 2)
                            after(dve, s["ot_psum"], NT * NST * b)
                            for i in range(NT):
                                last = dve.tensor_tensor(vs[:, i, :, 0:DH1], v_raw[:, i, :].rearrange("p (h v) -> p h v", h=H1),
                                                         rows[:, 0:D].rearrange("p (h v) -> p h v", h=H1), ALU.add)
                            last.then_inc(s["v_sb"], 1)
                        if n == 7 and finished:
                            scaled(tau - 1)
                        if n == 10 and finished:
                            rest(tau - 1, (t - 1) % NST)
                        if n == 11 and (ahead or t < NST - 2):
                            q_stacked(tau + 2, t + 2)
                        if NU * t + n in pieces:
                            pieces[NU * t + n]()

            for piece in front(0).values():
                piece()
            dve.wait_ge(s["v_pad"], 1)
            q_stacked(0, 0)
            for m in range(NU):
                maxima(0, m)
            q_stacked(1, 1)
            turn(0, True)
            with dve.Fori(1, B - 1) as b:
                turn(b, True)
            turn(B - 1, False)
            scaled(B * NST - 1)
            rest(B * NST - 1, NST - 1)
            for m in range(2):
                output(B - 1, m)

        @block.tensor
        def _(pe):
            def output(b, m):
                if isinstance(b, int) and b < 0:
                    return
                out = output_bank(b, m)
                if m == 0:
                    pe.wait_ge(s["wo_lo"], 1)
                    pe.wait_ge(s["o_lo"], NST * (b + 1))
                elif not (isinstance(b, int) and b == B - 1):
                    pe.wait_ge(s["x_out"], 2 * b + 1)
                for i in (2 * m, 2 * m + 1):
                    for k in range(NST):
                        tt = slice(i * P, (i + 1) * P)
                        last = mm3(pe, out[:, (i % 2) * D:(i % 2 + 1) * D], o_hi[:, k, tt], o_lo[:, k, tt],
                                   wo_hi[:, k, :], wo_lo[:, k, :], k == 0, k == NST - 1)
                last.then_inc(s["wo_psum"], 1)

            def front(f):
                def turned(k):
                    pe.wait_ge(s["xr"], f + 1)
                    if isinstance(f, int) and f == 0:
                        pass
                    elif k == 1:
                        pe.wait_ge(s["xT_hi"], KC * f + 1)
                    elif not isinstance(f, int) or f > 1:
                        pe.wait_ge(s["x_out"], 2 * f - 2)
                    elif f == 1:
                        pe.wait_ge(s["v_raw"], 2)
                    for i in range(NT):
                        last = pe.transpose(front_bank(f, k)[:, i * P:(i + 1) * P], xr[:, i, k * P:(k + 1) * P], ident)
                    last.then_inc(s["xT_psum"], 1)

                def project(m):
                    if m == 0:
                        pe.wait_ge(s["w_lo"], 1)
                        pe.wait_ge(s["xT_lo"], KC * f + KC)
                    elif not isinstance(f, int) or f > 0:
                        pe.wait_ge(s["rot"], 4 * f + m)
                    for k in range(KC):
                        col = m * P
                        last = mm3(pe, front_bank(f, 2 + m), w_hi[:, k, col:col + P], w_lo[:, k, col:col + P], xT_hi[:, k, :], xT_lo[:, k, :], k == 0, k == KC - 1)
                    last.then_inc(s["qk_psum"], 1)

                def values(m):
                    if isinstance(f, int) and f == 0:
                        pass
                    elif m == 0:
                        pe.wait_ge(s["rot"], 4 * f + 4)
                    else:
                        pe.wait_ge(s["v_raw"], 2 * f + 1)
                    for i in (2 * m, 2 * m + 1):
                        for k in range(KC):
                            tt = slice(i * P, (i + 1) * P)
                            last = mm3(pe, front_bank(f, 6 + m)[:, (i % 2) * D:(i % 2 + 1) * D], xT_hi[:, k, tt], xT_lo[:, k, tt],
                                       w_hi[:, k, W1V:W1V + D], w_lo[:, k, W1V:W1V + D], k == 0, k == KC - 1)
                    last.then_inc(s["v_psum"], 1)

                return every_step([lambda: output(f - 2, 0), lambda: output(f - 2, 1), lambda: turned(0), lambda: turned(1), lambda: project(0),
                                   lambda: project(1), lambda: project(2), lambda: project(3), lambda: values(0), lambda: values(1)], "pe")

            def stack(tau, t, w):
                if w == 1:
                    after(pe, s["mT"], tau)
                else:
                    pe.wait_ge(s["k_stack"], tau + 1)
                at = (t * 2 + w) * 2 * P
                pe.matmul(misc, sel[:, at:at + P], rot_hi[:, w, :], start=True, stop=False, skip_group_check=True)
                pe.matmul(misc, sel[:, at + P:at + 2 * P], rot_lo[:, w, :], start=False, stop=True, skip_group_check=True).then_inc(
                    s[("q_psum", "k_psum")[w]], 1)

            def scores(tau, t, m):
                blocks, hh = UNITS[m]
                i = blocks - 1
                if m == 0:
                    pe.wait_ge(s["q_stack_too"], tau + 1)
                after(pe, s["max"], NU * tau + m - 1 if m > 1 else NU * tau)
                out = heads(bank(2 + m % 2), UNITS[m])
                for e, h in enumerate(hh):
                    pe.matmul(out[:, e, :], q_stack[t % 2][:, h, i * P:(i + 1) * P], k_stack[t % 2][:, 0:(i + 1) * P],
                              start=True, stop=False, skip_group_check=True)
                    last = pe.matmul(out[:, e, i * P:(i + 1) * P], conb[:, 0:P], conb[:, P:2 * P],
                                     start=False, stop=True, skip_group_check=True)
                last.then_inc(s["score_psum"], 1)

            def maxima_turned(tau):
                pe.wait_ge(s["max_parts"], 4 * tau + 4)
                after(pe, s["sum_sb"], tau - 1)
                for i in range(NT):
                    last = pe.transpose(misc.bitcast(bf16)[:, i * P:(i + 1) * P], mparts[:, i, :, :].rearrange("p h k -> p (h k)"), conb[:, 0:P])
                last.then_inc(s["mT_psum"], 1)

            def keys(tau, t, n):
                blocks, hh = UNITS[n]
                j = NT - blocks
                if n == 0:
                    pe.wait_ge(s["mT"], tau + 1)
                after(pe, s["prob_ready"], NU * tau + n + 1 - KEY_BANKS)
                out = heads(bank(4 + n % KEY_BANKS), UNITS[n])
                for e, h in enumerate(hh):
                    pe.matmul(out[:, e, :], k_stack[t % 2][:, j * P:(j + 1) * P], q_stack[t % 2][:, h, j * P:],
                              start=True, stop=False, skip_group_check=True)
                    pe.matmul(out[:, e, :], conb[:, (2 + h) * P:(3 + h) * P], mT[t % 2][:, j * P:], start=False, stop=False, skip_group_check=True)
                    last = pe.matmul(out[:, e, 0:P], conb[:, P:2 * P], conb[:, 0:P], start=False, stop=True, skip_group_check=True)
                last.then_inc(s["key_psum"], 1)

            def weighted(tau, t, j):
                pe.wait_ge(s["prob_ready"], NU * tau + (4, 8, 10, 12)[j])
                if j == 0:
                    after(pe, s["o_raw"], tau)
                for hh in range(HPT):
                    q = 32 * hh
                    last = pe.matmul(bank(0)[q:q + 32, j * P:], vs[:, j, t * HPT + hh, :], prob[j % 2][:, hh, 0:T - j * P],
                                     start=(j == 0), stop=(j == NT - 1), tile_position=(0, q), skip_group_check=True)
                last.then_inc(s["ot_psum"], 1)

            def sums(tau):
                pe.wait_ge(s["o_raw"], tau + 1)
                after(pe, s["q_stack_too"], tau + 3 if not isinstance(tau, int) else min(tau + 3, B * NST))
                pe.matmul(misc, rope[:, C_SUM:C_SUM + P], o_raw[:, :], start=True, stop=True, skip_group_check=True).then_inc(s["sum_psum"], 1)

            def turn(b, ahead):
                pieces = front(b + 1) if ahead else {FRONT_AT["pe"][m]: (lambda m=m: output(b - 1, m)) for m in range(2)}
                for t in range(NST):
                    tau = NST * b + t
                    one, two = ahead or t < NST - 1, ahead or t < NST - 2
                    before = t > 0 or not isinstance(b, int) or b > 0
                    for n in range(NU):
                        if n + 2 < NU:
                            keys(tau, t, n + 2)
                        elif one:
                            keys(tau + 1, t + 1, n + 2 - NU)
                        for m in range(NU):
                            if one and MAX_STEP[m] == n:
                                scores(tau + 1, (t + 1) % NST, m)
                        if n == 3 and before:
                            sums(tau - 1)
                        if n == 8 and one:
                            maxima_turned(tau + 1)
                        if n == 9 and two:
                            if t == NST - 2:
                                pe.wait_ge(s["rot_lo"], 2 * (b + 1) + 2)
                            stack(tau + 2, (t + 2) % NST, 1)
                        if n == 4 and t == 0:
                            pe.wait_ge(s["v_sb"], b + 1)
                        if n == 0 and before:
                            weighted(tau - 1, (t - 1) % NST, NT - 1)
                        if n in VALUE_STEP:
                            weighted(tau, t, VALUE_STEP.index(n))
                        if n == 10 and two:
                            stack(tau + 2, (t + 2) % NST, 0)
                        if NU * t + n in pieces:
                            pieces[NU * t + n]()

            for piece in front(0).values():
                piece()
            pe.wait_ge(s["sel_r"], 1)
            pe.wait_ge(s["rot_lo"], 2)
            pe.wait_ge(s["v_raw"], 1)
            stack(0, 0, 1)
            stack(0, 0, 0)
            for m in range(NU):
                scores(0, 0, m)
            pe.wait_ge(s["q_stack_too"], 1)
            maxima_turned(0)
            stack(1, 1, 1)
            stack(1, 1, 0)
            keys(0, 0, 0)
            keys(0, 0, 1)
            turn(0, True)
            with pe.Fori(1, B - 1) as b:
                turn(b, True)
            turn(B - 1, False)
            weighted(B * NST - 1, NST - 1, NT - 1)
            sums(B * NST - 1)
            for m in range(2):
                output(B - 1, m)


def build(nc, dram, out):
    ctx = ExitStack()
    with ctx:
        x = ctx.enter_context(nc.sbuf_tensor("x", [P, B * NT * D], f32))
        con = ctx.enter_context(nc.sbuf_tensor("con", [P, C_ODD + 3], f32))
        conb = ctx.enter_context(nc.sbuf_tensor("conb", [P, (2 + HPT) * P], bf16))
        psum = ctx.enter_context(nc.psum_tensor("psum", [P, 8 * 512], f32))
        ident = con[:, C_ID:C_ID + P]
        kept = []
        linear_attention(nc, kept, x, psum, con, conb, ident, dram)
        experts(nc, kept, "e0", x, psum, con, conb, dram, "f0", CH0, GROUP0, "r0", E0, "sel0", golden_route)
        nc.clear_and_free_semaphores(kept)
        nc.all_engine_barrier()
        kept = []
        rotary_attention(nc, kept, x, psum, con, conb, dram)
        experts(nc, kept, "e1", x, psum, con, conb, dram, "f1", CH1, GROUP1, "r1", E1, "sel1", top_route)
        stored = ctx.enter_context(nc.semaphore("stored"))
        with nc.Block() as block:
            @block.sync
            def _(sp):
                for b in range(B):
                    sp.dma_start(out[b].rearrange("(i p) d -> p i d", p=P),
                                 x[:, b * NT * D:(b + 1) * NT * D].rearrange("p (i d) -> p i d", i=NT)).then_inc(stored, 16)
                sp.wait_ge(stored, 16 * B)


def host_constants():
    p = np.arange(P)
    con = np.zeros((P, C_ODD + 3), np.float32)
    con[:, C_ID:C_ID + P] = np.eye(P)
    con[:, C_TRI:C_TRI + P] = p[:, None] <= p[None, :]
    con[:, C_AVG:C_AVG + P] = (p[:, None] // DV0 == p[None, :] // DV0) / DV0
    con[:, C_DIAG:C_DIAG + D] = p[:, None] // DK0 == np.arange(D)[None, :] // DV0
    con[:, C_RST:C_RST + T] = np.arange(T)[None, :] % P != 0
    con[:, C_EVEN] = ((p // DK0) % 2 == 0) * np.float32(DV0 ** -0.5)
    con[:, C_ODD] = ((p // DK0) % 2 == 1) * np.float32(DV0 ** -0.5)
    con[:, C_ODD + 1] = EPS
    rope = np.zeros((P, C_SEL + 16 * P), np.float32)
    i = p % HALF
    freq = (np.float32(10000.0) ** (i.astype(np.float32) * np.float32(-2.0 / DH1))).astype(np.float32)
    ang = (np.arange(T, dtype=np.float32)[None, :] * freq[:, None]).astype(np.float32)
    cos, sin = np.cos(ang), np.sin(ang)
    even = (i % 2 == 0)[:, None]
    rope[:, C_COS:C_COS + T] = np.where(even, cos, sin)
    rope[:, C_SIN:C_SIN + T] = np.where(even, -sin, cos)
    for t in range(NST):
        for which, parts in enumerate(((0, 0, 1, 1), (0, 1, 0, 1))):
            for part in range(2):
                m = np.zeros((P, P), np.float32)
                for hh in range(HPT):
                    for c in range(4):
                        if parts[c] == part:
                            for e in range(HALF):
                                m[HALF * (HPT * t + hh) + e, 32 * hh + 8 * c + e] = 1.0
                at = C_SEL + ((t * 2 + which) * 2 + part) * P
                rope[:, at:at + P] = m
    rope[:, C_SUM:C_SUM + P] = p[:, None] == p[None, :] // 32 * 32 + DH1
    rope[:, C_HEAD:C_HEAD + HPT] = p[:, None] // 32 == np.arange(HPT)
    conb = np.zeros((P, (2 + HPT) * P), np.float32)
    for h in range(HPT):
        conb[32 * h:32 * h + 3, (2 + h) * P:(3 + h) * P] = 1.0
    conb[:, 0:P] = np.eye(P)
    conb[:, P:2 * P] = np.where(p[None, :] > p[:, None], -BIG, 0.0)
    sel0 = np.zeros((WR, CH0, P), np.float32)
    sel1 = np.zeros((WR, CH1, P), np.float32)
    for sel, nch, e_n, f in ((sel0, CH0, E0, F0), (sel1, CH1, E1, F1)):
        for c in range(nch):
            for j in range(P):
                e = (c * P + j) // f
                if e < e_n:
                    for part in range(3):
                        sel[part * e_n + e, c, j] = 1.0
                elif e_n == E1 and c * P + j < E1 * F1 + SH1:
                    sel[3 * E1, c, j] = 1.0
    tie = np.zeros((P, E0 * E0 + E1 * E1 + G1 * G1), np.float32)
    at = 0
    for n in (E0, E1, G1):
        e = np.arange(n)
        tie[:, at:at + n * n] = (e[None, :] < e[:, None]).astype(np.float32).reshape(1, -1)
        at += n * n
    half = lambda c: (c.view(np.uint32) >> 16).astype(np.uint16)
    return {"con": con, "rope": rope, "conb": half(conb), "sel0": half(sel0), "sel1": half(sel1), "tie": tie}


def kernel(**inputs):
    import concourse.bacc as _bacc
    from concourse.bass_utils import run_bass_kernel_spmd as _run

    a = {k: np.asarray(v) for k, v in inputs.items()}
    by_rows = lambda w: np.ascontiguousarray(w.reshape(-1, P, w.shape[-1]).transpose(1, 0, 2))
    pad = lambda w, r, c: np.concatenate([np.concatenate([w, np.zeros((w.shape[0], c - w.shape[1]), w.dtype)], 1),
                                          np.zeros((r - w.shape[0], c), w.dtype)], 0)
    host = dict(host_constants())
    host["x"] = a["L0_attn_x"]
    host["w0"] = by_rows(np.concatenate([a["L0_attn_Wq"], a["L0_attn_Wk"], a["L0_attn_Wg"], pad(a["L0_attn_Wkg1"], D, P), a["L0_attn_Wv"]], 1))
    host["wr0"] = pad(a["L0_attn_Wkg2"], P, P)
    host["cols0"] = np.stack([a["L0_attn_bkg2"], a["L0_attn_bg"][:P], a["L0_attn_bg"][P:]], 1)
    host["wo0"] = by_rows(a["L0_attn_Wo"])

    def experts(gate, up, down, chunks):
        g = gate.reshape(KC, P, chunks, P).transpose(2, 1, 0, 3).reshape(chunks, P, KC * P)
        u = up.reshape(KC, P, chunks, P).transpose(2, 1, 0, 3).reshape(chunks, P, KC * P)
        return np.ascontiguousarray(np.concatenate([g, u, down.reshape(chunks, P, D)], 2))

    side = lambda w: w.transpose(1, 0, 2).reshape(D, -1)
    host["f0"] = experts(side(a["L0_ffn_Wg"]), side(a["L0_ffn_Wu"]), a["L0_ffn_Wd"].reshape(-1, D), CH0)
    n1 = CH1 * P
    host["f1"] = experts(pad(np.concatenate([side(a["L1_ffn_w1"]), a["L1_ffn_sw1"]], 1), D, n1),
                         pad(np.concatenate([side(a["L1_ffn_w3"]), a["L1_ffn_sw3"]], 1), D, n1),
                         pad(np.concatenate([a["L1_ffn_w2"].reshape(-1, D), a["L1_ffn_sw2"]], 0), n1, D), CH1)
    host["r0"] = by_rows(a["L0_ffn_Wr"])
    host["temp"] = a["L0_ffn_temperature"].reshape(1, 1)
    host["r1"] = by_rows(np.ascontiguousarray(a["L1_ffn_gate_w"].T))
    host["ebias"] = a["L1_ffn_expert_bias"].reshape(1, E1)
    even, odd = lambda w: w[..., 0::2], lambda w: w[..., 1::2]
    q, k = a["L1_attn_wq"], a["L1_attn_wk"]
    host["w1"] = by_rows(np.concatenate([even(q), odd(q), even(k), odd(k), a["L1_attn_wv"]], 1))
    bq, bk, rw = a["L1_attn_bq"], a["L1_attn_bk"], a["L1_attn_rms_w"]
    host["cols1"] = np.stack([even(bq), odd(bq), even(bk), odd(bk), rw[:P], rw[P:]], 1)
    host["rows1"] = np.stack([a["L1_attn_bv"], a["L1_attn_bo"]], 0).reshape(1, 2 * D)
    wo = a["L1_attn_wo"].reshape(NST, HPT, DH1, D)
    host["wo1"] = np.ascontiguousarray(np.concatenate([wo, np.zeros_like(wo)], 2).reshape(NST, P, D).transpose(1, 0, 2))

    nc = _bacc.Bacc("TRN2", target_bir_lowering=False, num_devices=1)
    arrays, dram = {}, {}
    for name, v in host.items():
        v = np.ascontiguousarray(v)
        arrays[f"in_{name}"] = v
        dram[name] = nc.dram_tensor(f"in_{name}", v.shape, mybir.dt.from_np(v.dtype), kind="ExternalInput").ap()
    out = nc.dram_tensor("out", (B, T, D), f32, kind="ExternalOutput").ap()
    build(nc, dram, out)
    r = _run(nc, [arrays], core_ids=[0])
    return r.results[0]["out"]
```
